# Optimizing a Trainium2 kernel written in Bass

```python
import numpy as np
import jax
import jax.numpy as jnp

def _softmax(x, axis=-1):
    return jax.nn.softmax(x, axis=axis)

def _gelu(x):
    return jax.nn.gelu(x, approximate=True)

def _silu(x):
    return jax.nn.silu(x)

def _sigmoid(x):
    return jax.nn.sigmoid(x)

def _layernorm(x, axis=-1, eps=1e-05):
    m = jnp.mean(x, axis=axis, keepdims=True)
    v = jnp.var(x, axis=axis, keepdims=True)
    return (x - m) / jnp.sqrt(v + eps)

def _scatter_add(tgt, idx, src, axis=0):
    return tgt.at[idx].add(src)

def _segment_sum(src, seg, n):
    return jax.ops.segment_sum(src, seg, n)
kernel_name = 'mk_flamingo_gated_d2_seqx_r8_3d45a7'

def setup_inputs(seed: int=0):
    np.random.seed(seed)
    _w = jnp.asarray

    def _rec_inputs():
        import jax
        import jax.numpy as jnp
        _rk = jax.random.key(seed)
        x = -0.000125 + 0.9999 * jax.random.normal(jax.random.fold_in(_rk, 1), (8, 128, 512), jnp.float32)
        _lenS = 128 - jax.random.randint(jax.random.fold_in(_rk, 7), (8,), 0, max(1, 128 // 4) + 1, jnp.int32)
        _lenS2 = 128 - jax.random.randint(jax.random.fold_in(_rk, 8), (8,), 0, max(1, 128 // 4) + 1, jnp.int32)
        _ctx_4096P = jax.random.normal(jax.random.fold_in(_rk, 11), (8, 16, 512), jnp.float32)
        _ctx_4096c = jax.random.dirichlet(jax.random.fold_in(_rk, 511), 0.3 * jnp.ones((16,), jnp.float32), (8, 128))
        _ctx_4096t = jnp.einsum('bsk,bkd->bsd', _ctx_4096c, _ctx_4096P)
        _ctx_4096t = _ctx_4096t * jax.lax.rsqrt(jnp.mean(jnp.square(_ctx_4096t)) + 1e-12) * 0.953939
        ctx_4096 = -1.52775e-05 + 0.999936 * (_ctx_4096t + 0.3 * jax.random.normal(jax.random.fold_in(_rk, 611), (8, 128, 512), jnp.float32))
        _validS = jnp.arange(128)[None, :] < _lenS[:, None]
        _validS2 = jnp.arange(128)[None, :] < _lenS2[:, None]
        _causal = jnp.tril(jnp.ones((128, 128), dtype=bool))
        mask_1x1xSxS2_ff0 = jnp.where(jnp.ones((1, 1, 128, 128), dtype=bool), 0.0, -1000000000.0).astype(jnp.float32)
        _g = jax.random.normal(jax.random.fold_in(_rk, 9001), (2, 2), jnp.float32)
        _g = jnp.sign(_g) * jnp.maximum(jnp.abs(_g), 1.0) + (_g == 0) * 1.0
        g_xattn = _g[0]
        g_ffn = _g[1]
        return (x, ctx_4096, mask_1x1xSxS2_ff0, g_xattn, g_ffn)
    x, ctx_4096, mask_1x1xSxS2_ff0, g_xattn, g_ffn = _rec_inputs()

    def _L0_xattn_setup():
        import jax, jax.numpy as jnp
        import numpy as np
        H = 8
        C = 2

        def _autocorrelation(Q, K, V):
            B, L, D = Q.shape
            d = D // H
            q = Q.reshape(B, L, H, d).transpose(0, 2, 1, 3)
            k = K.reshape(B, L, H, d).transpose(0, 2, 1, 3)
            v = V.reshape(B, L, H, d).transpose(0, 2, 1, 3)
            qf = jnp.fft.fft(q, axis=2)
            kf = jnp.fft.fft(k, axis=2)
            corr = jnp.fft.ifft(qf * jnp.conj(kf), axis=2).real
            topk = int(C * np.log(L))
            w, idx = jax.lax.top_k(corr.transpose(0, 1, 3, 2), topk)
            w = jax.nn.softmax(w, axis=-1)
            pos = jnp.arange(L)[:, None]
            out = jnp.zeros_like(v)
            for i in range(topk):
                g = jnp.minimum(idx[:, :, None, :, i] + pos, L - 1)
                out = out + w[:, :, None, :, i] * jnp.take_along_axis(v, g, axis=2)
            return out.transpose(0, 2, 1, 3).reshape(B, L, D)
        key = jax.random.key(seed)
        k1, k2, k3 = jax.random.split(key, 3)
        B, L, D = (16, 64, 512)
        Q = jax.random.normal(k1, (B, L, D), dtype=jnp.float32)
        K = jax.random.normal(k2, (B, L, D), dtype=jnp.float32)
        V = jax.random.normal(k3, (B, L, D), dtype=jnp.float32)
        return {'Q': Q, 'K': K, 'V': V}
    _L0_xattn_all = _L0_xattn_setup()
    _L0_xattn_in = {k: v for k, v in _L0_xattn_all.items() if k in ()}
    del _L0_xattn_all

    def _L0_ffn_setup():
        import jax, jax.numpy as jnp
        import numpy as np
        BATCH, TOK, DIM, OUT = (4, 256, 512, 512)
        E, R, TOP_K = (8, 16, 2)
        SCALING = 16.0 / R
        key = jax.random.key(seed)
        ks = jax.random.split(key, 6)
        return {'x': jax.random.normal(ks[0], (BATCH, TOK, DIM), dtype=jnp.float32), 'W_base': jax.random.normal(ks[1], (OUT, DIM), dtype=jnp.float32) / np.sqrt(DIM), 'b_base': jax.random.normal(ks[2], (OUT,), dtype=jnp.float32) * 0.01, 'W_gate': jax.random.normal(ks[3], (E, DIM), dtype=jnp.float32) * 0.01, 'A': jax.random.normal(ks[4], (E, R, DIM), dtype=jnp.float32) / np.sqrt(DIM), 'B': jax.random.normal(ks[5], (OUT, OUT // OUT * R * 0 + R), dtype=jnp.float32)[None].repeat(E, 0) * 0.0 + jax.random.normal(ks[5], (E, OUT, R), dtype=jnp.float32) * 0.02}
    _L0_ffn_all = _L0_ffn_setup()
    _L0_ffn_in = {k: v for k, v in _L0_ffn_all.items() if k in ('W_base', 'b_base', 'W_gate', 'A', 'B')}
    del _L0_ffn_all

    def _L1_xattn_setup():
        import jax, jax.numpy as jnp
        import numpy as np
        B, Q, K, D = (1, 128, 6404, 512)
        H, KVH, HD = (32, 8, 128)
        GROUPS = H // KVH
        EPS = 1e-05

        def _rmsnorm(x, w):
            xf = x.astype(jnp.float32)
            var = jnp.mean(xf * xf, axis=-1, keepdims=True)
            return (xf * jax.lax.rsqrt(var + EPS)).astype(x.dtype) * w
        key = jax.random.key(seed)
        ks = jax.random.split(key, 8)
        s = 0.02
        return {'hidden_states': jax.random.normal(ks[0], (B, Q, D), jnp.float32), 'cross_attention_states': jax.random.normal(ks[1], (B, K, D), jnp.float32), 'attention_mask': jnp.zeros((B, 1, Q, K), jnp.float32), 'Wq': jax.random.normal(ks[2], (H * HD, D), jnp.float32) * s, 'Wk': jax.random.normal(ks[3], (KVH * HD, D), jnp.float32) * s, 'Wv': jax.random.normal(ks[4], (KVH * HD, D), jnp.float32) * s, 'Wo': jax.random.normal(ks[5], (D, H * HD), jnp.float32) * s, 'q_norm_w': jnp.ones((HD,), jnp.float32), 'k_norm_w': jnp.ones((HD,), jnp.float32)}
    _L1_xattn_all = _L1_xattn_setup()
    _L1_xattn_in = {k: v for k, v in _L1_xattn_all.items() if k in ('Wq', 'Wk', 'Wv', 'Wo', 'q_norm_w', 'k_norm_w')}
    del _L1_xattn_all

    def _L1_ffn_setup():
        import jax, jax.numpy as jnp
        import numpy as np
        B_, S, D_IN, D_OUT = (4, 256, 512, 512)
        N, RANK, ALPHA = (8, 16, 32)
        SCALE = ALPHA / RANK
        key = jax.random.key(seed)
        kx, ka, kb, kw, kbias = jax.random.split(key, 5)
        x = jax.random.normal(kx, (B_, S, D_IN), dtype=jnp.float32)
        lora_A = jax.random.normal(ka, (N, RANK, D_IN), dtype=jnp.float32) * (1.0 / np.sqrt(D_IN))
        lora_B = jax.random.normal(kb, (N, D_OUT, RANK), dtype=jnp.float32) * (1.0 / np.sqrt(RANK))
        W = jax.random.normal(kw, (D_OUT, D_IN), dtype=jnp.float32) * (1.0 / np.sqrt(D_IN))
        bias = jax.random.normal(kbias, (D_OUT,), dtype=jnp.float32) * 0.01
        lora_weights = jnp.full((N,), 1.0 / N, dtype=jnp.float32)
        return {'x': x, 'lora_A': lora_A, 'lora_B': lora_B, 'W': W, 'bias': bias, 'lora_weights': lora_weights}
    _L1_ffn_all = _L1_ffn_setup()
    _L1_ffn_in = {k: v for k, v in _L1_ffn_all.items() if k in ('lora_A', 'lora_B', 'W', 'bias', 'lora_weights')}
    del _L1_ffn_all
    return {'x': x, 'ctx_4096': ctx_4096, 'mask_1x1xSxS2_ff0': mask_1x1xSxS2_ff0, 'g_xattn': g_xattn, 'g_ffn': g_ffn, 'L0_ffn_W_base': _L0_ffn_in['W_base'], 'L0_ffn_b_base': _L0_ffn_in['b_base'], 'L0_ffn_W_gate': _L0_ffn_in['W_gate'], 'L0_ffn_A': _L0_ffn_in['A'], 'L0_ffn_B': _L0_ffn_in['B'], 'L1_xattn_Wq': _L1_xattn_in['Wq'], 'L1_xattn_Wk': _L1_xattn_in['Wk'], 'L1_xattn_Wv': _L1_xattn_in['Wv'], 'L1_xattn_Wo': _L1_xattn_in['Wo'], 'L1_xattn_q_norm_w': _L1_xattn_in['q_norm_w'], 'L1_xattn_k_norm_w': _L1_xattn_in['k_norm_w'], 'L1_ffn_lora_A': _L1_ffn_in['lora_A'], 'L1_ffn_lora_B': _L1_ffn_in['lora_B'], 'L1_ffn_W': _L1_ffn_in['W'], 'L1_ffn_bias': _L1_ffn_in['bias'], 'L1_ffn_lora_weights': _L1_ffn_in['lora_weights']}

def reference(x, ctx_4096, mask_1x1xSxS2_ff0, g_xattn, g_ffn, L0_ffn_W_base, L0_ffn_b_base, L0_ffn_W_gate, L0_ffn_A, L0_ffn_B, L1_xattn_Wq, L1_xattn_Wk, L1_xattn_Wv, L1_xattn_Wo, L1_xattn_q_norm_w, L1_xattn_k_norm_w, L1_ffn_lora_A, L1_ffn_lora_B, L1_ffn_W, L1_ffn_bias, L1_ffn_lora_weights):
    import jax
    import jax.numpy as jnp

    def _L0_xattn_ref(Q, K, V):
        import jax, jax.numpy as jnp
        import numpy as np
        H = 8
        C = 2

        def _autocorrelation(Q, K, V):
            B, L, D = Q.shape
            d = D // H
            q = Q.reshape(B, L, H, d).transpose(0, 2, 1, 3)
            k = K.reshape(B, L, H, d).transpose(0, 2, 1, 3)
            v = V.reshape(B, L, H, d).transpose(0, 2, 1, 3)
            qf = jnp.fft.fft(q, axis=2)
            kf = jnp.fft.fft(k, axis=2)
            corr = jnp.fft.ifft(qf * jnp.conj(kf), axis=2).real
            topk = int(C * np.log(L))
            w, idx = jax.lax.top_k(corr.transpose(0, 1, 3, 2), topk)
            w = jax.nn.softmax(w, axis=-1)
            pos = jnp.arange(L)[:, None]
            out = jnp.zeros_like(v)
            for i in range(topk):
                g = jnp.minimum(idx[:, :, None, :, i] + pos, L - 1)
                out = out + w[:, :, None, :, i] * jnp.take_along_axis(v, g, axis=2)
            return out.transpose(0, 2, 1, 3).reshape(B, L, D)
        return _autocorrelation(Q, K, V)

    def _L0_ffn_ref(x, W_base, b_base, W_gate, A, B):
        import jax, jax.numpy as jnp
        import numpy as np
        BATCH, TOK, DIM, OUT = (4, 256, 512, 512)
        E, R, TOP_K = (8, 16, 2)
        SCALING = 16.0 / R
        result = jnp.einsum('bnd,od->bno', x, W_base) + b_base
        logits = jnp.einsum('bnd,ed->bne', x, W_gate)
        probs = jax.nn.softmax(logits.astype(jnp.float32), axis=-1)
        top_p, top_i = jax.lax.top_k(probs, TOP_K)
        top_p = top_p / jnp.sum(top_p, axis=-1, keepdims=True)
        top_p = top_p.astype(x.dtype)
        route_w = jnp.sum(jax.nn.one_hot(top_i, E, dtype=x.dtype) * top_p[..., None], axis=-2)
        h = jnp.einsum('bnd,erd->bner', x, A)
        hw = h * route_w[..., None]
        delta = jnp.einsum('bner,eor->bno', hw, B)
        return result + delta * SCALING

    def _L1_xattn_ref(hidden_states, cross_attention_states, attention_mask, Wq, Wk, Wv, Wo, q_norm_w, k_norm_w):
        import jax, jax.numpy as jnp
        import numpy as np
        B, Q, K, D = (1, 128, 6404, 512)
        H, KVH, HD = (32, 8, 128)
        GROUPS = H // KVH
        EPS = 1e-05

        def _rmsnorm(x, w):
            xf = x.astype(jnp.float32)
            var = jnp.mean(xf * xf, axis=-1, keepdims=True)
            return (xf * jax.lax.rsqrt(var + EPS)).astype(x.dtype) * w
        bsz, q_len, _ = hidden_states.shape
        kv_len = cross_attention_states.shape[1]
        q = (hidden_states @ Wq.T).reshape(bsz, q_len, H, HD).transpose(0, 2, 1, 3)
        k = (cross_attention_states @ Wk.T).reshape(bsz, kv_len, KVH, HD).transpose(0, 2, 1, 3)
        v = (cross_attention_states @ Wv.T).reshape(bsz, kv_len, KVH, HD).transpose(0, 2, 1, 3)
        q = _rmsnorm(q, q_norm_w)
        k = jnp.repeat(k, GROUPS, axis=1)
        v = jnp.repeat(v, GROUPS, axis=1)
        k = _rmsnorm(k, k_norm_w)
        scale = 1.0 / np.sqrt(HD)
        scores = jnp.einsum('bhqd,bhkd->bhqk', q, k) * scale
        scores = scores + attention_mask[:, :, :, :kv_len]
        probs = jax.nn.softmax(scores.astype(jnp.float32), axis=-1).astype(q.dtype)
        out = jnp.einsum('bhqk,bhkd->bhqd', probs, v)
        out = out.transpose(0, 2, 1, 3).reshape(bsz, q_len, H * HD)
        return out @ Wo.T

    def _L1_ffn_ref(x, lora_A, lora_B, W, bias, lora_weights):
        import jax, jax.numpy as jnp
        import numpy as np
        B_, S, D_IN, D_OUT = (4, 256, 512, 512)
        N, RANK, ALPHA = (8, 16, 32)
        SCALE = ALPHA / RANK
        h = jnp.einsum('bsd,nrd->nbsr', x, lora_A)
        coef = (SCALE * lora_weights)[:, None, None]
        lora_out = jnp.einsum('nbsr,nor->bso', h, lora_B * coef)
        base = jnp.einsum('bsd,od->bso', x, W) + bias
        return base + lora_out
    x = x + jnp.tanh(g_xattn[0]) * _L0_xattn_ref(_layernorm(x, axis=-1), ctx_4096, ctx_4096)
    x = x + jnp.tanh(g_ffn[0]) * _L0_ffn_ref(_layernorm(x, axis=-1), L0_ffn_W_base, L0_ffn_b_base, L0_ffn_W_gate, L0_ffn_A, L0_ffn_B)
    x = x + jnp.tanh(g_xattn[1]) * _L1_xattn_ref(_layernorm(x, axis=-1), ctx_4096, mask_1x1xSxS2_ff0, L1_xattn_Wq, L1_xattn_Wk, L1_xattn_Wv, L1_xattn_Wo, L1_xattn_q_norm_w, L1_xattn_k_norm_w)
    x = x + jnp.tanh(g_ffn[1]) * _L1_ffn_ref(_layernorm(x, axis=-1), L1_ffn_lora_A, L1_ffn_lora_B, L1_ffn_W, L1_ffn_bias, L1_ffn_lora_weights)
    return x

_drawn_inputs = setup_inputs


def setup_inputs(seed=0):
    import zlib

    import numpy as np

    out = dict(_drawn_inputs(seed))
    spreads = {'g_ffn': (-1.0, 0.2),
     'L1_xattn_q_norm_w': (1.0, 0.6),
     'L1_xattn_k_norm_w': (1.0, 0.6),
     'L1_ffn_lora_weights': (0.125, 0.2)}
    factors = {'L0_ffn_b_base': 8.0, 'L1_ffn_bias': 8.0}
    for name, (base, spread) in spreads.items():
        noise = np.random.default_rng([zlib.crc32(name.encode()), seed]).standard_normal(out[name].shape)
        drawn = base * np.exp(spread * noise) if base else spread * noise
        out[name] = jnp.asarray(drawn.astype(out[name].dtype))
    for name, factor in factors.items():
        out[name] = (out[name] * factor).astype(out[name].dtype)
    return out
```

```python
from contextlib import ExitStack

import concourse.bass as bass
from concourse import mybir

F32 = mybir.dt.float32
F32R = mybir.dt.float32r
ALU = mybir.AluOpType
ACT = mybir.ActivationFunctionType
AX = mybir.AxisListType

P = 128
B = 8
D = 512
CH = D // P
G = 8
HG = 4
E = 8
R = 16
ER = E * R
TOPK = 9
NEG = -(2.0 ** 127)
LN_EPS = 1e-5
RMS_EPS = 1e-5

(K_FWD, K_FWD_SW, V_ODD, V_ODD_SW, W_ODD, C_INV1, C_INV2,
 E_INV1, E_INV2, O_INV1, O_INV2, HOLD, IDENT) = range(13)
N_DFT = 13


def need(eng, sem, value, hold=False):
    if isinstance(value, int) and value <= 0:
        return
    eng.wait_ge(sem, value)
    if hold and not isinstance(value, int):
        eng.nop(nofuse=True)


def cols(start, n):
    return slice(start, start + n) if isinstance(start, int) else bass.ds(start, n)


def flamingo_kernel(nc, x, ctx_n, ctx_t, mask, gates, dft_d, wbase_d, wag_d, bb_d, bcat_d,
                    wq_d, wkv_d, wo_d, qn_d, kn_d, lA_d, lB_d, lw_d, w1_d, b1_d, out):
    with ExitStack() as top:
        def sem(name):
            return top.enter_context(nc.semaphore(name))

        def sb(stack, name, shape, dt=F32):
            return stack.enter_context(nc.sbuf_tensor(name, shape, dt))

        bank = [top.enter_context(nc.psum_tensor(f"bank{i}", [P, 512], F32)) for i in range(8)]

        xres = sb(top, "xres", [P, B * D])
        nT_hi = sb(top, "nT_hi", [P, CH, B * P], F32R)
        nT_lo = sb(top, "nT_lo", [P, CH, B * P], F32R)
        cT_hi = sb(top, "cT_hi", [P, CH, B * P], F32R)
        cT_lo = sb(top, "cT_lo", [P, CH, B * P], F32R)
        gate = sb(top, "gate", [P, 4])
        ident = sb(top, "ident", [P, P])
        neghalf = sb(top, "neghalf", [P, 8])

        phase_a(nc, sem, sb, bank, xres, nT_hi, nT_lo, cT_hi, cT_lo, gate, ident, neghalf,
                x, ctx_n, ctx_t, gates, dft_d, wbase_d, wag_d, bb_d, bcat_d)
        phase_c(nc, sem, sb, bank, xres, nT_hi, nT_lo, cT_hi, cT_lo, gate, ident, neghalf,
                mask, wq_d, wkv_d, wo_d, qn_d, kn_d)
        phase_d(nc, sem, sb, bank, xres, gate, ident, neghalf, lA_d, lB_d, lw_d, w1_d, b1_d, out)


def phase_a(nc, sem, sb, bank, xres, nT_hi, nT_lo, cT_hi, cT_lo, gate, ident, neghalf,
            x, ctx_n, ctx_t, gates, dft_d, wbase_d, wag_d, bb_d, bcat_d):
    with ExitStack() as st:
        ctxn = sb(st, "ctxn", [P, B * D])
        ctxt = sb(st, "ctxt", [P, CH, B * P])
        dft = sb(st, "dft", [P, N_DFT, P])
        wbase = sb(st, "wbase", [P, CH, D])
        wag = sb(st, "wag", [P, CH, ER + E])
        bcat = sb(st, "bcat", [P, D])
        bb = sb(st, "bb", [P, D])
        gates_in = sb(st, "gates_in", [P, 4])
        f_stat = sb(st, "f_stat", [P, 6])
        f_mv = sb(st, "f_mv", [P, 2])
        f_rstd = sb(st, "f_rstd", [P, 1])
        nx = sb(st, "nx", [P, D])
        kf = sb(st, "kf", [P, 4, D])
        prod1 = sb(st, "prod1", [P, D])
        prod2 = sb(st, "prod2", [P, D])
        top8 = sb(st, "top8", [P, CH, 8])
        next8 = sb(st, "next8", [P, CH, 8])
        ninth = sb(st, "ninth", [P, CH, 8])
        ntop = sb(st, "ntop", [P, CH])
        rest8 = sb(st, "rest8", [P, CH, P])
        rest9 = sb(st, "rest9", [P, CH, P])
        elag = sb(st, "elag", [P, CH, P])
        wlag = sb(st, "wlag", [P, CH, P])
        wsum = sb(st, "wsum", [P, CH])
        wrec = sb(st, "wrec", [P, CH])
        wlagn = sb(st, "wlagn", [P, CH, P])
        wT = sb(st, "wT", [P, D])
        op = sb(st, "op", [P, 4, D])
        h_stat = sb(st, "h_stat", [P, 6])
        h_mv = sb(st, "h_mv", [P, 2])
        h_rstd = sb(st, "h_rstd", [P, 1])
        n1 = sb(st, "n1", [P, D])
        n1T = sb(st, "n1T", [P, CH, P])
        lg = sb(st, "lg", [P, 2 * E])
        lg8 = sb(st, "lg8", [P, 8])
        two = sb(st, "two", [P, 8])
        nlg = sb(st, "nlg", [P, 1])
        eg = sb(st, "eg", [P, E])
        lgr = sb(st, "lgr", [P, 2 * E])
        rw = sb(st, "rw", [P, E])
        rsum = sb(st, "rsum", [P, 1])
        rrec = sb(st, "rrec", [P, 1])
        rwn = sb(st, "rwn", [P, E])
        hw = sb(st, "hw", [P, ER])
        hwT = sb(st, "hwT", [P, P])
        g_stat = sb(st, "g_stat", [P, 6])
        g_mv = sb(st, "g_mv", [P, 2])
        g_rstd = sb(st, "g_rstd", [P, 1])
        n2 = sb(st, "n2", [P, D])

        ld_g = sem("a_gates_loaded")
        ld_x = [sem("a_x0_loaded"), sem("a_x_loaded")]
        ld_c = [sem("a_ctx0_loaded"), sem("a_ctx_loaded")]
        ld_dft = sem("a_dft_loaded")
        ld_w = [sem(f"a_weights_loaded{i}") for i in range(4)]
        ld_ct = sem("a_ctx_turned_loaded")
        ct_hi = sem("a_ctx_turned_hi")
        ct_lo = sem("a_ctx_turned_lo")
        lag9 = sem("a_ninth_steps")
        routed = sem("a_route_weights")
        consts = sem("a_consts")
        tanhed = sem("a_gates_tanh")
        bias_gated = sem("a_bias_gated")
        f_stats = sem("a_f_stats")
        f_root = sem("a_f_root")
        f_norm = sem("a_f_norm")
        q_fwd = sem("a_q_transformed")
        k_fwd = sem("a_ctx_transformed")
        k_copied = sem("a_ctx_dfts_copied")
        c_prod = sem("a_corr_products")
        corr = sem("a_corr_ready")
        picked = sem("a_lag_steps")
        e_lag = sem("a_exp_lags")
        w_norm = sem("a_lag_weights")
        w_trans = sem("a_lag_weights_turned")
        w_copied = sem("a_lag_weights_copied")
        w_fwd = sem("a_lag_weights_transformed")
        o_prod = sem("a_out_products")
        f_out = sem("a_f_out")
        f_added = sem("a_f_added")
        h_stats = sem("a_h_stats")
        h_root = sem("a_h_root")
        h_norm = sem("a_h_norm")
        h_trans = sem("a_h_turned")
        h_copied = sem("a_h_copied")
        h_low = sem("a_router_ready")
        h_step = sem("a_router_steps")
        h_exp = sem("a_router_exp")
        hw_trans = sem("a_hw_turned")
        hw_copied = sem("a_hw_copied")
        h_out = sem("a_h_out")
        h_bias = sem("a_bias_added")
        h_added = sem("a_h_added")
        g_stats = sem("a_g_stats")
        g_root = sem("a_g_root")
        g_norm = sem("a_g_norm")
        g_trans = sem("a_g_turned")
        g_hi = sem("a_g_hi")
        g_lo = sem("a_g_lo")

        PICK = 5
        ROUTE = 7

        def xb(b):
            return xres[:, cols(b * D, D)]

        def looped(eng, slot):
            slot(0, True, False)
            slot(1, True, True)
            with eng.Fori(2, B) as b:
                slot(b, True, True)
            slot(B, False, True)

        with nc.Block() as block:
            @block.sync
            def _(sp):
                sp.dma_start(xb(0), x[0]).then_inc(ld_x[0], 16)
                sp.dma_start(ctxn[:, 0:D], ctx_n[0]).then_inc(ld_c[0], 16)
                sp.dma_start(dft[:], dft_d[:]).then_inc(ld_dft, 16)
                sp.dma_start(xres[:, D:].rearrange("p (b d) -> p b d", d=D),
                             x[1:].rearrange("b p d -> p b d")).then_inc(ld_x[1], 16)
                sp.dma_start(ctxn[:, D:].rearrange("p (b d) -> p b d", d=D),
                             ctx_n[1:].rearrange("b p d -> p b d")).then_inc(ld_c[1], 16)
                sp.dma_start(ctxt[:], ctx_t[:]).then_inc(ld_ct, 16)

            @block.gpsimd
            def _(pool):
                pool.memset(neghalf[:], -0.5).then_inc(consts, 1)
                pool.memset(ninth[:], NEG).then_inc(consts, 1)
                pool.memset(lg[:], NEG).then_inc(consts, 1)
                pool.memset(two[:], NEG).then_inc(consts, 1)
                pool.wait_ge(consts, 4)

                def inverse_root(stats, root, mv, rstd, n):
                    need(pool, stats, 2 * n + 2, hold=True)
                    pool.tensor_scalar(mv[:, 1:2], mv[:, 1:2], LN_EPS, None, ALU.add).then_inc(root, 1)
                    need(pool, root, 2 * n + 1)
                    pool.tensor_tensor(rstd[:], mv[:, 1:2], neghalf[:, 0:1], ALU.pow).then_inc(root, 1)

                def slot(b, f, h):
                    if h:
                        inverse_root(h_stats, h_root, h_mv, h_rstd, b - 1)
                        need(pool, h_norm, b)
                        pool.tensor_tensor(xb(b - 1), xb(b - 1), bb[:], ALU.add).then_inc(h_bias, 1)
                        inverse_root(g_stats, g_root, g_mv, g_rstd, b - 1)
                    if f:
                        need(pool, picked, PICK * b + PICK)
                        need(pool, w_trans, b)
                        pool.tensor_tensor(wlagn[:], wlag[:],
                                           wrec[:].unsqueeze(2).broadcast_to([P, CH, P]),
                                           ALU.mult).then_inc(w_norm, 1)
                        if isinstance(b, int) and b == 0:
                            pool.wait_ge(ld_ct, 16)
                        here = cols(b * P, P)
                        pool.tensor_copy(cT_hi[:, :, here], ctxt[:, :, here]).then_inc(ct_hi, 1)
                        need(pool, ct_hi, b + 1)
                        pool.tensor_tensor(cT_lo[:, :, here], ctxt[:, :, here], cT_hi[:, :, here].bitcast(F32),
                                           ALU.subtract).then_inc(ct_lo, 1)

                inverse_root(f_stats, f_root, f_mv, f_rstd, 0)
                need(pool, bias_gated, 1)

                def slot_pool(b, f, h):
                    slot(b, f, h)
                    if f and not (isinstance(b, int) and b >= B - 1):
                        inverse_root(f_stats, f_root, f_mv, f_rstd, b + 1)

                slot_pool(0, True, False)
                slot_pool(1, True, True)
                with pool.Fori(2, B - 1) as b:
                    slot_pool(b, True, True)
                slot_pool(B - 1, True, True)
                slot_pool(B, False, True)

            @block.scalar
            def _(act):
                act.dma_start(gates_in[:], gates[:]).then_inc(ld_g, 16)
                act.dma_start(wbase[:], wbase_d[:]).then_inc(ld_w[0], 16)
                act.dma_start(wag[:], wag_d[:]).then_inc(ld_w[1], 16)
                act.dma_start(bcat[:], bcat_d[:]).then_inc(ld_w[2], 16)
                act.dma_start(bb[:], bb_d[:]).then_inc(ld_w[3], 16)
                act.wait_ge(ld_g, 16)
                act.activation(gate[:], gates_in[:], ACT.Tanh).then_inc(tanhed, 1)

                def slot(b, f, h):
                    if f:
                        for i in range(4):
                            need(act, k_fwd, 4 * b + i + 1)
                            if i == 0:
                                need(act, o_prod, 4 * b)
                            act.activation(kf[:, i, :], bank[1 + i][:], ACT.Copy).then_inc(k_copied, 1)
                    if h:
                        need(act, h_trans, b)
                        act.activation(n1T[:].rearrange("p c t -> p (c t)"), bank[5][:],
                                       ACT.Copy).then_inc(h_copied, 1)
                    if f:
                        need(act, corr, b + 1)
                        need(act, picked, PICK * b + 3)
                        for j in range(CH):
                            act.activation(elag[:, j, :], bank[1][:, j * P:(j + 1) * P], ACT.Exp,
                                           bias=ntop[:, j:j + 1]).then_inc(e_lag, 1)
                    if h:
                        need(act, h_step, ROUTE * (b - 1) + 3)
                        act.activation(eg[:], lg[:, 0:E], ACT.Exp, bias=nlg[:]).then_inc(h_exp, 1)
                        need(act, hw_trans, b)
                        act.activation(hwT[:], bank[5][:, 0:P], ACT.Copy).then_inc(hw_copied, 1)
                    if f:
                        need(act, w_trans, b + 1)
                        act.activation(wT[:], bank[2][:], ACT.Copy).then_inc(w_copied, 1)
                    if h:
                        need(act, g_trans, b)
                        act.activation(nT_hi[:, :, cols((b - 1) * P, P)],
                                       bank[5][:].rearrange("p (c t) -> p c t", c=CH),
                                       ACT.Copy).then_inc(g_hi, 1)

                looped(act, slot)

            @block.tensor
            def _(pe):
                pe.wait_ge(ld_dft, 16)

                def slot(b, f, h):
                    if f:
                        need(pe, f_norm, b + 1)
                        need(pe, f_added, b)
                        pe.matmul(bank[0][:], dft[:, K_FWD, :], nx[:], start=True, stop=True).then_inc(q_fwd, 1)
                        if isinstance(b, int) and b == 0:
                            pe.wait_ge(ld_c[0], 16)
                        else:
                            pe.wait_ge(ld_c[1], 16)
                        need(pe, o_prod, 4 * b)
                        for i, m in enumerate((K_FWD, K_FWD_SW, V_ODD, V_ODD_SW)):
                            pe.matmul(bank[1 + i][:], dft[:, m, :], ctxn[:, cols(b * D, D)],
                                      start=True, stop=True).then_inc(k_fwd, 1)
                    if h:
                        need(pe, h_norm, b)
                        need(pe, g_hi, b - 1)
                        need(pe, g_lo, b - 1)
                        for c in range(CH):
                            t = pe.transpose(bank[5][:, c * P:(c + 1) * P], n1[:, c * P:(c + 1) * P],
                                             dft[:, IDENT, :])
                        t.then_inc(h_trans, 1)
                    if f:
                        need(pe, c_prod, 2 * b + 2)
                        need(pe, k_copied, 4 * b + 1)
                        for j in range(CH):
                            o = bank[1][:, j * P:(j + 1) * P]
                            pe.matmul(o, prod1[:, j * P:(j + 1) * P], dft[:, C_INV1, :], start=True, stop=False)
                            t = pe.matmul(o, prod2[:, j * P:(j + 1) * P], dft[:, C_INV2, :],
                                          start=False, stop=True)
                        t.then_inc(corr, 1)
                    if h:
                        need(pe, h_copied, b)
                        need(pe, h_added, b - 1)
                        pe.wait_ge(ld_w[0], 16)
                        pe.wait_ge(ld_w[1], 16)
                        pe.wait_ge(ld_w[2], 16)
                        for c in range(CH):
                            t = pe.matmul(bank[7][:, 0:ER + E], n1T[:, c, :], wag[:, c, :],
                                          start=(c == 0), stop=(c == CH - 1))
                        t.then_inc(h_low, 1)
                        for c in range(CH):
                            pe.matmul(bank[6][:], n1T[:, c, :], wbase[:, c, :], start=(c == 0), stop=False)
                        need(pe, h_step, ROUTE * (b - 1) + ROUTE)
                        pe.transpose(bank[5][:, 0:P], hw[:], dft[:, IDENT, :]).then_inc(hw_trans, 1)
                        need(pe, hw_copied, b)
                        pe.matmul(bank[6][:], hwT[:], bcat[:], start=False, stop=True).then_inc(h_out, 1)
                    if f:
                        need(pe, w_norm, b + 1)
                        need(pe, k_copied, 4 * b + 4)
                        for j in range(CH):
                            t = pe.transpose(bank[2][:, j * P:(j + 1) * P], wlagn[:, j, :], dft[:, IDENT, :])
                        t.then_inc(w_trans, 1)
                        need(pe, w_copied, b + 1)
                        pe.matmul(bank[3][:], dft[:, K_FWD, :], wT[:], start=True, stop=True).then_inc(w_fwd, 1)
                        pe.matmul(bank[4][:], dft[:, W_ODD, :], wT[:], start=True, stop=True).then_inc(w_fwd, 1)
                    if h:
                        need(pe, g_norm, b)
                        for c in range(CH):
                            t = pe.transpose(bank[5][:, c * P:(c + 1) * P], n2[:, c * P:(c + 1) * P],
                                             dft[:, IDENT, :])
                        t.then_inc(g_trans, 1)
                    if f:
                        pe.matmul(bank[0][:], dft[:, HOLD, :], ctxn[:, cols(b * D, D)], start=True, stop=False)
                        for i, m in enumerate((E_INV1, E_INV2, O_INV1, O_INV2)):
                            need(pe, o_prod, 4 * b + i + 1)
                            t = pe.matmul(bank[0][:], dft[:, m, :], op[:, i, :], start=False, stop=(i == 3))
                        t.then_inc(f_out, 1)

                looped(pe, slot)

            @block.vector
            def _(dve):
                dve.wait_ge(tanhed, 1)
                dve.wait_ge(ld_w[3], 16)
                dve.tensor_scalar(bb[:], bb[:], gate[:, 1:2], None, ALU.mult).then_inc(bias_gated, 1)

                def statistics(src, stat, mv, done, n):
                    dve.bn_stats(stat[:], src).then_inc(done, 1)
                    need(dve, done, 2 * n + 1, hold=True)
                    dve.bn_aggr(mv[:], stat[:]).then_inc(done, 1)

                def normalise(dst, src, mv, rstd, root, done, n):
                    need(dve, root, 2 * n + 2)
                    dve.tensor_scalar(dst[:], src, mv[:, 0:1], rstd[:], ALU.subtract, ALU.mult).then_inc(done, 1)

                def pick_lags(b):
                    need(dve, corr, b + 1, hold=True)
                    for j in range(CH):
                        t = dve.max(top8[:, j, :], bank[1][:, j * P:(j + 1) * P])
                    t.then_inc(picked, 1)
                    need(dve, picked, PICK * b + 1)
                    dve.tensor_scalar(ntop[:], top8[:, :, 0], -1.0, None, ALU.mult).then_inc(picked, 1)
                    for j in range(CH):
                        t = dve.match_replace(rest8[:, j, :], top8[:, j, :], bank[1][:, j * P:(j + 1) * P], NEG)
                    t.then_inc(picked, 1)
                    need(dve, picked, PICK * b + 3, hold=True)
                    for j in range(CH):
                        t = dve.max(next8[:, j, :], rest8[:, j, :])
                    t.then_inc(lag9, 1)
                    need(dve, lag9, 3 * b + 1)
                    dve.tensor_copy(ninth[:, :, 0], next8[:, :, 0]).then_inc(lag9, 1)
                    need(dve, lag9, 3 * b + 2, hold=True)
                    for j in range(CH):
                        t = dve.match_replace(rest9[:, j, :], ninth[:, j, :], rest8[:, j, :], NEG)
                    t.then_inc(lag9, 1)
                    need(dve, lag9, 3 * b + 3)
                    need(dve, e_lag, CH * b + CH)
                    need(dve, w_norm, b)
                    for j in range(CH):
                        t = dve.scalar_tensor_tensor(wlag[:, j, :], rest9[:, j, :], NEG, elag[:, j, :],
                                                     ALU.is_equal, ALU.mult, accum_out=wsum[:, j:j + 1])
                    t.then_inc(picked, 1)
                    need(dve, picked, PICK * b + 4)
                    dve.reciprocal(wrec[:], wsum[:]).then_inc(picked, 1)

                def route(b):
                    n = ROUTE * b
                    need(dve, h_low, b + 1)
                    dve.tensor_copy(lg[:, 0:E], bank[7][:, ER:ER + E]).then_inc(h_step, 1)
                    need(dve, h_step, n + 1, hold=True)
                    dve.max(lg8[:], lg[:, 0:E]).then_inc(h_step, 1)
                    need(dve, h_step, n + 2)
                    dve.tensor_scalar(nlg[:], lg8[:, 0:1], -1.0, None, ALU.mult).then_inc(h_step, 1)
                    dve.tensor_copy(two[:, 0:2], lg8[:, 0:2]).then_inc(h_step, 1)
                    need(dve, h_step, n + 4, hold=True)
                    dve.match_replace(lgr[:], two[:], lg[:], NEG).then_inc(h_step, 1)
                    need(dve, h_step, n + 5)
                    need(dve, h_exp, b + 1)
                    dve.scalar_tensor_tensor(rw[:], lgr[:, 0:E], NEG, eg[:], ALU.is_equal, ALU.mult,
                                             accum_out=rsum[:]).then_inc(h_step, 1)
                    need(dve, h_step, n + 6)
                    dve.reciprocal(rrec[:], rsum[:]).then_inc(routed, 1)
                    need(dve, routed, 2 * b + 1)
                    dve.tensor_scalar(rwn[:], rw[:], rrec[:], None, ALU.mult).then_inc(routed, 1)
                    need(dve, routed, 2 * b + 2)
                    dve.tensor_tensor(hw[:].rearrange("p (e r) -> p e r", e=E),
                                      bank[7][:, 0:ER].rearrange("p (e r) -> p e r", e=E),
                                      rwn[:].unsqueeze(2).broadcast_to([P, E, R]), ALU.mult).then_inc(h_step, 1)

                def slot(b, f, h, more):
                    if f:
                        need(dve, q_fwd, b + 1)
                        need(dve, corr, b)
                        need(dve, k_copied, 4 * b + 1)
                        dve.tensor_tensor(prod1[:], bank[0][:], kf[:, 0, :], ALU.mult).then_inc(c_prod, 1)
                        need(dve, k_copied, 4 * b + 2)
                        dve.tensor_tensor(prod2[:], bank[0][:], kf[:, 1, :], ALU.mult).then_inc(c_prod, 1)
                    if f:
                        pick_lags(b)
                    if h:
                        route(b - 1)
                        need(dve, h_out, b)
                        need(dve, h_bias, b)
                        dve.scalar_tensor_tensor(xb(b - 1), bank[6][:], gate[:, 1:2], xb(b - 1),
                                                 ALU.mult, ALU.add).then_inc(h_added, 1)
                        need(dve, h_added, b, hold=True)
                        statistics(xb(b - 1), g_stat, g_mv, g_stats, b - 1)
                    if f:
                        need(dve, w_fwd, 2 * b + 1)
                        dve.tensor_tensor(op[:, 0, :], bank[3][:], kf[:, 0, :], ALU.mult).then_inc(o_prod, 1)
                        dve.tensor_tensor(op[:, 1, :], bank[3][:], kf[:, 1, :], ALU.mult).then_inc(o_prod, 1)
                        need(dve, w_fwd, 2 * b + 2)
                        dve.tensor_tensor(op[:, 2, :], bank[4][:], kf[:, 2, :], ALU.mult).then_inc(o_prod, 1)
                        dve.tensor_tensor(op[:, 3, :], bank[4][:], kf[:, 3, :], ALU.mult).then_inc(o_prod, 1)
                    if h:
                        need(dve, g_trans, b - 1)
                        normalise(n2, xb(b - 1), g_mv, g_rstd, g_root, g_norm, b - 1)
                    if more:
                        statistics(xb(b + 1), f_stat, f_mv, f_stats, b + 1)
                    if f:
                        need(dve, f_out, b + 1)
                        dve.scalar_tensor_tensor(xb(b), bank[0][:], gate[:, 0:1], xb(b),
                                                 ALU.mult, ALU.add).then_inc(f_added, 1)
                        need(dve, f_added, b + 1, hold=True)
                        statistics(xb(b), h_stat, h_mv, h_stats, b)
                    if more:
                        normalise(nx, xb(b + 1), f_mv, f_rstd, f_root, f_norm, b + 1)
                    if f:
                        normalise(n1, xb(b), h_mv, h_rstd, h_root, h_norm, b)
                    if h:
                        need(dve, g_trans, b)
                        need(dve, g_hi, b)
                        dve.tensor_tensor(nT_lo[:, :, cols((b - 1) * P, P)],
                                          bank[5][:].rearrange("p (c t) -> p c t", c=CH),
                                          nT_hi[:, :, cols((b - 1) * P, P)].bitcast(F32),
                                          ALU.subtract).then_inc(g_lo, 1)

                dve.wait_ge(consts, 4)
                dve.wait_ge(ld_dft, 16)
                dve.tensor_copy(ident[:], dft[:, IDENT, :]).then_inc(bias_gated, 1)
                dve.wait_ge(ld_x[0], 16)
                statistics(xb(0), f_stat, f_mv, f_stats, 0)
                normalise(nx, xb(0), f_mv, f_rstd, f_root, f_norm, 0)
                dve.wait_ge(ld_x[1], 16)
                slot(0, True, False, True)
                slot(1, True, True, True)
                with dve.Fori(2, B - 1) as b:
                    slot(b, True, True, True)
                slot(B - 1, True, True, False)
                slot(B, False, True, False)


def phase_c(nc, sem, sb, bank, xres, nT_hi, nT_lo, cT_hi, cT_lo, gate, ident, neghalf,
            mask, wq_d, wkv_d, wo_d, qn_d, kn_d):
    LAG = 4
    N = G * B
    WQ_SLOT = {2: (0,), 3: (1,), 4: (2,), 5: (3,)}
    WO_SLOT = {1: (0, 1, 2, 3)}
    with ExitStack() as st:
        qT_hi = sb(st, "qT_hi", [P, HG, B * P], F32R)
        qT_lo = sb(st, "qT_lo", [P, HG, B * P], F32R)
        kT_hi = sb(st, "kT_hi", [P, B * P], F32R)
        kT_lo = sb(st, "kT_lo", [P, B * P], F32R)
        v_hi = sb(st, "v_hi", [P, B * P], F32R)
        v_lo = sb(st, "v_lo", [P, B * P], F32R)
        wq_raw = sb(st, "wq_raw", [P, HG, CH * P])
        wq_hi = sb(st, "wq_hi", [P, HG, CH * P], F32R)
        wq_lo = sb(st, "wq_lo", [P, HG, CH * P], F32R)
        wo_raw = sb(st, "wo_raw", [P, HG, D])
        wo_hi = sb(st, "wo_hi", [P, HG, D], F32R)
        wo_lo = sb(st, "wo_lo", [P, HG, D], F32R)
        wkv_raw = sb(st, "wkv_raw", [P, CH * 2 * P])
        wkv_hi = sb(st, "wkv_hi", [P, CH * 2 * P], F32R)
        wkv_lo = sb(st, "wkv_lo", [P, CH * 2 * P], F32R)
        score = sb(st, "score", [P, HG, P])
        prob = sb(st, "prob", [P, HG, P])
        probn = sb(st, "probn", [P, HG, P])
        pT_hi = sb(st, "pT_hi", [P, HG * P], F32R)
        pT_lo = sb(st, "pT_lo", [P, HG * P], F32R)
        oT_hi = sb(st, "oT_hi", [P, HG * P], F32R)
        oT_lo = sb(st, "oT_lo", [P, HG * P], F32R)
        qsq = sb(st, "qsq", [P, 4 * P])
        knat = sb(st, "knat", [P, P])
        ksq = sb(st, "ksq", [P, P])
        maskt = sb(st, "maskt", [P, P])
        ones = sb(st, "ones", [P, 1])
        norm_w = sb(st, "norm_w", [P, 2])
        wqk = sb(st, "wqk", [P, 1])
        qss = sb(st, "qss", [P, 4])
        rq = sb(st, "rq", [P, HG, B])
        kss = sb(st, "kss", [P, 1])
        kse = sb(st, "kse", [P, 1])
        rk = sb(st, "rk", [P, 1])
        nmax = sb(st, "nmax", [P, HG])
        esum = sb(st, "esum", [P, HG])
        erec = sb(st, "erec", [P, HG])

        s_bank, q_bank, pt_bank, kv_bank, o_bank, y_bank, ss_bank, kt_bank = bank

        ld_mask = sem("c_mask_loaded")
        ld_norm = sem("c_norm_weights_loaded")
        ld_wq = [sem(f"c_wq_loaded{h}") for h in range(HG)]
        ld_wo = [sem(f"c_wo_loaded{h}") for h in range(HG)]
        ld_wkv = sem("c_wkv_loaded")
        ones_set = sem("c_ones_set")
        wqk_done = sem("c_wqk")
        wq_h = sem("c_wq_high")
        wq_l = sem("c_wq_low")
        wo_h = sem("c_wo_high")
        wo_l = sem("c_wo_low")
        wkv_h = sem("c_wkv_high")
        wkv_l = sem("c_wkv_low")
        s_done = sem("c_scores")
        q_done = sem("c_q")
        pt_done = sem("c_probs_turned")
        kv_done = sem("c_kv")
        y_done = sem("c_y")
        o_done = sem("c_o")
        kt_done = sem("c_k_turned")
        ss_done = sem("c_q_squares_summed")
        exped = sem("c_exp")
        q_h = sem("c_q_high")
        q_sq = sem("c_q_squared")
        p_h = sem("c_p_high")
        k_sq = sem("c_k_squared")
        v_h = sem("c_v_high")
        o_h = sem("c_o_high")
        k_h = sem("c_k_high")
        masked = sem("c_scores_masked")
        maxed = sem("c_max")
        recip = sem("c_sum_reciprocal")
        q_l = sem("c_q_low")
        ss_out = sem("c_q_squares_out")
        p_l = sem("c_p_low")
        k_nat = sem("c_k_normed")
        v_l = sem("c_v_low")
        y_add = sem("c_y_added")
        o_l = sem("c_o_low")
        k_l = sem("c_k_low")
        normed = sem("c_probs_normed")
        rq_done = sem("c_rq")
        k_eps = sem("c_k_eps")
        rk_done = sem("c_rk")

        def loops(eng, slot):
            for s in range(B - LAG, B):
                slot(-1, s)
            for s in range(B):
                slot(0, s)
            with eng.Fori(1, G - 1) as g:
                for s in range(B):
                    slot(g, s)
            for s in range(B):
                slot(G - 1, s)
            for s in range(2):
                slot(G, s)

        def on(g, s, ahead):
            return not isinstance(g, int) or 0 <= B * g + s + ahead < N

        def at(s, ahead, n=P, width=1):
            b = (s + ahead) % B
            return slice(b * P, (b + 1) * P)

        with nc.Block() as block:
            @block.sync
            def _(sp):
                def row(d, i):
                    return d[i] if isinstance(i, int) else d[bass.ds(i, 1)].rearrange("a p n -> p (a n)")

                sp.dma_start(wkv_raw[:], wkv_d[0]).then_inc(ld_wkv, 16)
                for h in range(HG):
                    sp.dma_start(wq_raw[:, h, :], wq_d[h]).then_inc(ld_wq[h], 16)
                sp.dma_start(norm_w[:, 0:1], qn_d[:]).then_inc(ld_norm, 16)
                sp.wait_ge(ld_norm, 16)
                sp.dma_start(norm_w[:, 1:2], kn_d[:]).then_inc(ld_norm, 16)
                sp.dma_start(maskt[:], mask[:]).then_inc(ld_mask, 16)
                for h in range(HG):
                    sp.dma_start(wo_raw[:, h, :], wo_d[h]).then_inc(ld_wo[h], 16)

                def refills(g):
                    need(sp, wkv_l, g + 1)
                    sp.dma_start(wkv_raw[:], row(wkv_d, g + 1)).then_inc(ld_wkv, 16)
                    for h in range(HG):
                        need(sp, wq_l, HG * g + h + 1)
                        sp.dma_start(wq_raw[:, h, :], row(wq_d, HG * (g + 1) + h)).then_inc(ld_wq[h], 16)
                    for h in range(HG):
                        need(sp, wo_l, HG * g + h + 1)
                        sp.dma_start(wo_raw[:, h, :], row(wo_d, HG * (g + 1) + h)).then_inc(ld_wo[h], 16)

                refills(0)
                with sp.Fori(1, G - 1) as g:
                    refills(g)

            @block.gpsimd
            def _(pool):
                pool.memset(ones[:], 1.0).then_inc(ones_set, 1)

                def low_wq(g, h):
                    need(pool, wq_h, HG * g + h + 1)
                    pool.tensor_tensor(wq_lo[:, h, :], wq_raw[:, h, :], wq_hi[:, h, :].bitcast(F32),
                                       ALU.subtract).then_inc(wq_l, 1)

                def low_wkv(g):
                    need(pool, wkv_h, g + 1)
                    pool.tensor_tensor(wkv_lo[:], wkv_raw[:], wkv_hi[:].bitcast(F32),
                                       ALU.subtract).then_inc(wkv_l, 1)

                def low_wo(g, h):
                    need(pool, wo_h, HG * g + h + 1)
                    pool.tensor_tensor(wo_lo[:, h, :], wo_raw[:, h, :], wo_hi[:, h, :].bitcast(F32),
                                       ALU.subtract).then_inc(wo_l, 1)

                low_wkv(0)
                for h in range(HG):
                    low_wq(0, h)

                def slot(g, s):
                    n = B * g + s
                    filling = isinstance(g, int) and g < 0
                    following = not filling and on(g, 0, B)
                    if s == 4 and following:
                        low_wkv(g + 1)
                    if on(g, s, LAG):
                        need(pool, k_sq, n + LAG + 1, hold=True)
                        pool.tensor_scalar(kse[:], kss[:], P * RMS_EPS, None, ALU.add).then_inc(k_eps, 1)
                        need(pool, k_eps, n + LAG + 1)
                        need(pool, k_nat, n + LAG)
                        pool.tensor_tensor(rk[:], kse[:], neghalf[:, 0:1], ALU.pow).then_inc(rk_done, 1)
                    if on(g, s, 0):
                        need(pool, recip, n + 1)
                        need(pool, pt_done, n)
                        pool.tensor_tensor(probn[:], prob[:], erec[:].unsqueeze(2).broadcast_to([P, HG, P]),
                                           ALU.mult).then_inc(normed, 1)
                    if on(g, s, LAG):
                        need(pool, ss_out, n + LAG + 1)
                        first = 0 if s >= 4 else 4
                        pool.tensor_tensor(rq[:, s % HG, first:first + 4], qss[:], neghalf[:, 0:4],
                                           ALU.pow).then_inc(rq_done, 1)
                    if following:
                        for h in WQ_SLOT.get(s, ()):
                            low_wq(g + 1, h)
                    if not filling and on(g, 0, 0):
                        for h in WO_SLOT.get(s, ()):
                            low_wo(g, h)

                loops(pool, slot)

            @block.scalar
            def _(act):
                def high_wq(g, h):
                    need(act, ld_wq[h], 16 * g + 16)
                    need(act, q_done, B * (g - 1) + HG + h + 1)
                    act.activation(wq_hi[:, h, :], wq_raw[:, h, :], ACT.Copy).then_inc(wq_h, 1)

                def high_wkv(g):
                    need(act, ld_wkv, 16 * g + 16)
                    need(act, kv_done, B * g)
                    act.activation(wkv_hi[:], wkv_raw[:], ACT.Copy).then_inc(wkv_h, 1)

                def high_wo(g, h):
                    need(act, ld_wo[h], 16 * g + 16)
                    need(act, y_done, B * g)
                    act.activation(wo_hi[:, h, :], wo_raw[:, h, :], ACT.Copy).then_inc(wo_h, 1)

                high_wkv(0)
                for h in range(HG):
                    high_wq(0, h)

                def slot(g, s):
                    n = B * g + s
                    filling = isinstance(g, int) and g < 0
                    following = not filling and on(g, 0, B)
                    if s == 4 and following:
                        high_wkv(g + 1)
                    if on(g, s, 0):
                        need(act, maxed, n + 1)
                        need(act, normed, n)
                        for h in range(HG):
                            t = act.activation(prob[:, h, :], score[:, h, :], ACT.Exp, bias=nmax[:, h:h + 1],
                                               accum_out=esum[:, h:h + 1])
                        t.then_inc(exped, 1)
                    if on(g, s, LAG):
                        first = 0 if s >= 4 else 4
                        need(act, q_done, n + LAG + 1)
                        act.activation(qT_hi[:, s % HG, first * P:(first + 4) * P], q_bank[:],
                                       ACT.Copy).then_inc(q_h, 1)
                        need(act, ss_done, n + LAG)
                        act.activation(qsq[:], q_bank[:], ACT.Square).then_inc(q_sq, 1)
                    if on(g, s, LAG - 1):
                        need(act, kt_done, n + LAG)
                        act.activation(kT_hi[:, at(s, LAG - 1)], kt_bank[:, 0:P], ACT.Copy,
                                       scale=wqk[:]).then_inc(k_h, 1)
                    if on(g, s, -1):
                        need(act, pt_done, n)
                        act.activation(pT_hi[:], pt_bank[:], ACT.Copy).then_inc(p_h, 1)
                    if on(g, s, LAG):
                        need(act, kv_done, n + LAG + 1)
                        need(act, k_eps, n + LAG)
                        act.activation(ksq[:], kv_bank[:, 0:P], ACT.Square, accum_out=kss[:]).then_inc(k_sq, 1)
                        act.activation(v_hi[:, at(s, LAG)], kv_bank[:, P:2 * P], ACT.Copy).then_inc(v_h, 1)
                    if on(g, s, -1):
                        need(act, o_done, n)
                        need(act, y_done, n - 1)
                        act.activation(oT_hi[:], o_bank[:], ACT.Copy).then_inc(o_h, 1)
                    if following:
                        for h in WQ_SLOT.get(s, ()):
                            high_wq(g + 1, h)
                    if not filling and on(g, 0, 0):
                        for h in WO_SLOT.get(s, ()):
                            high_wo(g, h)

                act.wait_ge(wqk_done, 2)
                loops(act, slot)

            @block.tensor
            def _(pe):
                pe.wait_ge(ones_set, 1)

                def three_pass(out, l_hi, l_lo, r_hi, r_lo, start, stop):
                    pe.matmul(out, l_hi, r_hi, start=start, stop=False)
                    pe.matmul(out, l_hi, r_lo, start=False, stop=False)
                    return pe.matmul(out, l_lo, r_hi, start=False, stop=stop)

                def scores(g, s):
                    n = B * g + s
                    need(pe, k_h, n + 1)
                    need(pe, k_l, n + 1)
                    if s % HG == 0:
                        need(pe, q_h, n + HG)
                        need(pe, q_l, n + HG)
                    need(pe, masked, n)
                    for h in range(HG):
                        t = three_pass(s_bank[:, h * P:(h + 1) * P],
                                       qT_hi[:, h, at(s, 0)], qT_lo[:, h, at(s, 0)],
                                       kT_hi[:, at(s, 0)], kT_lo[:, at(s, 0)], True, True)
                    t.then_inc(s_done, 1)

                def project_q(g, s):
                    n, h = B * g + s, s % HG
                    first = 0 if s >= 4 else 4
                    half = slice(first * P, (first + 4) * P)
                    if s >= 4:
                        need(pe, wq_l, HG * (g + 1) + h + 1)
                    need(pe, q_h, n + LAG)
                    need(pe, q_l, n + LAG)
                    need(pe, q_sq, n + LAG)
                    for c in range(CH):
                        w = slice(c * P, (c + 1) * P)
                        t = three_pass(q_bank[:], wq_hi[:, h, w], wq_lo[:, h, w],
                                       nT_hi[:, c, half], nT_lo[:, c, half], c == 0, c == CH - 1)
                    t.then_inc(q_done, 1)

                def turn_probs(g, s):
                    n = B * g + s
                    need(pe, normed, n)
                    need(pe, p_h, n - 1)
                    need(pe, p_l, n - 1)
                    for h in range(HG):
                        t = pe.transpose(pt_bank[:, h * P:(h + 1) * P], probn[:, h, :], ident[:])
                    t.then_inc(pt_done, 1)

                def project_kv(g, s):
                    n = B * g + s
                    if s == 4:
                        need(pe, wkv_l, g + 2)
                    need(pe, k_nat, n + LAG)
                    need(pe, v_h, n + LAG)
                    need(pe, v_l, n + LAG)
                    for c in range(CH):
                        w = slice(c * 2 * P, (c + 1) * 2 * P)
                        t = three_pass(kv_bank[:, 0:2 * P], cT_hi[:, c, at(s, LAG)], cT_lo[:, c, at(s, LAG)],
                                       wkv_hi[:, w], wkv_lo[:, w], c == 0, c == CH - 1)
                    t.then_inc(kv_done, 1)

                def project_out(g, s):
                    n = B * g + s
                    need(pe, o_h, n - 1)
                    need(pe, o_l, n - 1)
                    need(pe, y_add, n - 2)
                    for h in range(HG):
                        if s == 2:
                            need(pe, wo_l, HG * g + h + 1)
                        w = slice(h * P, (h + 1) * P)
                        t = three_pass(y_bank[:], oT_hi[:, w], oT_lo[:, w], wo_hi[:, h, :], wo_lo[:, h, :],
                                       h == 0, h == HG - 1)
                    t.then_inc(y_done, 1)

                def probs_v(g, s):
                    n = B * g + s
                    need(pe, p_h, n)
                    need(pe, p_l, n)
                    need(pe, o_h, n - 1)
                    need(pe, o_l, n - 1)
                    three_pass(o_bank[:], v_hi[:, at(s, -1)], v_lo[:, at(s, -1)], pT_hi[:], pT_lo[:],
                               True, True).then_inc(o_done, 1)

                def sum_squares(g, s):
                    n = B * g + s
                    need(pe, q_sq, n + LAG + 1)
                    need(pe, ss_out, n + LAG)
                    for j in range(4):
                        t = pe.matmul(ss_bank[:, j:j + 1], qsq[:, j * P:(j + 1) * P], ones[:],
                                      start=True, stop=True)
                    t.then_inc(ss_done, 1)

                def turn_k(g, s):
                    n = B * g + s
                    need(pe, k_nat, n + LAG)
                    need(pe, k_h, n + LAG - 1)
                    need(pe, k_l, n + LAG - 1)
                    pe.transpose(kt_bank[:, 0:P], knat[:], ident[:]).then_inc(kt_done, 1)

                def slot(g, s):
                    if on(g, s, 0):
                        scores(g, s)
                    if on(g, s, LAG):
                        project_q(g, s)
                    if on(g, s, LAG - 1):
                        turn_k(g, s)
                    if on(g, s, -2) and s == 1:
                        project_out(g, s)
                    if on(g, s, -1):
                        turn_probs(g, s)
                    if on(g, s, LAG):
                        project_kv(g, s)
                    if on(g, s, -2) and s not in (1, 2):
                        project_out(g, s)
                    if on(g, s, LAG):
                        sum_squares(g, s)
                    if on(g, s, -1):
                        probs_v(g, s)
                    if on(g, s, -2) and s == 2:
                        project_out(g, s)

                loops(pe, slot)

            @block.vector
            def _(dve):
                dve.wait_ge(ld_mask, 16)
                dve.wait_ge(ld_norm, 32)
                dve.tensor_scalar(wqk[:], norm_w[:, 0:1], float(P) ** 0.5, None, ALU.mult).then_inc(wqk_done, 1)
                dve.wait_ge(wqk_done, 1)
                dve.tensor_scalar(wqk[:], wqk[:], norm_w[:, 1:2], None, ALU.mult).then_inc(wqk_done, 1)
                dve.wait_ge(wqk_done, 2)

                def slot(g, s):
                    n = B * g + s
                    if on(g, s, 0):
                        need(dve, s_done, n + 1)
                        need(dve, exped, n)
                        if s % HG == 0:
                            need(dve, rq_done, n + HG)
                        for h in range(HG):
                            t = dve.scalar_tensor_tensor(score[:, h, :], s_bank[:, h * P:(h + 1) * P],
                                                         rq[:, h, s:s + 1], maskt[:], ALU.mult, ALU.add)
                        t.then_inc(masked, 1)
                        need(dve, masked, n + 1)
                        dve.tensor_reduce(nmax[:], score[:], AX.X, ALU.max, negate=True).then_inc(maxed, 1)
                    if on(g, s, LAG):
                        first = 0 if s >= 4 else 4
                        half = slice(first * P, (first + 4) * P)
                        need(dve, q_h, n + LAG + 1)
                        need(dve, q_sq, n + LAG + 1)
                        dve.tensor_tensor(qT_lo[:, s % HG, half], q_bank[:],
                                          qT_hi[:, s % HG, half].bitcast(F32), ALU.subtract).then_inc(q_l, 1)
                    if on(g, s, LAG - 1):
                        need(dve, k_h, n + LAG)
                        dve.scalar_tensor_tensor(kT_lo[:, at(s, LAG - 1)], kt_bank[:, 0:P], wqk[:],
                                                 kT_hi[:, at(s, LAG - 1)].bitcast(F32),
                                                 ALU.mult, ALU.subtract).then_inc(k_l, 1)
                    if on(g, s, -1):
                        need(dve, p_h, n)
                        dve.tensor_tensor(pT_lo[:], pt_bank[:], pT_hi[:].bitcast(F32),
                                          ALU.subtract).then_inc(p_l, 1)
                    if on(g, s, 0):
                        need(dve, exped, n + 1)
                        need(dve, normed, n)
                        dve.reciprocal(erec[:], esum[:]).then_inc(recip, 1)
                    if on(g, s, LAG):
                        need(dve, rk_done, n + LAG + 1)
                        need(dve, kt_done, n + LAG)
                        need(dve, v_h, n + LAG + 1)
                        dve.tensor_scalar(knat[:], kv_bank[:, 0:P], rk[:], None, ALU.mult).then_inc(k_nat, 1)
                        dve.tensor_tensor(v_lo[:, at(s, LAG)], kv_bank[:, P:2 * P],
                                          v_hi[:, at(s, LAG)].bitcast(F32), ALU.subtract).then_inc(v_l, 1)
                    if on(g, s, -2) and s != 2:
                        add_out(g, s)
                    if on(g, s, LAG):
                        need(dve, ss_done, n + LAG + 1)
                        need(dve, rq_done, n + LAG)
                        dve.tensor_scalar(qss[:], ss_bank[:, 0:4], P * RMS_EPS, None, ALU.add).then_inc(ss_out, 1)
                    if on(g, s, -1):
                        need(dve, o_h, n)
                        dve.tensor_tensor(oT_lo[:], o_bank[:], oT_hi[:].bitcast(F32),
                                          ALU.subtract).then_inc(o_l, 1)
                    if on(g, s, -2) and s == 2:
                        add_out(g, s)

                def add_out(g, s):
                    n = B * g + s
                    b = (s - 2) % B
                    xb = xres[:, b * D:(b + 1) * D]
                    need(dve, y_done, n - 1)
                    need(dve, y_add, n - 2)
                    dve.scalar_tensor_tensor(xb, y_bank[:], gate[:, 2:3], xb, ALU.mult, ALU.add).then_inc(y_add, 1)

                loops(dve, slot)


def phase_d(nc, sem, sb, bank, xres, gate, ident, neghalf, lA_d, lB_d, lw_d, w1_d, b1_d, out):
    with ExitStack() as st:
        lA = sb(st, "lA", [P, D])
        lB = sb(st, "lB", [P, D])
        lw = sb(st, "lw", [P, 1])
        w1 = sb(st, "w1", [P, CH, D])
        b1 = sb(st, "b1", [P, D])
        coef = sb(st, "coef", [P, 1])
        lBc = sb(st, "lBc", [P, D])
        weff = sb(st, "weff", [P, CH, D])
        we_hi = sb(st, "we_hi", [P, CH, D], F32R)
        we_lo = sb(st, "we_lo", [P, CH, D], F32R)
        bg = sb(st, "bg", [P, D])
        stat = sb(st, "d_stat", [P, 2, 6])
        mv = sb(st, "d_mv", [P, 2, 2])
        rstd = sb(st, "d_rstd", [P, 2])
        n3 = sb(st, "n3", [P, 2, D])
        tT_hi = sb(st, "tT_hi", [P, 2, D], F32R)
        tT_lo = sb(st, "tT_lo", [P, 2, D], F32R)
        y = sb(st, "y", [P, 2, D])

        ld = [sem(f"d_loaded{i}") for i in range(5)]
        coefd = sem("d_coef")
        folded = sem("d_folded")
        we_sum = sem("d_weight_sum")
        we_h = sem("d_weight_high")
        we_l = sem("d_weight_low")
        stats = sem("d_stats")
        root = sem("d_root")
        norm = sem("d_norm")
        bias = sem("d_bias")
        turned = sem("d_turned")
        t_h = sem("d_turned_high")
        t_l = sem("d_turned_low")
        mm = sem("d_product")
        ysum = sem("d_y")
        stored = [sem("d_stored0"), sem("d_stored1")]
        W_BANKS, T_BANKS, Y_BANKS = bank[0:4], bank[4:6], bank[6:8]

        def xb(b):
            return xres[:, b * D:(b + 1) * D]

        with nc.Block() as block:
            @block.sync
            def _(sp):
                for t, d, s_ in ((lA, lA_d, ld[0]), (lB, lB_d, ld[1]), (lw, lw_d, ld[2]), (w1, w1_d, ld[3]),
                                 (b1, b1_d, ld[4])):
                    sp.dma_start(t[:], d[:]).then_inc(s_, 16)
                for b in range(B):
                    sp.wait_ge(ysum, b + 1)
                    if b >= 2:
                        sp.wait_ge(stored[b % 2], 16 * (b // 2))
                    sp.dma_start(out[b], y[:, b % 2, :]).then_inc(stored[b % 2], 16)
                for i in range(2):
                    sp.wait_ge(stored[i], 16 * B // 2)

            @block.gpsimd
            def _(pool):
                for b in range(B):
                    i = b % 2
                    pool.wait_ge(stats, 2 * b + 2)
                    pool.tensor_scalar(mv[:, i, 1:2], mv[:, i, 1:2], LN_EPS, None, ALU.add).then_inc(root, 1)
                    pool.wait_ge(root, 2 * b + 1)
                    pool.tensor_tensor(rstd[:, i:i + 1], mv[:, i, 1:2], neghalf[:, 0:1],
                                       ALU.pow).then_inc(root, 1)
                    pool.wait_ge(coefd, 3)
                    pool.wait_ge(norm, b + 1)
                    pool.tensor_tensor(xb(b), xb(b), bg[:], ALU.add).then_inc(bias, 1)

            @block.scalar
            def _(act):
                for c in range(CH):
                    act.wait_ge(we_sum, c + 1)
                    act.activation(we_hi[:, c, :], weff[:, c, :], ACT.Copy).then_inc(we_h, 1)
                for b in range(B):
                    i = b % 2
                    act.wait_ge(turned, b + 1)
                    if b >= 2:
                        act.wait_ge(mm, b - 1)
                    act.activation(tT_hi[:, i, :], T_BANKS[i][:], ACT.Copy).then_inc(t_h, 1)

            @block.tensor
            def _(pe):
                pe.wait_ge(coefd, 2)
                pe.wait_ge(ld[0], 16)
                for c in range(CH):
                    pe.matmul(W_BANKS[c][:], lA[:, c * P:(c + 1) * P], lBc[:],
                              start=True, stop=True).then_inc(folded, 1)

                def turn(b):
                    pe.wait_ge(norm, b + 1)
                    if b >= 2:
                        pe.wait_ge(t_l, b - 1)
                    for c in range(CH):
                        t = pe.transpose(T_BANKS[b % 2][:, c * P:(c + 1) * P], n3[:, b % 2, c * P:(c + 1) * P],
                                         ident[:])
                    t.then_inc(turned, 1)

                turn(0)
                pe.wait_ge(we_l, CH)
                for b in range(B):
                    if b + 1 < B:
                        turn(b + 1)
                    i = b % 2
                    pe.wait_ge(t_h, b + 1)
                    pe.wait_ge(t_l, b + 1)
                    if b >= 2:
                        pe.wait_ge(ysum, b - 1)
                    for c in range(CH):
                        w = slice(c * P, (c + 1) * P)
                        pe.matmul(Y_BANKS[i][:], tT_hi[:, i, w], we_hi[:, c, :], start=(c == 0), stop=False)
                        pe.matmul(Y_BANKS[i][:], tT_hi[:, i, w], we_lo[:, c, :], start=False, stop=False)
                        t = pe.matmul(Y_BANKS[i][:], tT_lo[:, i, w], we_hi[:, c, :],
                                      start=False, stop=(c == CH - 1))
                    t.then_inc(mm, 1)

            @block.vector
            def _(dve):
                def layer_norm(b):
                    i = b % 2
                    dve.bn_stats(stat[:, i, :], xb(b)).then_inc(stats, 1)
                    dve.wait_ge(stats, 2 * b + 1)
                    dve.bn_aggr(mv[:, i, :], stat[:, i, :]).then_inc(stats, 1)

                def normalise(b):
                    i = b % 2
                    dve.wait_ge(root, 2 * b + 2)
                    if b >= 2:
                        dve.wait_ge(turned, b - 1)
                    dve.tensor_scalar(n3[:, i, :], xb(b), mv[:, i, 0:1], rstd[:, i:i + 1],
                                      ALU.subtract, ALU.mult).then_inc(norm, 1)

                layer_norm(0)
                for i in (1, 2, 4):
                    dve.wait_ge(ld[i], 16)
                dve.tensor_scalar(coef[:], lw[:], 2.0, None, ALU.mult).then_inc(coefd, 1)
                dve.wait_ge(coefd, 1)
                dve.tensor_scalar(lBc[:], lB[:], coef[:], None, ALU.mult).then_inc(coefd, 1)
                dve.tensor_scalar(bg[:], b1[:], gate[:, 3:4], None, ALU.mult).then_inc(coefd, 1)
                normalise(0)
                layer_norm(1)
                dve.wait_ge(ld[3], 16)
                for c in range(CH):
                    dve.wait_ge(folded, c + 1)
                    dve.tensor_tensor(weff[:, c, :], W_BANKS[c][:], w1[:, c, :], ALU.add).then_inc(we_sum, 1)
                for c in range(CH):
                    dve.wait_ge(we_h, c + 1)
                    dve.tensor_tensor(we_lo[:, c, :], weff[:, c, :], we_hi[:, c, :].bitcast(F32),
                                      ALU.subtract).then_inc(we_l, 1)

                def low_part(b):
                    dve.wait_ge(t_h, b + 1)
                    dve.tensor_tensor(tT_lo[:, b % 2, :], T_BANKS[b % 2][:], tT_hi[:, b % 2, :].bitcast(F32),
                                      ALU.subtract).then_inc(t_l, 1)

                low_part(0)
                for b in range(B):
                    if b + 1 < B:
                        normalise(b + 1)
                    if b + 2 < B:
                        layer_norm(b + 2)
                    if b + 1 < B:
                        low_part(b + 1)
                    dve.wait_ge(mm, b + 1)
                    dve.wait_ge(bias, b + 1)
                    if b >= 2:
                        dve.wait_ge(stored[b % 2], 16 * (b // 2))
                    dve.scalar_tensor_tensor(y[:, b % 2, :], Y_BANKS[b % 2][:], gate[:, 3:4], xb(b),
                                             ALU.mult, ALU.add).then_inc(ysum, 1)


def dft_constants():
    import numpy as np
    t = np.arange(P)
    f = np.concatenate([np.arange(0, P // 2 + 1), np.arange(1, P // 2)])
    is_im = (np.arange(P) > P // 2)[:, None]
    ph = 2 * np.pi * np.outer(f, t) / P
    fwd = np.where(is_im, -np.sin(ph), np.cos(ph))
    fwd_sw = np.where(is_im, np.cos(ph), -np.sin(ph))
    weight = np.where((f == 0) | (f == P // 2), 1.0, 2.0)[:, None]
    inv1 = weight * np.cos(ph) / P
    inv2 = np.where(is_im, -1, 1) * weight * np.sin(ph) / P
    odd = np.concatenate([np.arange(P // 2)] * 2)
    is_im = (np.arange(P) >= P // 2)[:, None]
    ph = 2 * np.pi * np.outer(2 * odd + 1, t) / (2 * P)
    odd_fwd = np.where(is_im, -np.sin(ph), np.cos(ph))
    odd_fwd_sw = np.where(is_im, np.cos(ph), -np.sin(ph))
    odd_inv1 = np.cos(ph) / P
    odd_inv2 = np.where(is_im, 1, -1) * np.sin(ph) / P

    def less_last_row(m):
        m = m.copy()
        m[:, P - 1] -= m.sum(1)
        return m

    hold = np.zeros((P, P))
    hold[P - 1, :] = 0.5
    m = [fwd.T, fwd_sw.T, less_last_row(odd_fwd).T, less_last_row(odd_fwd_sw).T, odd_fwd.T, inv1, inv2,
         inv1 / 2, -inv2 / 2, odd_inv1, odd_inv2, hold, np.eye(P)]
    return np.ascontiguousarray(np.stack(m, axis=1).astype(np.float32))


def kernel(**inputs):
    import numpy as np
    import concourse.bacc as bacc
    from concourse.bass_utils import run_bass_kernel_spmd

    a = {k: np.asarray(v) for k, v in inputs.items()}

    def chunked(w):
        return w.reshape(w.shape[0], CH, P).transpose(2, 1, 0)

    wk = a["L1_xattn_Wk"].reshape(G, P, CH, P).transpose(0, 3, 2, 1)
    wv = a["L1_xattn_Wv"].reshape(G, P, CH, P).transpose(0, 3, 2, 1)
    laid = {
        "x": a["x"],
        "ctx_n": a["ctx_4096"],
        "ctx_t": chunked(a["ctx_4096"].reshape(B * P, D)),
        "mask": a["mask_1x1xSxS2_ff0"].reshape(P, P),
        "gates": np.broadcast_to(np.stack([a["g_xattn"][0], a["g_ffn"][0], a["g_xattn"][1], a["g_ffn"][1]]), (P, 4)),
        "dft": dft_constants(),
        "wbase": chunked(a["L0_ffn_W_base"]),
        "wag": np.concatenate([chunked(a["L0_ffn_A"].reshape(ER, D)), chunked(a["L0_ffn_W_gate"])], axis=2),
        "bb": np.broadcast_to(a["L0_ffn_b_base"], (P, D)),
        "bcat": a["L0_ffn_B"].transpose(0, 2, 1).reshape(ER, D),
        "wq": a["L1_xattn_Wq"].reshape(G * HG, P, CH, P).transpose(0, 3, 2, 1).reshape(G * HG, P, D),
        "wkv": np.concatenate([wk, wv], axis=3).reshape(G, P, CH * 2 * P),
        "wo": a["L1_xattn_Wo"].reshape(D, G * HG, P).transpose(1, 2, 0),
        "qn": a["L1_xattn_q_norm_w"].reshape(P, 1),
        "kn": a["L1_xattn_k_norm_w"].reshape(P, 1),
        "lA": a["L1_ffn_lora_A"].reshape(P, D),
        "lB": a["L1_ffn_lora_B"].transpose(0, 2, 1).reshape(P, D),
        "lw": np.repeat(a["L1_ffn_lora_weights"], R).reshape(P, 1),
        "w1": chunked(a["L1_ffn_W"]),
        "b1": np.broadcast_to(a["L1_ffn_bias"], (P, D)),
    }
    nc = bacc.Bacc("TRN2", target_bir_lowering=False, num_devices=1)
    arrays, args = {}, []
    for name, v in laid.items():
        v = np.ascontiguousarray(v)
        arrays[f"in_{name}"] = v
        args.append(nc.dram_tensor(f"in_{name}", v.shape, mybir.dt.from_np(v.dtype), kind="ExternalInput").ap())
    args.append(nc.dram_tensor("out_0", (B, P, D), F32, kind="ExternalOutput").ap())
    names = list(laid)
    by = dict(zip(names, args))
    flamingo_kernel(nc, by["x"], by["ctx_n"], by["ctx_t"], by["mask"], by["gates"], by["dft"], by["wbase"],
                    by["wag"], by["bb"], by["bcat"], by["wq"], by["wkv"], by["wo"], by["qn"], by["kn"],
                    by["lA"], by["lB"], by["lw"], by["w1"], by["b1"], args[-1])
    r = run_bass_kernel_spmd(nc, [arrays], core_ids=[0])
    return r.results[0]["out_0"]
```

```python
from contextlib import ExitStack

import concourse.bass as bass
from concourse import mybir

F32 = mybir.dt.float32
F32R = mybir.dt.float32r
ALU = mybir.AluOpType
ACT = mybir.ActivationFunctionType
AX = mybir.AxisListType

P = 128
B = 8
D = 512
CH = D // P
G = 8
HG = 4
E = 8
R = 16
ER = E * R
TOPK = 9
NEG = -(2.0 ** 127)
LN_EPS = 1e-5
RMS_EPS = 1e-5

(K_FWD, K_FWD_SW, V_ODD, V_ODD_SW, W_ODD, C_INV1, C_INV2,
 E_INV1, E_INV2, O_INV1, O_INV2, HOLD, IDENT) = range(13)
N_DFT = 13


def need(eng, sem, value, hold=False):
    if isinstance(value, int) and value <= 0:
        return
    eng.wait_ge(sem, value)
    if hold and not isinstance(value, int):
        eng.nop(nofuse=True)


def cols(start, n):
    return slice(start, start + n) if isinstance(start, int) else bass.ds(start, n)


def flamingo_kernel(nc, x, ctx_n, ctx_t, mask, gates, dft_d, wbase_d, wag_d, bb_d, bcat_d,
                    wq_d, wkv_d, wo_d, qn_d, kn_d, lA_d, lB_d, lw_d, w1_d, b1_d, out):
    with ExitStack() as top:
        def sem(name):
            return top.enter_context(nc.semaphore(name))

        def sb(stack, name, shape, dt=F32):
            return stack.enter_context(nc.sbuf_tensor(name, shape, dt))

        bank = [top.enter_context(nc.psum_tensor(f"bank{i}", [P, 512], F32)) for i in range(8)]

        xres = sb(top, "xres", [P, B * D])
        nT_hi = sb(top, "nT_hi", [P, CH, B * P], F32R)
        nT_lo = sb(top, "nT_lo", [P, CH, B * P], F32R)
        cT_hi = sb(top, "cT_hi", [P, CH, B * P], F32R)
        cT_lo = sb(top, "cT_lo", [P, CH, B * P], F32R)
        gate = sb(top, "gate", [P, 4])
        ident = sb(top, "ident", [P, P])
        neghalf = sb(top, "neghalf", [P, 8])

        phase_a(nc, sem, sb, bank, xres, nT_hi, nT_lo, cT_hi, cT_lo, gate, ident, neghalf,
                x, ctx_n, ctx_t, gates, dft_d, wbase_d, wag_d, bb_d, bcat_d)
        phase_c(nc, sem, sb, bank, xres, nT_hi, nT_lo, cT_hi, cT_lo, gate, ident, neghalf,
                mask, wq_d, wkv_d, wo_d, qn_d, kn_d)
        phase_d(nc, sem, sb, bank, xres, gate, ident, neghalf, lA_d, lB_d, lw_d, w1_d, b1_d, out)


def phase_a(nc, sem, sb, bank, xres, nT_hi, nT_lo, cT_hi, cT_lo, gate, ident, neghalf,
            x, ctx_n, ctx_t, gates, dft_d, wbase_d, wag_d, bb_d, bcat_d):
    with ExitStack() as st:
        ctxn = sb(st, "ctxn", [P, B * D])
        ctxt = sb(st, "ctxt", [P, CH, B * P])
        dft = sb(st, "dft", [P, N_DFT, P])
        wbase = sb(st, "wbase", [P, CH, D])
        wag = sb(st, "wag", [P, CH, ER + E])
        bcat = sb(st, "bcat", [P, D])
        bb = sb(st, "bb", [P, D])
        gates_in = sb(st, "gates_in", [P, 4])
        f_stat = sb(st, "f_stat", [P, 6])
        f_mv = sb(st, "f_mv", [P, 2])
        f_rstd = sb(st, "f_rstd", [P, 1])
        nx = sb(st, "nx", [P, D])
        kf = sb(st, "kf", [P, 4, D])
        prod1 = sb(st, "prod1", [P, D])
        prod2 = sb(st, "prod2", [P, D])
        top8 = sb(st, "top8", [P, CH, 8])
        next8 = sb(st, "next8", [P, CH, 8])
        ninth = sb(st, "ninth", [P, CH, 8])
        ntop = sb(st, "ntop", [P, CH])
        rest8 = sb(st, "rest8", [P, CH, P])
        rest9 = sb(st, "rest9", [P, CH, P])
        elag = sb(st, "elag", [P, CH, P])
        wlag = sb(st, "wlag", [P, CH, P])
        wsum = sb(st, "wsum", [P, CH])
        wrec = sb(st, "wrec", [P, CH])
        wlagn = sb(st, "wlagn", [P, CH, P])
        wT = sb(st, "wT", [P, D])
        op = sb(st, "op", [P, 4, D])
        h_stat = sb(st, "h_stat", [P, 6])
        h_mv = sb(st, "h_mv", [P, 2])
        h_rstd = sb(st, "h_rstd", [P, 1])
        n1 = sb(st, "n1", [P, D])
        n1T = sb(st, "n1T", [P, CH, P])
        lg = sb(st, "lg", [P, 2 * E])
        lg8 = sb(st, "lg8", [P, 8])
        two = sb(st, "two", [P, 8])
        nlg = sb(st, "nlg", [P, 1])
        eg = sb(st, "eg", [P, E])
        lgr = sb(st, "lgr", [P, 2 * E])
        rw = sb(st, "rw", [P, E])
        rsum = sb(st, "rsum", [P, 1])
        rrec = sb(st, "rrec", [P, 1])
        rwn = sb(st, "rwn", [P, E])
        hw = sb(st, "hw", [P, ER])
        hwT = sb(st, "hwT", [P, P])
        g_stat = sb(st, "g_stat", [P, 6])
        g_mv = sb(st, "g_mv", [P, 2])
        g_rstd = sb(st, "g_rstd", [P, 1])
        n2 = sb(st, "n2", [P, D])

        ld_g = sem("a_gates_loaded")
        CUTS = (0, 1, 3, B)
        ld_x = [sem(f"a_x_loaded{i}") for i in range(3)]
        ld_c = [sem(f"a_ctx_loaded{i}") for i in range(3)]
        ld_ct = sem("a_ctx_turned_loaded")
        ld_dft = sem("a_dft_loaded")
        ld_w = [sem(f"a_weights_loaded{i}") for i in range(4)]
        consts = sem("a_consts")
        tanhed = sem("a_gates_tanh")
        bias_gated = sem("a_bias_gated")
        ident_done = sem("a_ident")
        f_stats = sem("a_f_stats")
        f_root = sem("a_f_root")
        f_norm = sem("a_f_norm")
        q_fwd = sem("a_q_transformed")
        k_fwd = sem("a_ctx_transformed")
        k_copied = sem("a_ctx_dfts_copied")
        c_prod = sem("a_corr_products")
        corr = sem("a_corr_ready")
        picked = sem("a_lag_steps")
        lag9 = sem("a_ninth_steps")
        e_lag = sem("a_exp_lags")
        w_norm = sem("a_lag_weights")
        w_trans = sem("a_lag_weights_turned")
        w_copied = sem("a_lag_weights_copied")
        w_fwd = sem("a_lag_weights_transformed")
        o_prod = sem("a_out_products")
        f_out = sem("a_f_out")
        f_added = sem("a_f_added")
        h_stats = sem("a_h_stats")
        h_root = sem("a_h_root")
        h_norm = sem("a_h_norm")
        h_trans = sem("a_h_turned")
        h_copied = sem("a_h_copied")
        h_low = sem("a_router_ready")
        h_step = sem("a_router_steps")
        routed = sem("a_route_weights")
        h_exp = sem("a_router_exp")
        hw_trans = sem("a_hw_turned")
        hw_copied = sem("a_hw_copied")
        h_out = sem("a_h_out")
        h_bias = sem("a_bias_added")
        h_added = sem("a_h_added")
        g_stats = sem("a_g_stats")
        g_root = sem("a_g_root")
        g_norm = sem("a_g_norm")
        g_trans = sem("a_g_turned")
        g_hi = sem("a_g_high")
        g_lo = sem("a_g_low")
        ct_hi = sem("a_ctx_turned_high")
        ct_lo = sem("a_ctx_turned_low")

        PICK = 5
        ROUTE = 7

        def xb(b):
            return xres[:, cols(b * D, D)]

        def on(b):
            return not isinstance(b, int) or 0 <= b < B

        def looped(eng, slot):
            for b in range(3):
                slot(b)
            with eng.Fori(3, B - 2) as b:
                slot(b)
            for b in range(B - 2, B + 2):
                slot(b)

        with nc.Block() as block:
            @block.sync
            def _(sp):
                def load_batches(i):
                    a, z = CUTS[i], CUTS[i + 1]
                    sp.dma_start(xres[:, a * D:z * D].rearrange("p (b d) -> p b d", d=D),
                                 x[a:z].rearrange("b p d -> p b d")).then_inc(ld_x[i], 16)
                    sp.dma_start(ctxn[:, a * D:z * D].rearrange("p (b d) -> p b d", d=D),
                                 ctx_n[a:z].rearrange("b p d -> p b d")).then_inc(ld_c[i], 16)

                load_batches(0)
                sp.dma_start(dft[:], dft_d[:]).then_inc(ld_dft, 16)
                sp.dma_start(gates_in[:], gates[:]).then_inc(ld_g, 16)
                load_batches(1)
                sp.dma_start(wag[:], wag_d[:]).then_inc(ld_w[1], 16)
                sp.dma_start(wbase[:], wbase_d[:]).then_inc(ld_w[0], 16)
                sp.dma_start(bb[:], bb_d[:]).then_inc(ld_w[3], 16)
                sp.dma_start(bcat[:], bcat_d[:]).then_inc(ld_w[2], 16)
                load_batches(2)
                sp.dma_start(ctxt[:], ctx_t[:]).then_inc(ld_ct, 16)

            @block.gpsimd
            def _(pool):
                pool.memset(neghalf[:], -0.5).then_inc(consts, 1)
                pool.memset(ninth[:], NEG).then_inc(consts, 1)
                pool.memset(lg[:], NEG).then_inc(consts, 1)
                pool.memset(two[:], NEG).then_inc(consts, 1)
                pool.wait_ge(consts, 4)

                def inverse_root(stats, root, mv, rstd, n):
                    need(pool, stats, 2 * n + 2, hold=True)
                    pool.tensor_scalar(mv[:, 1:2], mv[:, 1:2], LN_EPS, None, ALU.add).then_inc(root, 1)
                    need(pool, root, 2 * n + 1)
                    pool.tensor_tensor(rstd[:], mv[:, 1:2], neghalf[:, 0:1], ALU.pow).then_inc(root, 1)

                def slot(b):
                    if on(b):
                        need(pool, picked, PICK * b + PICK)
                        need(pool, w_trans, b)
                        pool.tensor_tensor(wlagn[:], wlag[:],
                                           wrec[:].unsqueeze(2).broadcast_to([P, CH, P]),
                                           ALU.mult).then_inc(w_norm, 1)
                    if on(b - 1):
                        inverse_root(h_stats, h_root, h_mv, h_rstd, b - 1)
                    if on(b - 2):
                        inverse_root(g_stats, g_root, g_mv, g_rstd, b - 2)
                    if on(b - 1):
                        need(pool, h_norm, b)
                        pool.tensor_tensor(xb(b - 1), xb(b - 1), bb[:], ALU.add).then_inc(h_bias, 1)
                    if on(b + 2):
                        inverse_root(f_stats, f_root, f_mv, f_rstd, b + 2)
                    if on(b):
                        here = cols(b * P, P)
                        need(pool, ct_hi, b + 1)
                        pool.tensor_tensor(cT_lo[:, :, here], ctxt[:, :, here], cT_hi[:, :, here].bitcast(F32),
                                           ALU.subtract).then_inc(ct_lo, 1)

                inverse_root(f_stats, f_root, f_mv, f_rstd, 0)
                inverse_root(f_stats, f_root, f_mv, f_rstd, 1)
                pool.wait_ge(bias_gated, 1)
                looped(pool, slot)

            @block.scalar
            def _(act):
                act.wait_ge(ld_g, 16)
                act.activation(gate[:], gates_in[:], ACT.Tanh).then_inc(tanhed, 1)

                def copy_ctx_dfts(b):
                    for i in range(4):
                        if i % 2 == 0:
                            need(act, o_prod, 4 * b + i - 2)
                        need(act, k_fwd, 4 * b + i + 1)
                        act.activation(kf[:, i, :], bank[1 + i % 2][:], ACT.Copy).then_inc(k_copied, 1)

                def slot(b):
                    if on(b - 2):
                        need(act, hw_trans, b - 1)
                        act.activation(hwT[:], bank[5][:, 0:P], ACT.Copy).then_inc(hw_copied, 1)
                    if on(b):
                        need(act, picked, PICK * b + 3)
                        for j in range(CH):
                            act.activation(elag[:, j, :], bank[0][:, j * P:(j + 1) * P], ACT.Exp,
                                           bias=ntop[:, j:j + 1]).then_inc(e_lag, 1)
                        need(act, w_trans, b + 1)
                        act.activation(wT[:], bank[4][:], ACT.Copy).then_inc(w_copied, 1)
                    if on(b - 1):
                        need(act, h_trans, b)
                        act.activation(n1T[:].rearrange("p c t -> p (c t)"), bank[5][:],
                                       ACT.Copy).then_inc(h_copied, 1)
                    if on(b + 1):
                        copy_ctx_dfts(b + 1)
                    if on(b - 2):
                        need(act, g_trans, b - 1)
                        act.activation(nT_hi[:, :, cols((b - 2) * P, P)],
                                       bank[1][:].rearrange("p (c t) -> p c t", c=CH),
                                       ACT.Copy).then_inc(g_hi, 1)
                    if on(b):
                        here = cols(b * P, P)
                        if isinstance(b, int) and b == 0:
                            act.wait_ge(ld_ct, 16)
                        act.activation(cT_hi[:, :, here], ctxt[:, :, here], ACT.Copy).then_inc(ct_hi, 1)
                    if on(b - 1):
                        need(act, h_step, ROUTE * (b - 1) + 3)
                        act.activation(eg[:], lg[:, 0:E], ACT.Exp, bias=nlg[:]).then_inc(h_exp, 1)

                copy_ctx_dfts(0)
                looped(act, slot)

            @block.tensor
            def _(pe):
                pe.wait_ge(ld_dft, 16)
                first_of = {CUTS[i]: i for i in range(3)}

                def even_transforms(b):
                    if isinstance(b, int) and b in first_of:
                        pe.wait_ge(ld_c[first_of[b]], 16)
                    need(pe, f_norm, b + 1)
                    need(pe, e_lag, CH * b)
                    pe.matmul(bank[0][:], dft[:, K_FWD, :], nx[:], start=True, stop=True).then_inc(q_fwd, 1)
                    need(pe, g_lo, b - 3)
                    ctx_transforms(b, ((0, K_FWD), (1, K_FWD_SW)))

                def ctx_transforms(b, which):
                    for i, m in which:
                        need(pe, k_copied, 4 * b + i - 1)
                        pe.matmul(bank[1 + i % 2][:], dft[:, m, :], ctxn[:, cols(b * D, D)],
                                  start=True, stop=True).then_inc(k_fwd, 1)

                def odd_transforms(b):
                    ctx_transforms(b, ((2, V_ODD), (3, V_ODD_SW)))

                def slot(b):
                    if on(b):
                        need(pe, c_prod, 2 * b + 2)
                        for j in range(CH):
                            o = bank[0][:, j * P:(j + 1) * P]
                            pe.matmul(o, prod1[:, j * P:(j + 1) * P], dft[:, C_INV1, :], start=True, stop=False)
                            t = pe.matmul(o, prod2[:, j * P:(j + 1) * P], dft[:, C_INV2, :],
                                          start=False, stop=True)
                        t.then_inc(corr, 1)
                    if on(b - 2):
                        need(pe, h_step, ROUTE * (b - 1))
                        pe.transpose(bank[5][:, 0:P], hw[:], dft[:, IDENT, :]).then_inc(hw_trans, 1)
                    if on(b - 1):
                        pe.matmul(bank[3][:], dft[:, HOLD, :], ctxn[:, cols((b - 1) * D, D)],
                                  start=True, stop=False)
                        need(pe, o_prod, 4 * b)
                        for i, m in enumerate((E_INV1, E_INV2, O_INV1, O_INV2)):
                            t = pe.matmul(bank[3][:], dft[:, m, :], op[:, i, :], start=False, stop=(i == 3))
                        t.then_inc(f_out, 1)
                    if on(b - 2):
                        need(pe, hw_copied, b - 1)
                        pe.matmul(bank[6][:], hwT[:], bcat[:], start=False, stop=True).then_inc(h_out, 1)
                    if on(b + 1):
                        even_transforms(b + 1)
                    if on(b):
                        need(pe, w_norm, b + 1)
                        need(pe, o_prod, 4 * b)
                        for j in range(CH):
                            t = pe.transpose(bank[4][:, j * P:(j + 1) * P], wlagn[:, j, :], dft[:, IDENT, :])
                        t.then_inc(w_trans, 1)
                        need(pe, w_copied, b + 1)
                        need(pe, f_added, b)
                        pe.matmul(bank[3][:], dft[:, K_FWD, :], wT[:], start=True, stop=True).then_inc(w_fwd, 1)
                        pe.matmul(bank[4][:], dft[:, W_ODD, :], wT[:], start=True, stop=True).then_inc(w_fwd, 1)
                    if on(b - 1):
                        need(pe, h_norm, b)
                        for c in range(CH):
                            t = pe.transpose(bank[5][:, c * P:(c + 1) * P], n1[:, c * P:(c + 1) * P],
                                             dft[:, IDENT, :])
                        t.then_inc(h_trans, 1)
                        if isinstance(b, int) and b == 1:
                            for w in ld_w[0:3]:
                                pe.wait_ge(w, 16)
                        need(pe, h_copied, b)
                        for c in range(CH):
                            t = pe.matmul(bank[7][:, 0:ER + E], n1T[:, c, :], wag[:, c, :],
                                          start=(c == 0), stop=(c == CH - 1))
                        t.then_inc(h_low, 1)
                    if on(b + 1):
                        odd_transforms(b + 1)
                    if on(b - 2):
                        need(pe, g_norm, b - 1)
                        need(pe, k_copied, 4 * b + 7 if not isinstance(b, int) else min(4 * b + 7, 4 * B))
                        for c in range(CH):
                            t = pe.transpose(bank[1][:, c * P:(c + 1) * P], n2[:, c * P:(c + 1) * P],
                                             dft[:, IDENT, :])
                        t.then_inc(g_trans, 1)
                    if on(b - 1):
                        need(pe, h_added, b - 1)
                        for c in range(CH):
                            pe.matmul(bank[6][:], n1T[:, c, :], wbase[:, c, :], start=(c == 0), stop=False)

                even_transforms(0)
                odd_transforms(0)
                looped(pe, slot)

            @block.vector
            def _(dve):
                def statistics(b, stat, mv, done):
                    dve.bn_stats(stat[:], xb(b)).then_inc(done, 1)
                    need(dve, done, 2 * b + 1, hold=True)
                    dve.bn_aggr(mv[:], stat[:]).then_inc(done, 1)

                def normalise(dst, b, mv, rstd, root, done):
                    need(dve, root, 2 * b + 2)
                    dve.tensor_scalar(dst[:], xb(b), mv[:, 0:1], rstd[:], ALU.subtract, ALU.mult).then_inc(done, 1)

                def corr_products(b):
                    need(dve, k_copied, 4 * b + 1)
                    need(dve, q_fwd, b + 1)
                    dve.tensor_tensor(prod1[:], bank[0][:], kf[:, 0, :], ALU.mult).then_inc(c_prod, 1)
                    need(dve, k_copied, 4 * b + 2)
                    dve.tensor_tensor(prod2[:], bank[0][:], kf[:, 1, :], ALU.mult).then_inc(c_prod, 1)

                def pick_lags(b):
                    need(dve, corr, b + 1, hold=True)
                    for j in range(CH):
                        t = dve.max(top8[:, j, :], bank[0][:, j * P:(j + 1) * P])
                    t.then_inc(picked, 1)
                    need(dve, picked, PICK * b + 1)
                    dve.tensor_scalar(ntop[:], top8[:, :, 0], -1.0, None, ALU.mult).then_inc(picked, 1)
                    for j in range(CH):
                        t = dve.match_replace(rest8[:, j, :], top8[:, j, :], bank[0][:, j * P:(j + 1) * P], NEG)
                    t.then_inc(picked, 1)
                    need(dve, picked, PICK * b + 3, hold=True)
                    for j in range(CH):
                        t = dve.max(next8[:, j, :], rest8[:, j, :])
                    t.then_inc(lag9, 1)
                    need(dve, lag9, 3 * b + 1)
                    dve.tensor_copy(ninth[:, :, 0], next8[:, :, 0]).then_inc(lag9, 1)
                    need(dve, lag9, 3 * b + 2, hold=True)
                    for j in range(CH):
                        t = dve.match_replace(rest9[:, j, :], ninth[:, j, :], rest8[:, j, :], NEG)
                    t.then_inc(lag9, 1)
                    need(dve, lag9, 3 * b + 3)
                    need(dve, e_lag, CH * b + CH)
                    need(dve, w_norm, b)
                    for j in range(CH):
                        t = dve.scalar_tensor_tensor(wlag[:, j, :], rest9[:, j, :], NEG, elag[:, j, :],
                                                     ALU.is_equal, ALU.mult, accum_out=wsum[:, j:j + 1])
                    t.then_inc(picked, 1)
                    need(dve, picked, PICK * b + 4)
                    dve.reciprocal(wrec[:], wsum[:]).then_inc(picked, 1)

                def route(b):
                    n = ROUTE * b
                    need(dve, h_low, b + 1)
                    dve.tensor_copy(lg[:, 0:E], bank[7][:, ER:ER + E]).then_inc(h_step, 1)
                    need(dve, h_step, n + 1, hold=True)
                    dve.max(lg8[:], lg[:, 0:E]).then_inc(h_step, 1)
                    need(dve, h_step, n + 2)
                    dve.tensor_scalar(nlg[:], lg8[:, 0:1], -1.0, None, ALU.mult).then_inc(h_step, 1)
                    dve.tensor_copy(two[:, 0:2], lg8[:, 0:2]).then_inc(h_step, 1)
                    need(dve, h_step, n + 4, hold=True)
                    dve.match_replace(lgr[:], two[:], lg[:], NEG).then_inc(h_step, 1)
                    need(dve, h_step, n + 5)
                    need(dve, h_exp, b + 1)
                    dve.scalar_tensor_tensor(rw[:], lgr[:, 0:E], NEG, eg[:], ALU.is_equal, ALU.mult,
                                             accum_out=rsum[:]).then_inc(h_step, 1)
                    need(dve, h_step, n + 6)
                    dve.reciprocal(rrec[:], rsum[:]).then_inc(routed, 1)
                    need(dve, routed, 2 * b + 1)
                    dve.tensor_scalar(rwn[:], rw[:], rrec[:], None, ALU.mult).then_inc(routed, 1)
                    need(dve, routed, 2 * b + 2)
                    dve.tensor_tensor(hw[:].rearrange("p (e r) -> p e r", e=E),
                                      bank[7][:, 0:ER].rearrange("p (e r) -> p e r", e=E),
                                      rwn[:].unsqueeze(2).broadcast_to([P, E, R]), ALU.mult).then_inc(h_step, 1)

                def slot(b):
                    if on(b):
                        pick_lags(b)
                    if on(b - 1):
                        need(dve, f_out, b)
                        dve.scalar_tensor_tensor(xb(b - 1), bank[3][:], gate[:, 0:1], xb(b - 1),
                                                 ALU.mult, ALU.add).then_inc(f_added, 1)
                        need(dve, f_added, b, hold=True)
                        statistics(b - 1, h_stat, h_mv, h_stats)
                    if on(b - 2):
                        need(dve, h_out, b - 1)
                        need(dve, h_bias, b - 1)
                        dve.scalar_tensor_tensor(xb(b - 2), bank[6][:], gate[:, 1:2], xb(b - 2),
                                                 ALU.mult, ALU.add).then_inc(h_added, 1)
                        need(dve, h_added, b - 1, hold=True)
                        statistics(b - 2, g_stat, g_mv, g_stats)
                    if on(b - 1):
                        normalise(n1, b - 1, h_mv, h_rstd, h_root, h_norm)
                    if on(b):
                        need(dve, w_fwd, 2 * b + 1)
                        dve.tensor_tensor(op[:, 0, :], bank[3][:], kf[:, 0, :], ALU.mult).then_inc(o_prod, 1)
                        dve.tensor_tensor(op[:, 1, :], bank[3][:], kf[:, 1, :], ALU.mult).then_inc(o_prod, 1)
                        need(dve, w_fwd, 2 * b + 2)
                        dve.tensor_tensor(op[:, 2, :], bank[4][:], kf[:, 2, :], ALU.mult).then_inc(o_prod, 1)
                        dve.tensor_tensor(op[:, 3, :], bank[4][:], kf[:, 3, :], ALU.mult).then_inc(o_prod, 1)
                    if on(b - 2):
                        normalise(n2, b - 2, g_mv, g_rstd, g_root, g_norm)
                    if on(b + 1):
                        corr_products(b + 1)
                    if on(b - 2):
                        need(dve, g_hi, b - 1)
                        dve.tensor_tensor(nT_lo[:, :, cols((b - 2) * P, P)],
                                          bank[1][:].rearrange("p (c t) -> p c t", c=CH),
                                          nT_hi[:, :, cols((b - 2) * P, P)].bitcast(F32),
                                          ALU.subtract).then_inc(g_lo, 1)
                    if on(b + 2):
                        if isinstance(b, int) and b + 2 == CUTS[2]:
                            dve.wait_ge(ld_x[2], 16)
                        statistics(b + 2, f_stat, f_mv, f_stats)
                        need(dve, q_fwd, b + 2)
                        normalise(nx, b + 2, f_mv, f_rstd, f_root, f_norm)
                    if on(b - 1):
                        route(b - 1)

                dve.wait_ge(ld_x[0], 16)
                statistics(0, f_stat, f_mv, f_stats)
                normalise(nx, 0, f_mv, f_rstd, f_root, f_norm)
                dve.wait_ge(ld_dft, 16)
                dve.tensor_copy(ident[:], dft[:, IDENT, :]).then_inc(ident_done, 1)
                corr_products(0)
                dve.wait_ge(ld_x[1], 16)
                statistics(1, f_stat, f_mv, f_stats)
                normalise(nx, 1, f_mv, f_rstd, f_root, f_norm)
                dve.wait_ge(tanhed, 1)
                dve.wait_ge(ld_w[3], 16)
                dve.tensor_scalar(bb[:], bb[:], gate[:, 1:2], None, ALU.mult).then_inc(bias_gated, 1)
                looped(dve, slot)


def phase_c(nc, sem, sb, bank, xres, nT_hi, nT_lo, cT_hi, cT_lo, gate, ident, neghalf,
            mask, wq_d, wkv_d, wo_d, qn_d, kn_d):
    LAG = 4
    N = G * B
    WQ_SLOT = {2: (0,), 3: (1,), 4: (2,), 5: (3,)}
    WO_SLOT = {1: (0, 1, 2, 3)}
    with ExitStack() as st:
        qT_hi = sb(st, "qT_hi", [P, HG, B * P], F32R)
        qT_lo = sb(st, "qT_lo", [P, HG, B * P], F32R)
        kT = sb(st, "kT", [P, B, 2, P], F32R)
        v_hi = sb(st, "v_hi", [P, B * P], F32R)
        v_lo = sb(st, "v_lo", [P, B * P], F32R)
        wq_raw = sb(st, "wq_raw", [P, HG, CH * P])
        wq_hi = sb(st, "wq_hi", [P, HG, CH * P], F32R)
        wq_lo = sb(st, "wq_lo", [P, HG, CH * P], F32R)
        wo_raw = sb(st, "wo_raw", [P, HG, D])
        wo_hi = sb(st, "wo_hi", [P, HG, D], F32R)
        wo_lo = sb(st, "wo_lo", [P, HG, D], F32R)
        wkv_raw = sb(st, "wkv_raw", [P, CH * 2 * P])
        wkv_hi = sb(st, "wkv_hi", [P, CH * 2 * P], F32R)
        wkv_lo = sb(st, "wkv_lo", [P, CH * 2 * P], F32R)
        score = sb(st, "score", [P, HG, P])
        prob = sb(st, "prob", [P, HG, P])
        probn = sb(st, "probn", [P, HG, P])
        pT_hi = sb(st, "pT_hi", [P, HG * P], F32R)
        pT_lo = sb(st, "pT_lo", [P, HG * P], F32R)
        oT_hi = sb(st, "oT_hi", [P, HG * P], F32R)
        oT_lo = sb(st, "oT_lo", [P, HG * P], F32R)
        qsq = sb(st, "qsq", [P, 4 * P])
        knat = sb(st, "knat", [P, P])
        ksq = sb(st, "ksq", [P, P])
        maskt = sb(st, "maskt", [P, P])
        ones = sb(st, "ones", [P, 1])
        norm_w = sb(st, "norm_w", [P, 2])
        wqk = sb(st, "wqk", [P, 1])
        qss = sb(st, "qss", [P, 4])
        rq = sb(st, "rq", [P, HG, B])
        kss = sb(st, "kss", [P, 1])
        kse = sb(st, "kse", [P, 1])
        rk = sb(st, "rk", [P, 1])
        nmax = sb(st, "nmax", [P, HG])
        esum = sb(st, "esum", [P, HG])
        erec = sb(st, "erec", [P, HG])

        s_banks = (bank[0], bank[7])
        q_bank, pt_bank, kv_bank, o_bank, y_bank = bank[1:6]
        kt_bank = bank[6][:, 0:P]
        ss_bank = bank[6][:, P:P + 4]

        ld_mask = sem("c_mask_loaded")
        ld_norm = sem("c_norm_weights_loaded")
        ld_wq = [sem(f"c_wq_loaded{h}") for h in range(HG)]
        ld_wo = [sem(f"c_wo_loaded{h}") for h in range(HG)]
        ld_wkv = sem("c_wkv_loaded")
        ones_set = sem("c_ones_set")
        wqk_done = sem("c_wqk")
        wq_h = sem("c_wq_high")
        wq_l = sem("c_wq_low")
        wo_h = sem("c_wo_high")
        wo_l = sem("c_wo_low")
        wkv_h = sem("c_wkv_high")
        wkv_l = sem("c_wkv_low")
        s_done = sem("c_scores")
        q_done = sem("c_q")
        pt_done = sem("c_probs_turned")
        kv_done = sem("c_kv")
        y_done = sem("c_y")
        o_done = sem("c_o")
        kt_done = sem("c_k_turned")
        ss_done = sem("c_q_squares_summed")
        exped = sem("c_exp")
        q_h = sem("c_q_high")
        q_sq = sem("c_q_squared")
        p_h = sem("c_p_high")
        k_sq = sem("c_k_squared")
        v_h = sem("c_v_high")
        o_h = sem("c_o_high")
        k_h = sem("c_k_high")
        masked = sem("c_scores_masked")
        maxed = sem("c_max")
        recip = sem("c_sum_reciprocal")
        q_l = sem("c_q_low")
        ss_out = sem("c_q_squares_out")
        p_l = sem("c_p_low")
        k_nat = sem("c_k_normed")
        v_l = sem("c_v_low")
        y_add = sem("c_y_added")
        o_l = sem("c_o_low")
        k_l = sem("c_k_low")
        normed = sem("c_probs_normed")
        rq_done = sem("c_rq")
        k_eps = sem("c_k_eps")
        rk_done = sem("c_rk")

        def loops(eng, slot):
            for s in range(B - LAG, B):
                slot(-1, s)
            for s in range(B):
                slot(0, s)
            with eng.Fori(1, G - 1) as g:
                for s in range(B):
                    slot(g, s)
            for s in range(B):
                slot(G - 1, s)
            for s in range(2):
                slot(G, s)

        def on(g, s, ahead):
            return not isinstance(g, int) or 0 <= B * g + s + ahead < N

        def at(s, ahead, n=P, width=1):
            b = (s + ahead) % B
            return slice(b * P, (b + 1) * P)

        with nc.Block() as block:
            @block.sync
            def _(sp):
                def row(d, i):
                    return d[i] if isinstance(i, int) else d[bass.ds(i, 1)].rearrange("a p n -> p (a n)")

                sp.dma_start(wkv_raw[:], wkv_d[0]).then_inc(ld_wkv, 16)
                for h in range(HG):
                    sp.dma_start(wq_raw[:, h, :], wq_d[h]).then_inc(ld_wq[h], 16)
                sp.dma_start(norm_w[:, 0:1], qn_d[:]).then_inc(ld_norm, 16)
                sp.wait_ge(ld_norm, 16)
                sp.dma_start(norm_w[:, 1:2], kn_d[:]).then_inc(ld_norm, 16)
                sp.dma_start(maskt[:], mask[:]).then_inc(ld_mask, 16)
                for h in range(HG):
                    sp.dma_start(wo_raw[:, h, :], wo_d[h]).then_inc(ld_wo[h], 16)

                def refills(g):
                    need(sp, wkv_l, g + 1)
                    sp.dma_start(wkv_raw[:], row(wkv_d, g + 1)).then_inc(ld_wkv, 16)
                    for h in range(HG):
                        need(sp, wq_l, HG * g + h + 1)
                        sp.dma_start(wq_raw[:, h, :], row(wq_d, HG * (g + 1) + h)).then_inc(ld_wq[h], 16)
                    for h in range(HG):
                        need(sp, wo_l, HG * g + h + 1)
                        sp.dma_start(wo_raw[:, h, :], row(wo_d, HG * (g + 1) + h)).then_inc(ld_wo[h], 16)

                refills(0)
                with sp.Fori(1, G - 1) as g:
                    refills(g)

            @block.gpsimd
            def _(pool):
                pool.memset(ones[:], 1.0).then_inc(ones_set, 1)

                def low_wq(g, h):
                    need(pool, wq_h, HG * g + h + 1)
                    pool.tensor_tensor(wq_lo[:, h, :], wq_raw[:, h, :], wq_hi[:, h, :].bitcast(F32),
                                       ALU.subtract).then_inc(wq_l, 1)

                def low_wkv(g):
                    need(pool, wkv_h, g + 1)
                    pool.tensor_tensor(wkv_lo[:], wkv_raw[:], wkv_hi[:].bitcast(F32),
                                       ALU.subtract).then_inc(wkv_l, 1)

                def low_wo(g, h):
                    need(pool, wo_h, HG * g + h + 1)
                    pool.tensor_tensor(wo_lo[:, h, :], wo_raw[:, h, :], wo_hi[:, h, :].bitcast(F32),
                                       ALU.subtract).then_inc(wo_l, 1)

                low_wkv(0)
                for h in range(HG):
                    low_wq(0, h)

                def slot(g, s):
                    n = B * g + s
                    filling = isinstance(g, int) and g < 0
                    following = not filling and on(g, 0, B)
                    if s == 4 and following:
                        low_wkv(g + 1)
                    if on(g, s, 0):
                        need(pool, recip, n + 1)
                        need(pool, pt_done, n)
                        pool.tensor_tensor(probn[:], prob[:], erec[:].unsqueeze(2).broadcast_to([P, HG, P]),
                                           ALU.mult).then_inc(normed, 1)
                    if on(g, s, LAG):
                        need(pool, k_sq, n + LAG + 1, hold=True)
                        pool.tensor_scalar(kse[:], kss[:], P * RMS_EPS, None, ALU.add).then_inc(k_eps, 1)
                        need(pool, k_eps, n + LAG + 1)
                        need(pool, k_nat, n + LAG)
                        pool.tensor_tensor(rk[:], kse[:], neghalf[:, 0:1], ALU.pow).then_inc(rk_done, 1)
                    if on(g, s, LAG):
                        need(pool, ss_out, n + LAG + 1)
                        first = 0 if s >= 4 else 4
                        pool.tensor_tensor(rq[:, s % HG, first:first + 4], qss[:], neghalf[:, 0:4],
                                           ALU.pow).then_inc(rq_done, 1)
                    if following:
                        for h in WQ_SLOT.get(s, ()):
                            low_wq(g + 1, h)
                    if not filling and on(g, 0, 0):
                        for h in WO_SLOT.get(s, ()):
                            low_wo(g, h)

                loops(pool, slot)

            @block.scalar
            def _(act):
                def high_wq(g, h):
                    need(act, ld_wq[h], 16 * g + 16)
                    need(act, q_done, B * (g - 1) + HG + h + 1)
                    act.activation(wq_hi[:, h, :], wq_raw[:, h, :], ACT.Copy).then_inc(wq_h, 1)

                def high_wkv(g):
                    need(act, ld_wkv, 16 * g + 16)
                    need(act, kv_done, B * g)
                    act.activation(wkv_hi[:], wkv_raw[:], ACT.Copy).then_inc(wkv_h, 1)

                def high_wo(g, h):
                    need(act, ld_wo[h], 16 * g + 16)
                    need(act, y_done, B * g)
                    act.activation(wo_hi[:, h, :], wo_raw[:, h, :], ACT.Copy).then_inc(wo_h, 1)

                def exponents(n):
                    need(act, maxed, n + 1)
                    need(act, normed, n)
                    for h in range(HG):
                        t = act.activation(prob[:, h, :], score[:, h, :], ACT.Exp, bias=nmax[:, h:h + 1],
                                           accum_out=esum[:, h:h + 1])
                    t.then_inc(exped, 1)

                high_wkv(0)
                for h in range(HG):
                    high_wq(0, h)

                def slot(g, s):
                    n = B * g + s
                    filling = isinstance(g, int) and g < 0
                    following = not filling and on(g, 0, B)
                    if s == 4 and following:
                        high_wkv(g + 1)
                    if on(g, s, LAG):
                        first = 0 if s >= 4 else 4
                        need(act, q_done, n + LAG + 1)
                        act.activation(qT_hi[:, s % HG, first * P:(first + 4) * P], q_bank[:],
                                       ACT.Copy).then_inc(q_h, 1)
                        need(act, ss_done, n + LAG)
                        act.activation(qsq[:], q_bank[:], ACT.Square).then_inc(q_sq, 1)
                    if on(g, s, LAG - 1):
                        need(act, kt_done, n + LAG)
                        act.activation(kT[:, (s + LAG - 1) % B, 0, :], kt_bank, ACT.Copy,
                                       scale=wqk[:]).then_inc(k_h, 1)
                    if on(g, s, 0) and s != 2:
                        exponents(n)
                    if on(g, s, -1):
                        need(act, pt_done, n)
                        act.activation(pT_hi[:], pt_bank[:], ACT.Copy).then_inc(p_h, 1)
                    if on(g, s, 0) and s == 2:
                        exponents(n)
                    if on(g, s, LAG):
                        need(act, kv_done, n + LAG + 1)
                        need(act, k_eps, n + LAG)
                        act.activation(ksq[:], kv_bank[:, 0:P], ACT.Square, accum_out=kss[:]).then_inc(k_sq, 1)
                        act.activation(v_hi[:, at(s, LAG)], kv_bank[:, P:2 * P], ACT.Copy).then_inc(v_h, 1)
                    if on(g, s, -1):
                        need(act, o_done, n)
                        need(act, y_done, n - 1)
                        act.activation(oT_hi[:], o_bank[:], ACT.Copy).then_inc(o_h, 1)
                    if following:
                        for h in WQ_SLOT.get(s, ()):
                            high_wq(g + 1, h)
                    if not filling and on(g, 0, 0):
                        for h in WO_SLOT.get(s, ()):
                            high_wo(g, h)

                act.wait_ge(wqk_done, 2)
                loops(act, slot)

            @block.tensor
            def _(pe):
                pe.wait_ge(ones_set, 1)

                def three_pass(out, l_hi, l_lo, r_hi, r_lo, start, stop):
                    pe.matmul(out, l_hi, r_hi, start=start, stop=False)
                    pe.matmul(out, l_hi, r_lo, start=False, stop=False)
                    return pe.matmul(out, l_lo, r_hi, start=False, stop=stop)

                def scores(g, s):
                    n = B * g + s
                    need(pe, k_h, n + 1)
                    need(pe, k_l, n + 1)
                    if s % HG == 0:
                        need(pe, q_h, n + HG)
                        need(pe, q_l, n + HG)
                    need(pe, masked, 2 * n)
                    for h in range(HG):
                        o = s_banks[h // 2][:, h % 2 * 2 * P:(h % 2 + 1) * 2 * P]
                        pe.matmul(o, qT_hi[:, h, at(s, 0)], kT[:, s, :, :].rearrange("p i t -> p (i t)"),
                                  start=True, stop=True, skip_group_check=True)
                        t = pe.matmul(o[:, 0:P], qT_lo[:, h, at(s, 0)], kT[:, s, 0, :], start=False, stop=True,
                                      skip_group_check=True)
                    t.then_inc(s_done, 1)

                def project_q(g, s):
                    n, h = B * g + s, s % HG
                    first = 0 if s >= 4 else 4
                    half = slice(first * P, (first + 4) * P)
                    if s >= 4:
                        need(pe, wq_l, HG * (g + 1) + h + 1)
                    need(pe, q_h, n + LAG)
                    need(pe, q_l, n + LAG)
                    need(pe, q_sq, n + LAG)
                    for c in range(CH):
                        w = slice(c * P, (c + 1) * P)
                        t = three_pass(q_bank[:], wq_hi[:, h, w], wq_lo[:, h, w],
                                       nT_hi[:, c, half], nT_lo[:, c, half], c == 0, c == CH - 1)
                    t.then_inc(q_done, 1)

                def turn_probs(g, s):
                    n = B * g + s
                    need(pe, normed, n)
                    need(pe, p_h, n - 1)
                    need(pe, p_l, n - 1)
                    for h in range(HG):
                        t = pe.transpose(pt_bank[:, h * P:(h + 1) * P], probn[:, h, :], ident[:])
                    t.then_inc(pt_done, 1)

                def project_kv(g, s):
                    n = B * g + s
                    if s == 4:
                        need(pe, wkv_l, g + 2)
                    need(pe, k_nat, n + LAG)
                    need(pe, v_h, n + LAG)
                    need(pe, v_l, n + LAG)
                    for c in range(CH):
                        w = slice(c * 2 * P, (c + 1) * 2 * P)
                        t = three_pass(kv_bank[:, 0:2 * P], cT_hi[:, c, at(s, LAG)], cT_lo[:, c, at(s, LAG)],
                                       wkv_hi[:, w], wkv_lo[:, w], c == 0, c == CH - 1)
                    t.then_inc(kv_done, 1)

                def project_out(g, s):
                    n = B * g + s
                    need(pe, o_h, n - 1)
                    need(pe, o_l, n - 1)
                    need(pe, y_add, n - 2)
                    for h in range(HG):
                        if s == 2:
                            need(pe, wo_l, HG * g + h + 1)
                        w = slice(h * P, (h + 1) * P)
                        t = three_pass(y_bank[:], oT_hi[:, w], oT_lo[:, w], wo_hi[:, h, :], wo_lo[:, h, :],
                                       h == 0, h == HG - 1)
                    t.then_inc(y_done, 1)

                def probs_v(g, s):
                    n = B * g + s
                    need(pe, p_h, n)
                    need(pe, p_l, n)
                    need(pe, o_h, n - 1)
                    need(pe, o_l, n - 1)
                    three_pass(o_bank[:], v_hi[:, at(s, -1)], v_lo[:, at(s, -1)], pT_hi[:], pT_lo[:],
                               True, True).then_inc(o_done, 1)

                def sum_squares(g, s):
                    n = B * g + s
                    need(pe, q_sq, n + LAG + 1)
                    need(pe, k_h, n + LAG)
                    need(pe, k_l, n + LAG)
                    for j in range(4):
                        t = pe.matmul(ss_bank[:, j:j + 1], qsq[:, j * P:(j + 1) * P], ones[:],
                                      start=True, stop=True)
                    t.then_inc(ss_done, 1)

                def turn_k(g, s):
                    n = B * g + s
                    need(pe, k_nat, n + LAG)
                    need(pe, ss_out, n + LAG)
                    pe.transpose(kt_bank, knat[:], ident[:]).then_inc(kt_done, 1)

                def slot(g, s):
                    if on(g, s, 0):
                        scores(g, s)
                    if on(g, s, LAG):
                        project_q(g, s)
                    if on(g, s, LAG - 1):
                        turn_k(g, s)
                    if on(g, s, -2) and s != 2:
                        project_out(g, s)
                    if on(g, s, -1):
                        turn_probs(g, s)
                    if on(g, s, LAG):
                        project_kv(g, s)
                    if on(g, s, LAG):
                        sum_squares(g, s)
                    if on(g, s, -1):
                        probs_v(g, s)
                    if on(g, s, -2) and s == 2:
                        project_out(g, s)

                loops(pe, slot)

            @block.vector
            def _(dve):
                dve.wait_ge(ld_mask, 16)
                dve.wait_ge(ld_norm, 32)
                dve.tensor_scalar(wqk[:], norm_w[:, 0:1], float(P) ** 0.5, None, ALU.mult).then_inc(wqk_done, 1)
                dve.wait_ge(wqk_done, 1)
                dve.tensor_scalar(wqk[:], wqk[:], norm_w[:, 1:2], None, ALU.mult).then_inc(wqk_done, 1)
                dve.wait_ge(wqk_done, 2)

                def slot(g, s):
                    n = B * g + s
                    if on(g, s, 0):
                        need(dve, s_done, n + 1)
                        need(dve, exped, n)
                        if s % HG == 0:
                            need(dve, rq_done, n + HG)
                        for part, more in ((1, maskt), (0, None)):
                            for h in range(HG):
                                o = s_banks[h // 2][:, (h % 2 * 2 + part) * P:(h % 2 * 2 + part + 1) * P]
                                t = dve.scalar_tensor_tensor(score[:, h, :], o, rq[:, h, s:s + 1],
                                                             score[:, h, :] if more is None else more[:],
                                                             ALU.mult, ALU.add)
                            t.then_inc(masked, 1)
                            need(dve, masked, 2 * n + 2 - part)
                        dve.tensor_reduce(nmax[:], score[:], AX.X, ALU.max, negate=True).then_inc(maxed, 1)
                    if on(g, s, LAG):
                        first = 0 if s >= 4 else 4
                        half = slice(first * P, (first + 4) * P)
                        need(dve, q_h, n + LAG + 1)
                        need(dve, q_sq, n + LAG + 1)
                        dve.tensor_tensor(qT_lo[:, s % HG, half], q_bank[:],
                                          qT_hi[:, s % HG, half].bitcast(F32), ALU.subtract).then_inc(q_l, 1)
                    if on(g, s, LAG - 1):
                        need(dve, k_h, n + LAG)
                        dve.scalar_tensor_tensor(kT[:, (s + LAG - 1) % B, 1, :], kt_bank, wqk[:],
                                                 kT[:, (s + LAG - 1) % B, 0, :].bitcast(F32),
                                                 ALU.mult, ALU.subtract).then_inc(k_l, 1)
                    if on(g, s, 0) and s != 2:
                        reciprocals(n)
                    if on(g, s, -2) and s != 2:
                        add_out(g, s)
                    if on(g, s, -1):
                        need(dve, p_h, n)
                        dve.tensor_tensor(pT_lo[:], pt_bank[:], pT_hi[:].bitcast(F32),
                                          ALU.subtract).then_inc(p_l, 1)
                    if on(g, s, 0) and s == 2:
                        reciprocals(n)
                    if on(g, s, LAG):
                        need(dve, rk_done, n + LAG + 1)
                        need(dve, kt_done, n + LAG)
                        need(dve, v_h, n + LAG + 1)
                        dve.tensor_scalar(knat[:], kv_bank[:, 0:P], rk[:], None, ALU.mult).then_inc(k_nat, 1)
                        dve.tensor_tensor(v_lo[:, at(s, LAG)], kv_bank[:, P:2 * P],
                                          v_hi[:, at(s, LAG)].bitcast(F32), ALU.subtract).then_inc(v_l, 1)
                    if on(g, s, LAG):
                        need(dve, ss_done, n + LAG + 1)
                        need(dve, rq_done, n + LAG)
                        dve.tensor_scalar(qss[:], ss_bank, P * RMS_EPS, None, ALU.add).then_inc(ss_out, 1)
                    if on(g, s, -1):
                        need(dve, o_h, n)
                        dve.tensor_tensor(oT_lo[:], o_bank[:], oT_hi[:].bitcast(F32),
                                          ALU.subtract).then_inc(o_l, 1)
                    if on(g, s, -2) and s == 2:
                        add_out(g, s)

                def reciprocals(n):
                    need(dve, exped, n + 1)
                    need(dve, normed, n)
                    dve.reciprocal(erec[:], esum[:]).then_inc(recip, 1)

                def add_out(g, s):
                    n = B * g + s
                    b = (s - 2) % B
                    xb = xres[:, b * D:(b + 1) * D]
                    need(dve, y_done, n - 1)
                    need(dve, y_add, n - 2)
                    dve.scalar_tensor_tensor(xb, y_bank[:], gate[:, 2:3], xb, ALU.mult, ALU.add).then_inc(y_add, 1)

                loops(dve, slot)


def phase_d(nc, sem, sb, bank, xres, gate, ident, neghalf, lA_d, lB_d, lw_d, w1_d, b1_d, out):
    with ExitStack() as st:
        lA = sb(st, "lA", [P, D])
        lB = sb(st, "lB", [P, D])
        lw = sb(st, "lw", [P, 1])
        w1 = sb(st, "w1", [P, CH, D])
        b1 = sb(st, "b1", [P, D])
        coef = sb(st, "coef", [P, 1])
        lBc = sb(st, "lBc", [P, D])
        weff = sb(st, "weff", [P, CH, D])
        we_hi = sb(st, "we_hi", [P, CH, D], F32R)
        we_lo = sb(st, "we_lo", [P, CH, D], F32R)
        bg = sb(st, "bg", [P, D])
        stat = sb(st, "d_stat", [P, 2, 6])
        mv = sb(st, "d_mv", [P, 2, 2])
        rstd = sb(st, "d_rstd", [P, 2])
        n3 = sb(st, "n3", [P, 2, D])
        tT_hi = sb(st, "tT_hi", [P, 2, D], F32R)
        tT_lo = sb(st, "tT_lo", [P, 2, D], F32R)
        y = sb(st, "y", [P, 2, D])

        ld = [sem(f"d_loaded{i}") for i in range(5)]
        coefd = sem("d_coef")
        folded = sem("d_folded")
        we_sum = sem("d_weight_sum")
        we_h = sem("d_weight_high")
        we_l = sem("d_weight_low")
        stats = sem("d_stats")
        root = sem("d_root")
        norm = sem("d_norm")
        bias = sem("d_bias")
        turned = sem("d_turned")
        t_h = sem("d_turned_high")
        t_l = sem("d_turned_low")
        mm = sem("d_product")
        ysum = sem("d_y")
        stored = [sem("d_stored0"), sem("d_stored1")]
        W_BANKS, T_BANKS, Y_BANKS = bank[0:4], bank[4:6], bank[6:8]

        def xb(b):
            return xres[:, b * D:(b + 1) * D]

        with nc.Block() as block:
            @block.sync
            def _(sp):
                for t, d, s_ in ((lA, lA_d, ld[0]), (lB, lB_d, ld[1]), (lw, lw_d, ld[2]), (w1, w1_d, ld[3]),
                                 (b1, b1_d, ld[4])):
                    sp.dma_start(t[:], d[:]).then_inc(s_, 16)
                for b in range(B):
                    sp.wait_ge(ysum, b + 1)
                    if b >= 2:
                        sp.wait_ge(stored[b % 2], 16 * (b // 2))
                    sp.dma_start(out[b], y[:, b % 2, :]).then_inc(stored[b % 2], 16)
                for i in range(2):
                    sp.wait_ge(stored[i], 16 * B // 2)

            @block.gpsimd
            def _(pool):
                for b in range(B):
                    i = b % 2
                    pool.wait_ge(stats, 2 * b + 2)
                    pool.tensor_scalar(mv[:, i, 1:2], mv[:, i, 1:2], LN_EPS, None, ALU.add).then_inc(root, 1)
                    pool.wait_ge(root, 2 * b + 1)
                    pool.tensor_tensor(rstd[:, i:i + 1], mv[:, i, 1:2], neghalf[:, 0:1],
                                       ALU.pow).then_inc(root, 1)
                    pool.wait_ge(coefd, 3)
                    pool.wait_ge(norm, b + 1)
                    pool.tensor_tensor(xb(b), xb(b), bg[:], ALU.add).then_inc(bias, 1)

            @block.scalar
            def _(act):
                for c in range(CH):
                    act.wait_ge(we_sum, c + 1)
                    act.activation(we_hi[:, c, :], weff[:, c, :], ACT.Copy).then_inc(we_h, 1)
                for b in range(B):
                    i = b % 2
                    act.wait_ge(turned, b + 1)
                    if b >= 2:
                        act.wait_ge(mm, b - 1)
                    act.activation(tT_hi[:, i, :], T_BANKS[i][:], ACT.Copy).then_inc(t_h, 1)

            @block.tensor
            def _(pe):
                pe.wait_ge(coefd, 2)
                pe.wait_ge(ld[0], 16)
                for c in range(CH):
                    pe.matmul(W_BANKS[c][:], lA[:, c * P:(c + 1) * P], lBc[:],
                              start=True, stop=True).then_inc(folded, 1)

                def turn(b):
                    pe.wait_ge(norm, b + 1)
                    if b >= 2:
                        pe.wait_ge(t_l, b - 1)
                    for c in range(CH):
                        t = pe.transpose(T_BANKS[b % 2][:, c * P:(c + 1) * P], n3[:, b % 2, c * P:(c + 1) * P],
                                         ident[:])
                    t.then_inc(turned, 1)

                turn(0)
                pe.wait_ge(we_l, CH)
                for b in range(B):
                    if b + 1 < B:
                        turn(b + 1)
                    i = b % 2
                    pe.wait_ge(t_h, b + 1)
                    pe.wait_ge(t_l, b + 1)
                    if b >= 2:
                        pe.wait_ge(ysum, b - 1)
                    for c in range(CH):
                        w = slice(c * P, (c + 1) * P)
                        pe.matmul(Y_BANKS[i][:], tT_hi[:, i, w], we_hi[:, c, :], start=(c == 0), stop=False)
                        pe.matmul(Y_BANKS[i][:], tT_hi[:, i, w], we_lo[:, c, :], start=False, stop=False)
                        t = pe.matmul(Y_BANKS[i][:], tT_lo[:, i, w], we_hi[:, c, :],
                                      start=False, stop=(c == CH - 1))
                    t.then_inc(mm, 1)

            @block.vector
            def _(dve):
                def layer_norm(b):
                    i = b % 2
                    dve.bn_stats(stat[:, i, :], xb(b)).then_inc(stats, 1)
                    dve.wait_ge(stats, 2 * b + 1)
                    dve.bn_aggr(mv[:, i, :], stat[:, i, :]).then_inc(stats, 1)

                def normalise(b):
                    i = b % 2
                    dve.wait_ge(root, 2 * b + 2)
                    if b >= 2:
                        dve.wait_ge(turned, b - 1)
                    dve.tensor_scalar(n3[:, i, :], xb(b), mv[:, i, 0:1], rstd[:, i:i + 1],
                                      ALU.subtract, ALU.mult).then_inc(norm, 1)

                layer_norm(0)
                for i in (1, 2, 4):
                    dve.wait_ge(ld[i], 16)
                dve.tensor_scalar(coef[:], lw[:], 2.0, None, ALU.mult).then_inc(coefd, 1)
                dve.wait_ge(coefd, 1)
                dve.tensor_scalar(lBc[:], lB[:], coef[:], None, ALU.mult).then_inc(coefd, 1)
                dve.tensor_scalar(bg[:], b1[:], gate[:, 3:4], None, ALU.mult).then_inc(coefd, 1)
                normalise(0)
                layer_norm(1)
                dve.wait_ge(ld[3], 16)
                for c in range(CH):
                    dve.wait_ge(folded, c + 1)
                    dve.tensor_tensor(weff[:, c, :], W_BANKS[c][:], w1[:, c, :], ALU.add).then_inc(we_sum, 1)
                for c in range(CH):
                    dve.wait_ge(we_h, c + 1)
                    dve.tensor_tensor(we_lo[:, c, :], weff[:, c, :], we_hi[:, c, :].bitcast(F32),
                                      ALU.subtract).then_inc(we_l, 1)

                def low_part(b):
                    dve.wait_ge(t_h, b + 1)
                    dve.tensor_tensor(tT_lo[:, b % 2, :], T_BANKS[b % 2][:], tT_hi[:, b % 2, :].bitcast(F32),
                                      ALU.subtract).then_inc(t_l, 1)

                low_part(0)
                for b in range(B):
                    if b + 1 < B:
                        normalise(b + 1)
                    if b + 2 < B:
                        layer_norm(b + 2)
                    if b + 1 < B:
                        low_part(b + 1)
                    dve.wait_ge(mm, b + 1)
                    dve.wait_ge(bias, b + 1)
                    if b >= 2:
                        dve.wait_ge(stored[b % 2], 16 * (b // 2))
                    dve.scalar_tensor_tensor(y[:, b % 2, :], Y_BANKS[b % 2][:], gate[:, 3:4], xb(b),
                                             ALU.mult, ALU.add).then_inc(ysum, 1)


def dft_constants():
    import numpy as np
    t = np.arange(P)
    f = np.concatenate([np.arange(0, P // 2 + 1), np.arange(1, P // 2)])
    is_im = (np.arange(P) > P // 2)[:, None]
    ph = 2 * np.pi * np.outer(f, t) / P
    fwd = np.where(is_im, -np.sin(ph), np.cos(ph))
    fwd_sw = np.where(is_im, np.cos(ph), -np.sin(ph))
    weight = np.where((f == 0) | (f == P // 2), 1.0, 2.0)[:, None]
    inv1 = weight * np.cos(ph) / P
    inv2 = np.where(is_im, -1, 1) * weight * np.sin(ph) / P
    odd = np.concatenate([np.arange(P // 2)] * 2)
    is_im = (np.arange(P) >= P // 2)[:, None]
    ph = 2 * np.pi * np.outer(2 * odd + 1, t) / (2 * P)
    odd_fwd = np.where(is_im, -np.sin(ph), np.cos(ph))
    odd_fwd_sw = np.where(is_im, np.cos(ph), -np.sin(ph))
    odd_inv1 = np.cos(ph) / P
    odd_inv2 = np.where(is_im, 1, -1) * np.sin(ph) / P

    def less_last_row(m):
        m = m.copy()
        m[:, P - 1] -= m.sum(1)
        return m

    hold = np.zeros((P, P))
    hold[P - 1, :] = 0.5
    m = [fwd.T, fwd_sw.T, less_last_row(odd_fwd).T, less_last_row(odd_fwd_sw).T, odd_fwd.T, inv1, inv2,
         inv1 / 2, -inv2 / 2, odd_inv1, odd_inv2, hold, np.eye(P)]
    return np.ascontiguousarray(np.stack(m, axis=1).astype(np.float32))


def kernel(**inputs):
    import numpy as np
    import concourse.bacc as bacc
    from concourse.bass_utils import run_bass_kernel_spmd

    a = {k: np.asarray(v) for k, v in inputs.items()}

    def chunked(w):
        return w.reshape(w.shape[0], CH, P).transpose(2, 1, 0)

    wk = a["L1_xattn_Wk"].reshape(G, P, CH, P).transpose(0, 3, 2, 1)
    wv = a["L1_xattn_Wv"].reshape(G, P, CH, P).transpose(0, 3, 2, 1)
    laid = {
        "x": a["x"],
        "ctx_n": a["ctx_4096"],
        "ctx_t": chunked(a["ctx_4096"].reshape(B * P, D)),
        "mask": a["mask_1x1xSxS2_ff0"].reshape(P, P),
        "gates": np.broadcast_to(np.stack([a["g_xattn"][0], a["g_ffn"][0], a["g_xattn"][1], a["g_ffn"][1]]), (P, 4)),
        "dft": dft_constants(),
        "wbase": chunked(a["L0_ffn_W_base"]),
        "wag": np.concatenate([chunked(a["L0_ffn_A"].reshape(ER, D)), chunked(a["L0_ffn_W_gate"])], axis=2),
        "bb": np.broadcast_to(a["L0_ffn_b_base"], (P, D)),
        "bcat": a["L0_ffn_B"].transpose(0, 2, 1).reshape(ER, D),
        "wq": a["L1_xattn_Wq"].reshape(G * HG, P, CH, P).transpose(0, 3, 2, 1).reshape(G * HG, P, D),
        "wkv": np.concatenate([wk, wv], axis=3).reshape(G, P, CH * 2 * P),
        "wo": a["L1_xattn_Wo"].reshape(D, G * HG, P).transpose(1, 2, 0),
        "qn": a["L1_xattn_q_norm_w"].reshape(P, 1),
        "kn": a["L1_xattn_k_norm_w"].reshape(P, 1),
        "lA": a["L1_ffn_lora_A"].reshape(P, D),
        "lB": a["L1_ffn_lora_B"].transpose(0, 2, 1).reshape(P, D),
        "lw": np.repeat(a["L1_ffn_lora_weights"], R).reshape(P, 1),
        "w1": chunked(a["L1_ffn_W"]),
        "b1": np.broadcast_to(a["L1_ffn_bias"], (P, D)),
    }
    nc = bacc.Bacc("TRN2", target_bir_lowering=False, num_devices=1)
    arrays, args = {}, []
    for name, v in laid.items():
        v = np.ascontiguousarray(v)
        arrays[f"in_{name}"] = v
        args.append(nc.dram_tensor(f"in_{name}", v.shape, mybir.dt.from_np(v.dtype), kind="ExternalInput").ap())
    args.append(nc.dram_tensor("out_0", (B, P, D), F32, kind="ExternalOutput").ap())
    names = list(laid)
    by = dict(zip(names, args))
    flamingo_kernel(nc, by["x"], by["ctx_n"], by["ctx_t"], by["mask"], by["gates"], by["dft"], by["wbase"],
                    by["wag"], by["bb"], by["bcat"], by["wq"], by["wkv"], by["wo"], by["qn"], by["kn"],
                    by["lA"], by["lB"], by["lw"], by["w1"], by["b1"], args[-1])
    r = run_bass_kernel_spmd(nc, [arrays], core_ids=[0])
    return r.results[0]["out_0"]
```

```python
from contextlib import ExitStack

import concourse.bass as bass
from concourse import mybir

F32 = mybir.dt.float32
F32R = mybir.dt.float32r
ALU = mybir.AluOpType
ACT = mybir.ActivationFunctionType
AX = mybir.AxisListType

P = 128
B = 8
D = 512
CH = D // P
G = 8
HG = 4
E = 8
R = 16
ER = E * R
TOPK = 9
NEG = -(2.0 ** 127)
LN_EPS = 1e-5
RMS_EPS = 1e-5

(K_FWD, K_FWD_SW, V_ODD, V_ODD_SW, W_ODD, C_INV1, C_INV2,
 E_INV1, E_INV2, O_INV1, O_INV2, IDENT) = range(12)
N_DFT = 12


def need(eng, sem, value, hold=False):
    if isinstance(value, int) and value <= 0:
        return
    eng.wait_ge(sem, value)
    if hold and not isinstance(value, int):
        eng.nop(nofuse=True)


def cols(start, n):
    return slice(start, start + n) if isinstance(start, int) else bass.ds(start, n)


def three_pass(pe, out, l_hi, l_lo, r_hi, r_lo, start, stop):
    pe.matmul(out, l_hi, r_hi, start=start, stop=False)
    pe.matmul(out, l_hi, r_lo, start=False, stop=False)
    return pe.matmul(out, l_lo, r_hi, start=False, stop=stop)


def flamingo_kernel(nc, x, ctx_n, ctx_t, mask, gates, dft_d, wbase_d, wag_d, bb_d, bcat_d,
                    wq_d, wkv_d, wo_d, qn_d, kn_d, lA_d, lB_d, lw_d, w1_d, b1_d, out):
    with ExitStack() as top:
        def sem(name):
            return top.enter_context(nc.semaphore(name))

        def sb(stack, name, shape, dt=F32):
            return stack.enter_context(nc.sbuf_tensor(name, shape, dt))

        bank = [top.enter_context(nc.psum_tensor(f"bank{i}", [P, 512], F32)) for i in range(8)]

        xres = sb(top, "xres", [P, B * D])
        nT_hi = sb(top, "nT_hi", [P, CH, B * P], F32R)
        nT_lo = sb(top, "nT_lo", [P, CH, B * P], F32R)
        cT_hi = sb(top, "cT_hi", [P, CH, B * P], F32R)
        cT_lo = sb(top, "cT_lo", [P, CH, B * P], F32R)
        gate = sb(top, "gate", [P, 4])
        ident = sb(top, "ident", [P, P])
        neghalf = sb(top, "neghalf", [P, 8])
        wq_raw = sb(top, "wq_raw", [P, HG, CH * P])
        wo_raw = sb(top, "wo_raw", [P, HG, D])
        wkv_raw = sb(top, "wkv_raw", [P, CH * 2 * P])
        maskt = sb(top, "maskt", [P, P])
        norm_w = sb(top, "norm_w", [P, 2])
        ld_wq = [sem(f"c_wq_loaded{h}") for h in range(HG)]
        ld_wo = [sem(f"c_wo_loaded{h}") for h in range(HG)]
        ld_wkv = sem("c_wkv_loaded")
        ld_mask = sem("c_mask_loaded")
        ld_norm = [sem("c_q_norm_loaded"), sem("c_k_norm_loaded")]

        wkv_hi = sb(top, "wkv_hi", [P, CH * 2 * P], F32R)
        wkv_lo = sb(top, "wkv_lo", [P, CH * 2 * P], F32R)
        wq_hi = [sb(top, "wq_hi0", [P, CH * P], F32R)]
        wq_lo = [sb(top, "wq_lo0", [P, CH * P], F32R)]
        wq_h = sem("c_wq_high")
        wq_l = sem("c_wq_low")
        wkv_h = sem("c_wkv_high")
        wkv_l = sem("c_wkv_low")

        def first_high(act):
            act.wait_ge(ld_wq[0], 16)
            act.activation(wq_hi[0][:], wq_raw[:, 0, :], ACT.Copy).then_inc(wq_h, 1)
            act.wait_ge(ld_wkv, 16)
            act.activation(wkv_hi[:], wkv_raw[:], ACT.Copy).then_inc(wkv_h, 1)

        def first_low(pool):
            pool.wait_ge(wq_h, 1)
            pool.tensor_tensor(wq_lo[0][:], wq_raw[:, 0, :], wq_hi[0][:].bitcast(F32), ALU.subtract).then_inc(wq_l, 1)
            pool.wait_ge(wkv_h, 1)
            pool.tensor_tensor(wkv_lo[:], wkv_raw[:], wkv_hi[:].bitcast(F32), ALU.subtract).then_inc(wkv_l, 1)

        def first_weights(sp):
            sp.dma_start(wkv_raw[:], wkv_d[0]).then_inc(ld_wkv, 16)
            for h in range(HG):
                sp.dma_start(wq_raw[:, h, :], wq_d[h]).then_inc(ld_wq[h], 16)
            sp.dma_start(norm_w[:, 0:1], qn_d[:]).then_inc(ld_norm[0], 16)
            sp.dma_start(norm_w[:, 1:2], kn_d[:]).then_inc(ld_norm[1], 16)
            sp.dma_start(maskt[:], mask[:]).then_inc(ld_mask, 16)
            for h in range(HG):
                sp.dma_start(wo_raw[:, h, :], wo_d[h]).then_inc(ld_wo[h], 16)

        phase_a(nc, sem, sb, bank, xres, nT_hi, nT_lo, cT_hi, cT_lo, gate, ident, neghalf,
                x, ctx_n, ctx_t, gates, dft_d, wbase_d, wag_d, bb_d, bcat_d, first_weights, first_high, first_low)
        phase_c(nc, sem, sb, bank, xres, nT_hi, nT_lo, cT_hi, cT_lo, gate, ident, neghalf,
                wq_raw, wo_raw, wkv_raw, maskt, norm_w, ld_wq, ld_wo, ld_wkv, ld_mask, ld_norm,
                wkv_hi, wkv_lo, wq_hi, wq_lo, wkv_h, wkv_l, wq_h, wq_l,
                wq_d, wkv_d, wo_d, lA_d, lB_d, lw_d, w1_d, b1_d, out)


def phase_a(nc, sem, sb, bank, xres, nT_hi, nT_lo, cT_hi, cT_lo, gate, ident, neghalf,
            x, ctx_n, ctx_t, gates, dft_d, wbase_d, wag_d, bb_d, bcat_d, first_weights, first_high, first_low):
    with ExitStack() as st:
        ctxn = sb(st, "ctxn", [P, D])
        cx_hi = sb(st, "cx_hi", [P, D], F32R)
        cx_lo = sb(st, "cx_lo", [P, D], F32R)
        ctxt = sb(st, "ctxt", [P, CH, P])
        dft = sb(st, "dft", [P, N_DFT, P])
        fwd_hi = sb(st, "fwd_hi", [P, 4, P], F32R)
        fwd_lo = sb(st, "fwd_lo", [P, 4, P], F32R)
        inv_hi = sb(st, "inv_hi", [P, 4, P], F32R)
        inv_lo = sb(st, "inv_lo", [P, 4, P], F32R)
        wbase = sb(st, "wbase", [P, CH, D])
        wag = sb(st, "wag", [P, CH, ER + E])
        bcat = sb(st, "bcat", [P, D])
        bb = sb(st, "bb", [P, D])
        gates_in = sb(st, "gates_in", [P, 4])
        f_stat = sb(st, "f_stat", [P, 6])
        f_mv = sb(st, "f_mv", [P, 2])
        f_rstd = sb(st, "f_rstd", [P, 1])
        nx = sb(st, "nx", [P, D])
        kf = sb(st, "kf", [P, 4, D])
        prod1 = sb(st, "prod1", [P, D])
        prod2 = sb(st, "prod2", [P, D])
        n2T = prod1
        top8 = sb(st, "top8", [P, CH, 8])
        next8 = sb(st, "next8", [P, CH, 8])
        ninth = sb(st, "ninth", [P, CH, 8])
        ntop = sb(st, "ntop", [P, CH])
        rest8 = sb(st, "rest8", [P, CH, P])
        rest9 = sb(st, "rest9", [P, CH, P])
        elag = sb(st, "elag", [P, CH, P])
        wlag = sb(st, "wlag", [P, CH, P])
        wsum = sb(st, "wsum", [P, CH])
        wrec = sb(st, "wrec", [P, CH])
        wlagn = sb(st, "wlagn", [P, CH, P])
        wT = sb(st, "wT", [P, D])
        op = sb(st, "op", [P, 4, D])
        op_hi = sb(st, "op_hi", [P, 4, D], F32R)
        op_lo = sb(st, "op_lo", [P, 4, D], F32R)
        h_stat = sb(st, "h_stat", [P, 6])
        h_mv = sb(st, "h_mv", [P, 2])
        h_rstd = sb(st, "h_rstd", [P, 1])
        n1 = sb(st, "n1", [P, D])
        n1T = sb(st, "n1T", [P, CH, P])
        lg = sb(st, "lg", [P, 2 * E])
        lg8 = sb(st, "lg8", [P, 8])
        two = sb(st, "two", [P, 8])
        nlg = sb(st, "nlg", [P, 1])
        eg = sb(st, "eg", [P, E])
        lgr = sb(st, "lgr", [P, 2 * E])
        rw = sb(st, "rw", [P, E])
        rsum = sb(st, "rsum", [P, 1])
        rrec = sb(st, "rrec", [P, 1])
        rwn = sb(st, "rwn", [P, E])
        hw = sb(st, "hw", [P, ER])
        hwT = sb(st, "hwT", [P, P])
        g_stat = sb(st, "g_stat", [P, 6])
        g_mv = sb(st, "g_mv", [P, 2])
        g_rstd = sb(st, "g_rstd", [P, 1])
        n2 = sb(st, "n2", [P, D])

        ld_g = sem("a_gates_loaded")
        CUTS = (0, 1, 3, B)
        ld_x = [sem(f"a_x_loaded{i}") for i in range(3)]
        ld_c = sem("a_ctx_loaded")
        ld_ct = sem("a_ctx_turned_loaded")
        ld_dft = sem("a_dft_loaded")
        ld_w = [sem(f"a_weights_loaded{i}") for i in range(4)]
        consts = sem("a_consts")
        tanhed = sem("a_gates_tanh")
        bias_gated = sem("a_bias_gated")
        f_stats = sem("a_f_stats")
        f_root = sem("a_f_root")
        f_norm = sem("a_f_norm")
        dft_h = sem("a_dft_high")
        dft_l = sem("a_dft_low")
        cx_h = sem("a_ctx_high")
        cx_l = sem("a_ctx_low")
        op_h = sem("a_out_products_high")
        op_l = sem("a_out_products_low")
        q_fwd = sem("a_q_transformed")
        k_fwd = sem("a_ctx_transformed")
        k_copied = sem("a_ctx_dfts_copied")
        c_prod = sem("a_corr_products")
        corr = sem("a_corr_ready")
        picked = sem("a_lag_steps")
        lag9 = sem("a_ninth_steps")
        e_lag = sem("a_exp_lags")
        w_norm = sem("a_lag_weights")
        w_trans = sem("a_lag_weights_turned")
        w_copied = sem("a_lag_weights_copied")
        w_fwd = sem("a_lag_weights_transformed")
        o_prod = sem("a_out_products")
        f_out = sem("a_f_out")
        f_added = sem("a_f_added")
        h_stats = sem("a_h_stats")
        h_root = sem("a_h_root")
        h_norm = sem("a_h_norm")
        h_trans = sem("a_h_turned")
        h_copied = sem("a_h_copied")
        h_low = sem("a_router_ready")
        h_step = sem("a_router_steps")
        routed = sem("a_route_weights")
        h_exp = sem("a_router_exp")
        hw_trans = sem("a_hw_turned")
        hw_copied = sem("a_hw_copied")
        h_out = sem("a_h_out")
        h_bias = sem("a_bias_added")
        h_added = sem("a_h_added")
        g_stats = sem("a_g_stats")
        g_root = sem("a_g_root")
        g_norm = sem("a_g_norm")
        g_trans = sem("a_g_turned")
        g_copied = sem("a_g_copied")
        g_hi = sem("a_g_high")
        g_lo = sem("a_g_low")
        ct_hi = sem("a_ctx_turned_high")
        ct_lo = sem("a_ctx_turned_low")

        PICK = 5
        ROUTE = 7

        def xb(b):
            return xres[:, cols(b * D, D)]

        def on(b):
            return not isinstance(b, int) or 0 <= b < B

        def ending(b):
            return isinstance(b, int) and b > B

        def closing(b):
            return isinstance(b, int) and b == B + 2

        def looped(eng, slot):
            for b in range(3):
                slot(b)
            with eng.Fori(3, B - 2) as b:
                slot(b)
            for b in range(B - 2, B + 3):
                slot(b)

        with nc.Block() as block:
            @block.sync
            def _(sp):
                def load_batches(i):
                    a, z = CUTS[i], CUTS[i + 1]
                    sp.dma_start(xres[:, a * D:z * D].rearrange("p (b d) -> p b d", d=D),
                                 x[a:z].rearrange("b p d -> p b d")).then_inc(ld_x[i], 16)

                def row(d, i):
                    return d[i] if isinstance(i, int) else d[bass.ds(i, 1)].rearrange("a p n -> p (a n)")

                def load_ctx(b):
                    need(sp, cx_l, b)
                    sp.dma_start(ctxn[:], row(ctx_n, b)).then_inc(ld_c, 16)

                def load_turned_ctx(b):
                    need(sp, ct_lo, b)
                    sp.dma_start(ctxt[:].rearrange("p c t -> p (c t)"), row(ctx_t, b)).then_inc(ld_ct, 16)

                load_batches(0)
                load_ctx(0)
                sp.dma_start(dft[:], dft_d[:]).then_inc(ld_dft, 16)
                sp.dma_start(gates_in[:], gates[:]).then_inc(ld_g, 16)
                load_batches(1)
                load_ctx(1)
                sp.dma_start(wag[:], wag_d[:]).then_inc(ld_w[1], 16)
                sp.dma_start(wbase[:], wbase_d[:]).then_inc(ld_w[0], 16)
                sp.dma_start(bb[:], bb_d[:]).then_inc(ld_w[3], 16)
                sp.dma_start(bcat[:], bcat_d[:]).then_inc(ld_w[2], 16)
                load_turned_ctx(0)
                load_batches(2)
                load_ctx(2)
                load_turned_ctx(1)
                first_weights(sp)
                with sp.Fori(3, B) as b:
                    load_ctx(b)
                    load_turned_ctx(b - 1)
                load_turned_ctx(B - 1)

            @block.gpsimd
            def _(pool):
                pool.memset(neghalf[:], -0.5).then_inc(consts, 1)
                pool.memset(ninth[:], NEG).then_inc(consts, 1)
                pool.memset(lg[:], NEG).then_inc(consts, 1)
                pool.memset(two[:], NEG).then_inc(consts, 1)
                pool.wait_ge(consts, 4)

                def inverse_root(stats, root, mv, rstd, n):
                    need(pool, stats, 2 * n + 2, hold=True)
                    pool.tensor_scalar(mv[:, 1:2], mv[:, 1:2], LN_EPS, None, ALU.add).then_inc(root, 1)
                    need(pool, root, 2 * n + 1)
                    pool.tensor_tensor(rstd[:], mv[:, 1:2], neghalf[:, 0:1], ALU.pow).then_inc(root, 1)

                def slot(b):
                    if on(b):
                        need(pool, picked, PICK * b + PICK)
                        need(pool, w_trans, b)
                        pool.tensor_tensor(wlagn[:], wlag[:],
                                           wrec[:].unsqueeze(2).broadcast_to([P, CH, P]),
                                           ALU.mult).then_inc(w_norm, 1)
                    if on(b - 1):
                        inverse_root(h_stats, h_root, h_mv, h_rstd, b - 1)
                    if on(b + 2):
                        inverse_root(f_stats, f_root, f_mv, f_rstd, b + 2)
                    if on(b - 3) and not closing(b):
                        need(pool, g_hi, b - 2)
                        pool.tensor_tensor(nT_lo[:, :, cols((b - 3) * P, P)],
                                           n2T[:].rearrange("p (c t) -> p c t", c=CH),
                                           nT_hi[:, :, cols((b - 3) * P, P)].bitcast(F32),
                                           ALU.subtract).then_inc(g_lo, 1)
                    if on(b - 1):
                        need(pool, h_norm, b)
                        pool.tensor_tensor(xb(b - 1), xb(b - 1), bb[:], ALU.add).then_inc(h_bias, 1)
                    if on(b):
                        here = cols(b * P, P)
                        need(pool, ct_hi, b + 1)
                        pool.tensor_tensor(cT_lo[:, :, here], ctxt[:], cT_hi[:, :, here].bitcast(F32),
                                           ALU.subtract).then_inc(ct_lo, 1)
                        low_products(b, (0, 1))
                    if on(b - 2):
                        inverse_root(g_stats, g_root, g_mv, g_rstd, b - 2)
                    if on(b):
                        low_products(b, (2, 3))
                    if on(b + 2):
                        low_ctx(b + 2)
                    if isinstance(b, int) and b == B - 1:
                        first_low(pool)

                def low_ctx(b):
                    need(pool, cx_h, b + 1)
                    pool.tensor_tensor(cx_lo[:], ctxn[:], cx_hi[:].bitcast(F32), ALU.subtract).then_inc(cx_l, 1)

                def low_products(b, which):
                    for i in which:
                        need(pool, op_h, 4 * b + i + 1)
                        pool.tensor_tensor(op_lo[:, i, :], op[:, i, :], op_hi[:, i, :].bitcast(F32),
                                           ALU.subtract).then_inc(op_l, 1)

                low_ctx(0)
                inverse_root(f_stats, f_root, f_mv, f_rstd, 0)
                inverse_root(f_stats, f_root, f_mv, f_rstd, 1)
                low_ctx(1)
                pool.wait_ge(bias_gated, 1)
                looped(pool, slot)

            @block.scalar
            def _(act):

                def high_ctx(b):
                    need(act, ld_c, 16 * b + 16)
                    need(act, k_fwd, 4 * b)
                    act.activation(cx_hi[:], ctxn[:], ACT.Copy).then_inc(cx_h, 1)

                def high_products(b, which):
                    need(act, f_out, b)
                    for i in which:
                        need(act, o_prod, 4 * b + i + 1)
                        act.activation(op_hi[:, i, :], op[:, i, :], ACT.Copy).then_inc(op_h, 1)

                def copy_hw(b):
                    need(act, hw_trans, b - 1)
                    act.activation(hwT[:], bank[5][:, 0:P], ACT.Copy).then_inc(hw_copied, 1)

                def copy_ctx_dfts(b, which):
                    for i in which:
                        if i % 2 == 0:
                            need(act, o_prod, 4 * b + i - 2)
                        need(act, k_fwd, 4 * b + i + 1)
                        act.activation(kf[:, i, :], bank[1 + i % 2][:], ACT.Copy).then_inc(k_copied, 1)

                def slot(b):
                    if on(b):
                        need(act, picked, PICK * b + 3)
                        for j in range(CH):
                            act.activation(elag[:, j, :], bank[0][:, j * P:(j + 1) * P], ACT.Exp,
                                           bias=ntop[:, j:j + 1]).then_inc(e_lag, 1)
                    if ending(b) and on(b - 2):
                        copy_hw(b)
                    if on(b - 3):
                        nT = nT_hi[:, :, cols((b - 3) * P, P)]
                        need(act, g_trans, b - 2)
                        if closing(b):
                            act.activation(nT, bank[1][:].rearrange("p (c t) -> p c t", c=CH),
                                           ACT.Copy).then_inc(g_hi, 1)
                        else:
                            act.activation(n2T[:], bank[1][:], ACT.Copy).then_inc(g_copied, 1)
                            need(act, g_copied, b - 2)
                            act.activation(nT, n2T[:].rearrange("p (c t) -> p c t", c=CH),
                                           ACT.Copy).then_inc(g_hi, 1)
                    if on(b - 2) and not ending(b):
                        copy_hw(b)
                    if on(b):
                        need(act, ld_ct, 16 * b + 16)
                        act.activation(cT_hi[:, :, cols(b * P, P)], ctxt[:], ACT.Copy).then_inc(ct_hi, 1)
                        need(act, w_trans, b + 1)
                        act.activation(wT[:], bank[4][:], ACT.Copy).then_inc(w_copied, 1)
                    if on(b + 1):
                        copy_ctx_dfts(b + 1, (0,))
                    if on(b - 1):
                        need(act, h_trans, b)
                        act.activation(n1T[:].rearrange("p c t -> p (c t)"), bank[5][:],
                                       ACT.Copy).then_inc(h_copied, 1)
                    if on(b + 1):
                        copy_ctx_dfts(b + 1, (1,))
                    if on(b):
                        high_products(b, range(4))
                    if on(b - 1):
                        need(act, h_step, ROUTE * (b - 1) + 3)
                        act.activation(eg[:], lg[:, 0:E], ACT.Exp, bias=nlg[:]).then_inc(h_exp, 1)
                    if on(b + 1):
                        copy_ctx_dfts(b + 1, (2, 3))
                    if on(b + 2):
                        high_ctx(b + 2)
                    if isinstance(b, int) and b == B - 1:
                        first_high(act)

                high_ctx(0)
                act.wait_ge(ld_dft, 16)
                act.activation(fwd_hi[:], dft[:, K_FWD:K_FWD + 4, :], ACT.Copy).then_inc(dft_h, 1)
                act.activation(inv_hi[:], dft[:, E_INV1:E_INV1 + 4, :], ACT.Copy).then_inc(dft_h, 1)
                act.wait_ge(ld_g, 16)
                act.activation(gate[:], gates_in[:], ACT.Tanh).then_inc(tanhed, 1)
                copy_ctx_dfts(0, range(4))
                high_ctx(1)
                looped(act, slot)

            @block.tensor
            def _(pe):
                pe.wait_ge(ld_dft, 16)

                def q_transform(b):
                    need(pe, f_norm, b + 1)
                    need(pe, e_lag, CH * b)
                    pe.matmul(bank[0][:], dft[:, K_FWD, :], nx[:], start=True, stop=True).then_inc(q_fwd, 1)

                def ctx_transform(b, i):
                    if i == 0:
                        need(pe, cx_l, b + 1)
                        need(pe, g_copied, b - 3)
                    need(pe, k_copied, 4 * b + i - 1)
                    three_pass(pe, bank[1 + i % 2][:], fwd_hi[:, i, :], fwd_lo[:, i, :], cx_hi[:], cx_lo[:],
                               True, True).then_inc(k_fwd, 1)

                def turn_hw(b):
                    need(pe, h_step, ROUTE * (b - 1))
                    pe.transpose(bank[5][:, 0:P], hw[:], dft[:, IDENT, :]).then_inc(hw_trans, 1)

                def inverse(b, which):
                    for i in which:
                        need(pe, op_l, 4 * b + i + 1)
                        t = three_pass(pe, bank[3][:], inv_hi[:, i, :], inv_lo[:, i, :], op_hi[:, i, :],
                                       op_lo[:, i, :], i == 0, i == 3)
                    return t

                def base_products(b, chunks):
                    need(pe, h_added, b)
                    for c in chunks:
                        pe.matmul(bank[6][:], n1T[:, c, :], wbase[:, c, :], start=(c == 0), stop=False)

                def slot(b):
                    if on(b):
                        need(pe, c_prod, 2 * b + 2)
                        for j in range(CH):
                            o = bank[0][:, j * P:(j + 1) * P]
                            pe.matmul(o, prod1[:, j * P:(j + 1) * P], dft[:, C_INV1, :], start=True, stop=False)
                            t = pe.matmul(o, prod2[:, j * P:(j + 1) * P], dft[:, C_INV2, :],
                                          start=False, stop=True)
                        t.then_inc(corr, 1)
                    if on(b - 1):
                        if isinstance(b, int) and b == 1:
                            pe.wait_ge(dft_l, 2)
                        need(pe, o_prod, 4 * b)
                        inverse(b - 1, (0, 1))
                    fills = on(b - 2) and not (isinstance(b, int) and b == B + 1)
                    if fills:
                        base_products(b - 2, (0, 1))
                    if on(b - 1):
                        inverse(b - 1, (2, 3)).then_inc(f_out, 1)
                    if ending(b) and on(b - 2):
                        turn_hw(b)
                        base_products(b - 2, (3,))
                    if on(b - 3):
                        need(pe, g_norm, b - 2)
                        need(pe, k_copied, 4 * b + 3 if not isinstance(b, int) else min(4 * b + 3, 4 * B))
                        if closing(b):
                            need(pe, g_copied, b - 3)
                        for c in range(CH):
                            t = pe.transpose(bank[1][:, c * P:(c + 1) * P], n2[:, c * P:(c + 1) * P],
                                             dft[:, IDENT, :])
                        t.then_inc(g_trans, 1)
                    if on(b - 2) and not ending(b):
                        turn_hw(b)
                    if on(b + 1):
                        q_transform(b + 1)
                        ctx_transform(b + 1, 0)
                        ctx_transform(b + 1, 1)
                    if on(b):
                        need(pe, w_norm, b + 1)
                        need(pe, o_prod, 4 * b)
                        for j in range(CH):
                            t = pe.transpose(bank[4][:, j * P:(j + 1) * P], wlagn[:, j, :], dft[:, IDENT, :])
                        t.then_inc(w_trans, 1)
                    if fills:
                        base_products(b - 2, (2,))
                    if on(b):
                        need(pe, w_copied, b + 1)
                        need(pe, f_added, b)
                        pe.matmul(bank[3][:], dft[:, K_FWD, :], wT[:], start=True, stop=True).then_inc(w_fwd, 1)
                        pe.matmul(bank[4][:], dft[:, W_ODD, :], wT[:], start=True, stop=True).then_inc(w_fwd, 1)
                    if fills:
                        base_products(b - 2, (3,))
                    if on(b - 1):
                        need(pe, h_norm, b)
                        need(pe, hw_copied, b - 1)
                        for c in range(CH):
                            t = pe.transpose(bank[5][:, c * P:(c + 1) * P], n1[:, c * P:(c + 1) * P],
                                             dft[:, IDENT, :])
                        t.then_inc(h_trans, 1)
                    if on(b - 2):
                        need(pe, hw_copied, b - 1)
                        pe.matmul(bank[6][:], hwT[:], bcat[:], start=False, stop=True).then_inc(h_out, 1)
                    if on(b - 1):
                        if isinstance(b, int) and b == 1:
                            for w in ld_w[0:3]:
                                pe.wait_ge(w, 16)
                        need(pe, h_copied, b)
                        for c in range(CH):
                            t = pe.matmul(bank[7][:, 0:ER + E], n1T[:, c, :], wag[:, c, :],
                                          start=(c == 0), stop=(c == CH - 1))
                        t.then_inc(h_low, 1)
                    if on(b + 1):
                        ctx_transform(b + 1, 2)
                        ctx_transform(b + 1, 3)
                    if isinstance(b, int) and b == B:
                        base_products(B - 1, (0, 1, 2))

                q_transform(0)
                pe.wait_ge(dft_l, 1)
                for i in range(4):
                    ctx_transform(0, i)
                looped(pe, slot)

            @block.vector
            def _(dve):
                def statistics(b, stat, mv, done):
                    dve.bn_stats(stat[:], xb(b)).then_inc(done, 1)
                    need(dve, done, 2 * b + 1, hold=True)
                    dve.bn_aggr(mv[:], stat[:]).then_inc(done, 1)

                def normalise(dst, b, mv, rstd, root, done):
                    need(dve, root, 2 * b + 2)
                    dve.tensor_scalar(dst[:], xb(b), mv[:, 0:1], rstd[:], ALU.subtract, ALU.mult).then_inc(done, 1)

                def corr_products(b):
                    need(dve, k_copied, 4 * b + 1)
                    need(dve, q_fwd, b + 1)
                    need(dve, g_lo, b - 3)
                    dve.tensor_tensor(prod1[:], bank[0][:], kf[:, 0, :], ALU.mult).then_inc(c_prod, 1)
                    need(dve, k_copied, 4 * b + 2)
                    dve.tensor_tensor(prod2[:], bank[0][:], kf[:, 1, :], ALU.mult).then_inc(c_prod, 1)

                def pick_lags(b):
                    need(dve, corr, b + 1, hold=True)
                    for j in range(CH):
                        t = dve.max(top8[:, j, :], bank[0][:, j * P:(j + 1) * P])
                    t.then_inc(picked, 1)
                    need(dve, picked, PICK * b + 1)
                    dve.tensor_scalar(ntop[:], top8[:, :, 0], -1.0, None, ALU.mult).then_inc(picked, 1)
                    for j in range(CH):
                        t = dve.match_replace(rest8[:, j, :], top8[:, j, :], bank[0][:, j * P:(j + 1) * P], NEG)
                    t.then_inc(picked, 1)
                    need(dve, picked, PICK * b + 3, hold=True)
                    for j in range(CH):
                        t = dve.max(next8[:, j, :], rest8[:, j, :])
                    t.then_inc(lag9, 1)
                    need(dve, lag9, 3 * b + 1)
                    dve.tensor_copy(ninth[:, :, 0], next8[:, :, 0]).then_inc(lag9, 1)
                    need(dve, lag9, 3 * b + 2, hold=True)
                    for j in range(CH):
                        t = dve.match_replace(rest9[:, j, :], ninth[:, j, :], rest8[:, j, :], NEG)
                    t.then_inc(lag9, 1)
                    need(dve, lag9, 3 * b + 3)
                    need(dve, e_lag, CH * b + CH)
                    need(dve, w_norm, b)
                    for j in range(CH):
                        t = dve.scalar_tensor_tensor(wlag[:, j, :], rest9[:, j, :], NEG, elag[:, j, :],
                                                     ALU.is_equal, ALU.mult, accum_out=wsum[:, j:j + 1])
                    t.then_inc(picked, 1)
                    need(dve, picked, PICK * b + 4)
                    dve.reciprocal(wrec[:], wsum[:]).then_inc(picked, 1)

                def route_and_add(b):
                    n = ROUTE * (b - 1)
                    routing, adding = on(b - 1), on(b - 2)
                    if routing:
                        need(dve, h_low, b)
                        dve.tensor_copy(lg[:, 0:E], bank[7][:, ER:ER + E]).then_inc(h_step, 1)
                    if adding:
                        need(dve, h_out, b - 1)
                        need(dve, h_bias, b - 1)
                        dve.scalar_tensor_tensor(xb(b - 2), bank[6][:], gate[:, 1:2], xb(b - 2),
                                                 ALU.mult, ALU.add).then_inc(h_added, 1)
                    if routing:
                        need(dve, h_step, n + 1, hold=True)
                        dve.max(lg8[:], lg[:, 0:E]).then_inc(h_step, 1)
                    if adding:
                        need(dve, h_added, b - 1, hold=True)
                        dve.bn_stats(g_stat[:], xb(b - 2)).then_inc(g_stats, 1)
                    if routing:
                        need(dve, h_step, n + 2)
                        dve.tensor_scalar(nlg[:], lg8[:, 0:1], -1.0, None, ALU.mult).then_inc(h_step, 1)
                        dve.tensor_copy(two[:, 0:2], lg8[:, 0:2]).then_inc(h_step, 1)
                    if adding:
                        need(dve, g_stats, 2 * b - 3, hold=True)
                        dve.bn_aggr(g_mv[:], g_stat[:]).then_inc(g_stats, 1)
                    if routing:
                        need(dve, h_step, n + 4, hold=True)
                        dve.match_replace(lgr[:], two[:], lg[:], NEG).then_inc(h_step, 1)
                        need(dve, h_step, n + 5)
                        need(dve, h_exp, b)
                        dve.scalar_tensor_tensor(rw[:], lgr[:, 0:E], NEG, eg[:], ALU.is_equal, ALU.mult,
                                                 accum_out=rsum[:]).then_inc(h_step, 1)
                        need(dve, h_step, n + 6)
                        dve.reciprocal(rrec[:], rsum[:]).then_inc(routed, 1)
                        need(dve, routed, 2 * b - 1)
                        dve.tensor_scalar(rwn[:], rw[:], rrec[:], None, ALU.mult).then_inc(routed, 1)
                    if adding:
                        normalise(n2, b - 2, g_mv, g_rstd, g_root, g_norm)
                    if routing:
                        need(dve, routed, 2 * b)
                        dve.tensor_tensor(hw[:].rearrange("p (e r) -> p e r", e=E),
                                          bank[7][:, 0:ER].rearrange("p (e r) -> p e r", e=E),
                                          rwn[:].unsqueeze(2).broadcast_to([P, E, R]), ALU.mult).then_inc(h_step, 1)

                def slot(b):
                    if on(b):
                        pick_lags(b)
                    if on(b - 1):
                        need(dve, f_out, b)
                        dve.scalar_tensor_tensor(xb(b - 1), bank[3][:], gate[:, 0:1], xb(b - 1),
                                                 ALU.mult, ALU.add).then_inc(f_added, 1)
                        need(dve, f_added, b, hold=True)
                        statistics(b - 1, h_stat, h_mv, h_stats)
                    if on(b + 2):
                        if isinstance(b, int) and b + 2 == CUTS[2]:
                            dve.wait_ge(ld_x[2], 16)
                        statistics(b + 2, f_stat, f_mv, f_stats)
                    if on(b - 1):
                        normalise(n1, b - 1, h_mv, h_rstd, h_root, h_norm)
                    if on(b + 2):
                        need(dve, q_fwd, b + 2)
                        normalise(nx, b + 2, f_mv, f_rstd, f_root, f_norm)
                    if on(b):
                        need(dve, op_l, 4 * b)
                        need(dve, w_fwd, 2 * b + 1)
                        dve.tensor_tensor(op[:, 0, :], bank[3][:], kf[:, 0, :], ALU.mult).then_inc(o_prod, 1)
                        dve.tensor_tensor(op[:, 1, :], bank[3][:], kf[:, 1, :], ALU.mult).then_inc(o_prod, 1)
                        need(dve, w_fwd, 2 * b + 2)
                        dve.tensor_tensor(op[:, 2, :], bank[4][:], kf[:, 2, :], ALU.mult).then_inc(o_prod, 1)
                        dve.tensor_tensor(op[:, 3, :], bank[4][:], kf[:, 3, :], ALU.mult).then_inc(o_prod, 1)
                    if on(b + 1):
                        corr_products(b + 1)
                    route_and_add(b)
                    if closing(b):
                        need(dve, g_hi, b - 2)
                        dve.tensor_tensor(nT_lo[:, :, cols((b - 3) * P, P)],
                                          bank[1][:].rearrange("p (c t) -> p c t", c=CH),
                                          nT_hi[:, :, cols((b - 3) * P, P)].bitcast(F32),
                                          ALU.subtract).then_inc(g_lo, 1)

                dve.wait_ge(ld_x[0], 16)
                statistics(0, f_stat, f_mv, f_stats)
                normalise(nx, 0, f_mv, f_rstd, f_root, f_norm)
                dve.wait_ge(ld_dft, 16)
                for i, (lo, hi, m) in enumerate(((fwd_lo, fwd_hi, K_FWD), (inv_lo, inv_hi, E_INV1))):
                    dve.wait_ge(dft_h, i + 1)
                    dve.tensor_tensor(lo[:], dft[:, m:m + 4, :], hi[:].bitcast(F32), ALU.subtract).then_inc(dft_l, 1)
                dve.tensor_copy(ident[:], dft[:, IDENT, :])
                corr_products(0)
                dve.wait_ge(ld_x[1], 16)
                statistics(1, f_stat, f_mv, f_stats)
                normalise(nx, 1, f_mv, f_rstd, f_root, f_norm)
                dve.wait_ge(tanhed, 1)
                dve.wait_ge(ld_w[3], 16)
                dve.tensor_scalar(bb[:], bb[:], gate[:, 1:2], None, ALU.mult).then_inc(bias_gated, 1)
                looped(dve, slot)


def phase_c(nc, sem, sb, bank, xres, nT_hi, nT_lo, cT_hi, cT_lo, gate, ident, neghalf,
            wq_raw, wo_raw, wkv_raw, maskt, norm_w, ld_wq, ld_wo, ld_wkv, ld_mask, ld_norm,
            wkv_hi, wkv_lo, wq_hi, wq_lo, wkv_h, wkv_l, wq_h, wq_l,
            wq_d, wkv_d, wo_d, lA_d, lB_d, lw_d, w1_d, b1_d, out):
    LAG = 4
    N = G * B
    WQ_SLOT = {2: (0,), 3: (1,), 4: (2,), 5: (3,)}
    WO_SLOT = {1: (0, 1, 2, 3)}
    LOW_SLOT = {0: (0,), 2: (1,), 3: (2, 3)}
    with ExitStack() as st:
        qT_hi = sb(st, "qT_hi", [P, HG, B * P], F32R)
        qT_lo = sb(st, "qT_lo", [P, HG, B * P], F32R)
        kT = sb(st, "kT", [P, B, 2, P], F32R)
        v_hi = sb(st, "v_hi", [P, B * P], F32R)
        v_lo = sb(st, "v_lo", [P, B * P], F32R)
        wq_hi = wq_hi + [sb(st, f"wq_hi{h}", [P, CH * P], F32R) for h in range(1, HG)]
        wq_lo = wq_lo + [sb(st, f"wq_lo{h}", [P, CH * P], F32R) for h in range(1, HG)]
        wo_hi = sb(st, "wo_hi", [P, HG, D], F32R)
        wo_lo = sb(st, "wo_lo", [P, HG, D], F32R)
        score = sb(st, "score", [P, HG, P])
        prob = sb(st, "prob", [P, HG, P])
        probn = sb(st, "probn", [P, HG, P])
        pT_hi = sb(st, "pT_hi", [P, HG * P], F32R)
        pT_lo = sb(st, "pT_lo", [P, HG * P], F32R)
        oT_hi = sb(st, "oT_hi", [P, HG * P], F32R)
        oT_lo = sb(st, "oT_lo", [P, HG * P], F32R)
        qsq = sb(st, "qsq", [P, 4 * P])
        knat = sb(st, "knat", [P, P])
        ksq = sb(st, "ksq", [P, P])
        ones = sb(st, "ones", [P, 1])
        wqk = sb(st, "wqk", [P, 1])
        qss = sb(st, "qss", [P, 4])
        rq = sb(st, "rq", [P, HG, B])
        kss = sb(st, "kss", [P, 1])
        kse = sb(st, "kse", [P, 1])
        rk = sb(st, "rk", [P, 1])
        nmax = sb(st, "nmax", [P, HG])
        esum = sb(st, "esum", [P, HG])
        erec = sb(st, "erec", [P, HG])

        w1 = wq_raw
        lA, lBc = wkv_raw[:, 0:D], wkv_raw[:, D:2 * D]
        bg = wo_raw[:, 0, :]
        n3 = (wo_raw[:, 1, :], wo_raw[:, 2, :])
        y = (wkv_raw[:, 0:D], wkv_raw[:, D:2 * D])
        we_hi, we_lo = cT_hi[:, :, 0:D], cT_lo[:, :, 0:D]
        tT_hi, tT_lo = nT_hi, nT_lo
        lw = sb(st, "lw", [P, 1])
        coef = sb(st, "coef", [P, 1])
        d_stat = sb(st, "d_stat", [P, 2, 6])
        d_mv = sb(st, "d_mv", [P, 2, 2])
        d_rstd = sb(st, "d_rstd", [P, 2])

        s_banks = (bank[0], bank[7])
        q_bank, pt_bank, kv_bank, o_bank, y_bank = bank[1:6]
        kt_bank = bank[6][:, 0:P]
        ss_bank = bank[6][:, P:P + 4]
        t_bank, f_banks = bank[1], (bank[3], bank[6])

        ones_set = sem("c_ones_set")
        wqk_done = sem("c_wqk")
        wo_h = sem("c_wo_high")
        wo_l = sem("c_wo_low")
        s_done = sem("c_scores")
        q_done = sem("c_q")
        pt_done = sem("c_probs_turned")
        kv_done = sem("c_kv")
        y_done = sem("c_y")
        o_done = sem("c_o")
        kt_done = sem("c_k_turned")
        ss_done = sem("c_q_squares_summed")
        exped = sem("c_exp")
        q_h = sem("c_q_high")
        q_sq = sem("c_q_squared")
        p_h = sem("c_p_high")
        k_sq = sem("c_k_squared")
        v_h = sem("c_v_high")
        o_h = sem("c_o_high")
        k_h = sem("c_k_high")
        masked = sem("c_scores_masked")
        maxed = sem("c_max")
        recip = sem("c_sum_reciprocal")
        q_l = sem("c_q_low")
        ss_out = sem("c_q_squares_out")
        p_l = sem("c_p_low")
        k_nat = sem("c_k_normed")
        v_l = sem("c_v_low")
        y_add = sem("c_y_added")
        o_l = sem("c_o_low")
        k_l = sem("c_k_low")
        normed = sem("c_probs_normed")
        rq_done = sem("c_rq")
        k_eps = sem("c_k_eps")
        rk_done = sem("c_rk")

        ld_d = [sem(f"d_loaded{i}") for i in range(5)]
        coefd = sem("d_coef")
        folded = sem("d_folded")
        we_sum = sem("d_weight_sum")
        we_h = sem("d_weight_high")
        we_l = sem("d_weight_low")
        d_stats = sem("d_stats")
        d_root = sem("d_root")
        d_norm = sem("d_norm")
        d_bias = sem("d_bias")
        turned = sem("d_turned")
        t_h = sem("d_turned_high")
        t_l = sem("d_turned_low")
        mm = sem("d_product")
        ysum = sem("d_y")
        stored = [sem("d_stored0"), sem("d_stored1")]
        FOLD = N - B
        STAT, NORM, TURN, PROD = (N - B + 2 + i for i in range(4))

        def batch(g, s, first):
            b = B * g + s - first if isinstance(g, int) else -1
            return b if 0 <= b < B else None

        def chunk(g, s):
            c = B * g + s - FOLD if isinstance(g, int) else -1
            return c if 0 <= c < CH else None

        def xb(b):
            return xres[:, b * D:(b + 1) * D]

        def loops(eng, slot):
            for s in range(B - LAG, B):
                slot(-1, s)
            for s in range(B):
                slot(0, s)
            with eng.Fori(1, G - 1) as g:
                for s in range(B):
                    slot(g, s)
            for s in range(B):
                slot(G - 1, s)
            for s in range(PROD + B - N):
                slot(G, s)

        def on(g, s, ahead):
            return not isinstance(g, int) or 0 <= B * g + s + ahead < N

        def soon(g, s):
            return s == 2 or (isinstance(g, int) and g == 0 and s == 1)

        def at(s, ahead):
            b = (s + ahead) % B
            return slice(b * P, (b + 1) * P)

        with nc.Block() as block:
            @block.sync
            def _(sp):
                def row(d, i):
                    return d[i] if isinstance(i, int) else d[bass.ds(i, 1)].rearrange("a p n -> p (a n)")

                def refills(g):
                    need(sp, wkv_l, g + 1)
                    sp.dma_start(wkv_raw[:], row(wkv_d, g + 1)).then_inc(ld_wkv, 16)
                    for h in range(HG):
                        need(sp, wq_l, HG * g + h + 1)
                        sp.dma_start(wq_raw[:, h, :], row(wq_d, HG * (g + 1) + h)).then_inc(ld_wq[h], 16)
                    for h in range(HG):
                        need(sp, wo_l, HG * g + h + 1)
                        sp.dma_start(wo_raw[:, h, :], row(wo_d, HG * (g + 1) + h)).then_inc(ld_wo[h], 16)

                refills(0)
                with sp.Fori(1, G - 1) as g:
                    refills(g)

                sp.dma_start(lw[:], lw_d[:]).then_inc(ld_d[2], 16)
                sp.wait_ge(wkv_l, G)
                sp.dma_start(lA, lA_d[:]).then_inc(ld_d[0], 16)
                sp.dma_start(lBc, lB_d[:]).then_inc(ld_d[1], 16)
                sp.wait_ge(wq_l, HG * G)
                sp.dma_start(w1[:], w1_d[:]).then_inc(ld_d[3], 16)
                sp.wait_ge(wo_l, HG * G)
                sp.dma_start(bg, b1_d[:]).then_inc(ld_d[4], 16)
                for b in range(B):
                    sp.wait_ge(ysum, b + 1)
                    if b >= 2:
                        sp.wait_ge(stored[b % 2], 16 * (b // 2))
                    sp.dma_start(out[b], y[b % 2]).then_inc(stored[b % 2], 16)
                for i in range(2):
                    sp.wait_ge(stored[i], 16 * B // 2)

            @block.gpsimd
            def _(pool):
                pool.memset(ones[:], 1.0).then_inc(ones_set, 1)

                def low_wq(g, h):
                    need(pool, wq_h, HG * g + h + 1)
                    pool.tensor_tensor(wq_lo[h][:], wq_raw[:, h, :], wq_hi[h][:].bitcast(F32),
                                       ALU.subtract).then_inc(wq_l, 1)

                def low_wkv(g):
                    need(pool, wkv_h, g + 1)
                    pool.tensor_tensor(wkv_lo[:], wkv_raw[:], wkv_hi[:].bitcast(F32),
                                       ALU.subtract).then_inc(wkv_l, 1)

                def low_wo(g, h):
                    need(pool, wo_h, HG * g + h + 1)
                    pool.tensor_tensor(wo_lo[:, h, :], wo_raw[:, h, :], wo_hi[:, h, :].bitcast(F32),
                                       ALU.subtract).then_inc(wo_l, 1)

                for h in range(1, HG):
                    low_wq(0, h)

                def slot(g, s):
                    n = B * g + s
                    filling = isinstance(g, int) and g < 0
                    following = not filling and on(g, 0, B)
                    if s == 4 and following:
                        low_wkv(g + 1)
                    b = batch(g, s, TURN)
                    if b is not None:
                        pool.wait_ge(coefd, 3)
                        pool.wait_ge(d_norm, b + 1)
                        pool.tensor_tensor(xb(b), xb(b), bg, ALU.add).then_inc(d_bias, 1)
                    if on(g, s, 0):
                        need(pool, recip, n + 1)
                        need(pool, pt_done, n)
                        pool.tensor_tensor(probn[:], prob[:], erec[:].unsqueeze(2).broadcast_to([P, HG, P]),
                                           ALU.mult).then_inc(normed, 1)
                    if on(g, s, LAG):
                        need(pool, k_sq, n + LAG + 1, hold=True)
                        pool.tensor_scalar(kse[:], kss[:], P * RMS_EPS, None, ALU.add).then_inc(k_eps, 1)
                        need(pool, k_eps, n + LAG + 1)
                        need(pool, k_nat, n + LAG)
                        pool.tensor_tensor(rk[:], kse[:], neghalf[:, 0:1], ALU.pow).then_inc(rk_done, 1)
                    if on(g, s, LAG):
                        need(pool, ss_out, n + LAG + 1)
                        first = 0 if s >= 4 else 4
                        pool.tensor_tensor(rq[:, s % HG, first:first + 4], qss[:], neghalf[:, 0:4],
                                           ALU.pow).then_inc(rq_done, 1)
                    if following:
                        for h in WQ_SLOT.get(s, ()):
                            low_wq(g + 1, h)
                    b = batch(g, s, STAT)
                    if b is not None:
                        i = b % 2
                        pool.wait_ge(d_stats, 2 * b + 2)
                        pool.tensor_scalar(d_mv[:, i, 1:2], d_mv[:, i, 1:2], LN_EPS, None,
                                           ALU.add).then_inc(d_root, 1)
                        pool.wait_ge(d_root, 2 * b + 1)
                        pool.tensor_tensor(d_rstd[:, i:i + 1], d_mv[:, i, 1:2], neghalf[:, 0:1],
                                           ALU.pow).then_inc(d_root, 1)
                    if not filling and on(g, 0, 0):
                        for h in WO_SLOT.get(s, ()):
                            low_wo(g, h)
                    for c in LOW_SLOT.get(s, ()) if chunk(g, 0) == 0 else ():
                        pool.wait_ge(we_h, c + 1)
                        pool.tensor_tensor(we_lo[:, c, :], w1[:, c, :], we_hi[:, c, :].bitcast(F32),
                                           ALU.subtract).then_inc(we_l, 1)

                loops(pool, slot)

            @block.scalar
            def _(act):
                def high_wq(g, h):
                    need(act, ld_wq[h], 16 * g + 16)
                    need(act, q_done, B * (g - 1) + HG + h + 1)
                    act.activation(wq_hi[h][:], wq_raw[:, h, :], ACT.Copy).then_inc(wq_h, 1)

                def high_wkv(g):
                    need(act, ld_wkv, 16 * g + 16)
                    need(act, kv_done, B * g)
                    act.activation(wkv_hi[:], wkv_raw[:], ACT.Copy).then_inc(wkv_h, 1)

                def high_wo(g, h):
                    need(act, ld_wo[h], 16 * g + 16)
                    need(act, y_done, B * g)
                    act.activation(wo_hi[:, h, :], wo_raw[:, h, :], ACT.Copy).then_inc(wo_h, 1)

                def exponents(n):
                    need(act, maxed, n + 1)
                    need(act, normed, n)
                    for h in range(HG):
                        t = act.activation(prob[:, h, :], score[:, h, :], ACT.Exp, bias=nmax[:, h:h + 1],
                                           accum_out=esum[:, h:h + 1])
                    t.then_inc(exped, 1)

                def high_probs(n):
                    need(act, pt_done, n)
                    act.activation(pT_hi[:], pt_bank[:], ACT.Copy).then_inc(p_h, 1)

                for h in range(1, HG):
                    high_wq(0, h)

                def slot(g, s):
                    n = B * g + s
                    filling = isinstance(g, int) and g < 0
                    following = not filling and on(g, 0, B)
                    if s == 4 and following:
                        high_wkv(g + 1)
                    b = batch(g, s, TURN)
                    if on(g, s, -1) and b is not None:
                        high_probs(n)
                    if b is not None:
                        act.wait_ge(turned, b + 1)
                        act.activation(tT_hi[:, :, b * P:(b + 1) * P], t_bank[:].rearrange("p (c t) -> p c t", c=CH),
                                       ACT.Copy).then_inc(t_h, 1)
                    if on(g, s, LAG):
                        first = 0 if s >= 4 else 4
                        need(act, q_done, n + LAG + 1)
                        act.activation(qT_hi[:, s % HG, first * P:(first + 4) * P], q_bank[:],
                                       ACT.Copy).then_inc(q_h, 1)
                    if on(g, s, LAG - 1):
                        need(act, kt_done, n + LAG)
                        act.activation(kT[:, (s + LAG - 1) % B, 0, :], kt_bank, ACT.Copy,
                                       scale=wqk[:]).then_inc(k_h, 1)
                    if on(g, s, -1) and soon(g, s):
                        high_probs(n)
                    if on(g, s, LAG):
                        need(act, ss_done, n + LAG)
                        act.activation(qsq[:], q_bank[:], ACT.Square).then_inc(q_sq, 1)
                    if on(g, s, 0):
                        exponents(n)
                    if on(g, s, -1) and b is None and not soon(g, s):
                        high_probs(n)
                    if on(g, s, LAG):
                        need(act, kv_done, n + LAG + 1)
                        need(act, k_eps, n + LAG)
                        act.activation(ksq[:], kv_bank[:, 0:P], ACT.Square, accum_out=kss[:]).then_inc(k_sq, 1)
                        act.activation(v_hi[:, at(s, LAG)], kv_bank[:, P:2 * P], ACT.Copy).then_inc(v_h, 1)
                    if on(g, s, -1):
                        need(act, o_done, n)
                        need(act, y_done, n - 1)
                        act.activation(oT_hi[:], o_bank[:], ACT.Copy).then_inc(o_h, 1)
                    if following:
                        for h in WQ_SLOT.get(s, ()):
                            high_wq(g + 1, h)
                    if not filling and on(g, 0, 0):
                        for h in WO_SLOT.get(s, ()):
                            high_wo(g, h)
                    c = chunk(g, s)
                    if c is not None:
                        act.wait_ge(we_sum, c + 1)
                        act.wait_ge(kv_done, N - LAG)
                        act.activation(we_hi[:, c, :], w1[:, c, :], ACT.Copy).then_inc(we_h, 1)

                act.wait_ge(wqk_done, 2)
                loops(act, slot)

            @block.tensor
            def _(pe):
                pe.wait_ge(ones_set, 1)

                def scores(g, s):
                    n = B * g + s
                    need(pe, k_h, n + 1)
                    need(pe, k_l, n + 1)
                    if s % HG == 0:
                        need(pe, q_h, n + HG)
                        need(pe, q_l, n + HG)
                    need(pe, masked, 2 * n)
                    for h in range(HG):
                        o = s_banks[h // 2][:, h % 2 * 2 * P:(h % 2 + 1) * 2 * P]
                        pe.matmul(o, qT_hi[:, h, at(s, 0)], kT[:, s, :, :].rearrange("p i t -> p (i t)"),
                                  start=True, stop=True, skip_group_check=True)
                        t = pe.matmul(o[:, 0:P], qT_lo[:, h, at(s, 0)], kT[:, s, 0, :], start=False, stop=True,
                                      skip_group_check=True)
                    t.then_inc(s_done, 1)

                def project_q(g, s):
                    n, h = B * g + s, s % HG
                    first = 0 if s >= 4 else 4
                    half = slice(first * P, (first + 4) * P)
                    if s >= 4:
                        need(pe, wq_l, HG * (g + 1) + h + 1)
                    need(pe, q_h, n + LAG)
                    need(pe, q_l, n + LAG)
                    need(pe, q_sq, n + LAG)
                    for c in range(CH):
                        w = slice(c * P, (c + 1) * P)
                        t = three_pass(pe, q_bank[:], wq_hi[h][:, w], wq_lo[h][:, w],
                                       nT_hi[:, c, half], nT_lo[:, c, half], c == 0, c == CH - 1)
                    t.then_inc(q_done, 1)

                def turn_probs(g, s):
                    n = B * g + s
                    need(pe, normed, n)
                    need(pe, p_h, n - 1)
                    need(pe, p_l, n - 1)
                    for h in range(HG):
                        t = pe.transpose(pt_bank[:, h * P:(h + 1) * P], probn[:, h, :], ident[:])
                    t.then_inc(pt_done, 1)

                def project_kv(g, s):
                    n = B * g + s
                    if s == 4:
                        need(pe, wkv_l, g + 2)
                    need(pe, k_nat, n + LAG)
                    need(pe, v_h, n + LAG)
                    need(pe, v_l, n + LAG)
                    for c in range(CH):
                        w = slice(c * 2 * P, (c + 1) * 2 * P)
                        t = three_pass(pe, kv_bank[:, 0:2 * P], cT_hi[:, c, at(s, LAG)], cT_lo[:, c, at(s, LAG)],
                                       wkv_hi[:, w], wkv_lo[:, w], c == 0, c == CH - 1)
                    t.then_inc(kv_done, 1)

                def project_out(g, s):
                    n = B * g + s
                    need(pe, o_h, n - 1)
                    need(pe, o_l, n - 1)
                    need(pe, y_add, n - 2)
                    c = chunk(g, s)
                    if c or (c is None and chunk(g, s - 1) is not None):
                        pe.wait_ge(we_sum, c + (s == 2) if c else CH)
                    for h in range(HG):
                        if s == 2:
                            need(pe, wo_l, HG * g + h + 1)
                        w = slice(h * P, (h + 1) * P)
                        t = three_pass(pe, y_bank[:], oT_hi[:, w], oT_lo[:, w], wo_hi[:, h, :], wo_lo[:, h, :],
                                       h == 0, h == HG - 1)
                    t.then_inc(y_done, 1)

                def probs_v(g, s):
                    n = B * g + s
                    need(pe, p_h, n)
                    need(pe, p_l, n)
                    need(pe, o_h, n - 1)
                    need(pe, o_l, n - 1)
                    three_pass(pe, o_bank[:], v_hi[:, at(s, -1)], v_lo[:, at(s, -1)], pT_hi[:], pT_lo[:],
                               True, True).then_inc(o_done, 1)

                def sum_squares(g, s):
                    n = B * g + s
                    need(pe, q_sq, n + LAG + 1)
                    need(pe, k_h, n + LAG)
                    need(pe, k_l, n + LAG)
                    for j in range(4):
                        t = pe.matmul(ss_bank[:, j:j + 1], qsq[:, j * P:(j + 1) * P], ones[:],
                                      start=True, stop=True)
                    t.then_inc(ss_done, 1)

                def turn_k(g, s):
                    n = B * g + s
                    need(pe, k_nat, n + LAG)
                    need(pe, ss_out, n + LAG)
                    pe.transpose(kt_bank, knat[:], ident[:]).then_inc(kt_done, 1)

                def fold(c):
                    if c == 0:
                        pe.wait_ge(ld_d[0], 16)
                        pe.wait_ge(coefd, 2)
                    pe.wait_ge(y_add, FOLD + c - (1 if c != 2 else 2))
                    pe.matmul(y_bank[:], lA[:, c * P:(c + 1) * P], lBc, start=True, stop=True).then_inc(folded, 1)

                def turn_batch(b):
                    if b == 0:
                        pe.wait_ge(q_l, N)
                        pe.wait_ge(q_sq, N)
                    pe.wait_ge(d_norm, b + 1)
                    if b >= 1:
                        pe.wait_ge(t_l, b)
                    for c in range(CH):
                        t = pe.transpose(t_bank[:, c * P:(c + 1) * P], n3[b % 2][:, c * P:(c + 1) * P], ident[:])
                    t.then_inc(turned, 1)

                def feed_forward(b):
                    if b == 0:
                        pe.wait_ge(we_l, CH)
                        pe.wait_ge(k_nat, N)
                        pe.wait_ge(v_l, N)
                    if b == 1:
                        pe.wait_ge(k_l, N)
                        pe.wait_ge(ss_out, N)
                    pe.wait_ge(t_h, b + 1)
                    pe.wait_ge(t_l, b + 1)
                    if b >= 2:
                        pe.wait_ge(ysum, b - 1)
                    for c in range(CH):
                        t = three_pass(pe, f_banks[b % 2][:], tT_hi[:, c, b * P:(b + 1) * P],
                                       tT_lo[:, c, b * P:(b + 1) * P], we_hi[:, c, :], we_lo[:, c, :],
                                       c == 0, c == CH - 1)
                    t.then_inc(mm, 1)

                def slot(g, s):
                    c, turning, multiplied = chunk(g, s), batch(g, s, TURN), batch(g, s, PROD)
                    if on(g, s, 0):
                        scores(g, s)
                    if on(g, s, LAG):
                        project_q(g, s)
                    if on(g, s, LAG - 1):
                        turn_k(g, s)
                    if on(g, s, -1) and turning is not None:
                        turn_probs(g, s)
                    if turning is not None:
                        turn_batch(turning)
                    if multiplied is not None:
                        feed_forward(multiplied)
                    if on(g, s, -2) and s != 2:
                        project_out(g, s)
                    if on(g, s, -1) and turning is None:
                        turn_probs(g, s)
                    if on(g, s, LAG):
                        project_kv(g, s)
                    if on(g, s, LAG):
                        sum_squares(g, s)
                    if c is not None:
                        fold(c)
                    if on(g, s, -1):
                        probs_v(g, s)
                    if on(g, s, -2) and s == 2:
                        project_out(g, s)

                loops(pe, slot)

            @block.vector
            def _(dve):
                dve.wait_ge(ld_mask, 16)
                dve.wait_ge(ld_norm[0], 16)
                dve.wait_ge(ld_norm[1], 16)
                dve.tensor_scalar(wqk[:], norm_w[:, 0:1], float(P) ** 0.5, None, ALU.mult).then_inc(wqk_done, 1)
                dve.wait_ge(wqk_done, 1)
                dve.tensor_scalar(wqk[:], wqk[:], norm_w[:, 1:2], None, ALU.mult).then_inc(wqk_done, 1)
                dve.wait_ge(wqk_done, 2)

                def slot(g, s):
                    n = B * g + s
                    if chunk(g, s) == 0:
                        dve.wait_ge(ld_d[1], 16)
                        dve.wait_ge(ld_d[2], 16)
                        dve.tensor_scalar(coef[:], lw[:], 2.0, None, ALU.mult).then_inc(coefd, 1)
                        dve.wait_ge(coefd, 1)
                        dve.tensor_scalar(lBc, lBc, coef[:], None, ALU.mult).then_inc(coefd, 1)
                    if on(g, s, 0):
                        need(dve, s_done, n + 1)
                        need(dve, exped, n)
                        if s % HG == 0:
                            need(dve, rq_done, n + HG)
                        for part, more in ((1, maskt), (0, None)):
                            for h in range(HG):
                                o = s_banks[h // 2][:, (h % 2 * 2 + part) * P:(h % 2 * 2 + part + 1) * P]
                                t = dve.scalar_tensor_tensor(score[:, h, :], o, rq[:, h, s:s + 1],
                                                             score[:, h, :] if more is None else more[:],
                                                             ALU.mult, ALU.add)
                            t.then_inc(masked, 1)
                            need(dve, masked, 2 * n + 2 - part)
                        dve.tensor_reduce(nmax[:], score[:], AX.X, ALU.max, negate=True).then_inc(maxed, 1)
                    if on(g, s, -1) and batch(g, s, TURN) is not None:
                        low_probs(n)
                    b = batch(g, s, NORM)
                    if b is not None:
                        i = b % 2
                        if b == 0:
                            dve.wait_ge(wo_l, HG * G)
                        dve.wait_ge(d_root, 2 * b + 2)
                        if b >= 2:
                            dve.wait_ge(turned, b - 1)
                        dve.tensor_scalar(n3[i], xb(b), d_mv[:, i, 0:1], d_rstd[:, i:i + 1],
                                          ALU.subtract, ALU.mult).then_inc(d_norm, 1)
                    b = batch(g, s, TURN)
                    if b is not None:
                        dve.wait_ge(t_h, b + 1)
                        dve.tensor_tensor(tT_lo[:, :, b * P:(b + 1) * P],
                                          t_bank[:].rearrange("p (c t) -> p c t", c=CH),
                                          tT_hi[:, :, b * P:(b + 1) * P].bitcast(F32),
                                          ALU.subtract).then_inc(t_l, 1)
                    b = batch(g, s, PROD)
                    if b is not None:
                        dve.wait_ge(mm, b + 1)
                        dve.wait_ge(d_bias, b + 1)
                        if b >= 2:
                            dve.wait_ge(stored[b % 2], 16 * (b // 2))
                        dve.scalar_tensor_tensor(y[b % 2], f_banks[b % 2][:], gate[:, 3:4], xb(b),
                                                 ALU.mult, ALU.add).then_inc(ysum, 1)
                    if on(g, s, LAG - 1):
                        need(dve, k_h, n + LAG)
                        dve.scalar_tensor_tensor(kT[:, (s + LAG - 1) % B, 1, :], kt_bank, wqk[:],
                                                 kT[:, (s + LAG - 1) % B, 0, :].bitcast(F32),
                                                 ALU.mult, ALU.subtract).then_inc(k_l, 1)
                    if on(g, s, -1) and soon(g, s):
                        low_probs(n)
                    if on(g, s, LAG):
                        first = 0 if s >= 4 else 4
                        half = slice(first * P, (first + 4) * P)
                        need(dve, q_h, n + LAG + 1)
                        need(dve, q_sq, n + LAG + 1)
                        dve.tensor_tensor(qT_lo[:, s % HG, half], q_bank[:],
                                          qT_hi[:, s % HG, half].bitcast(F32), ALU.subtract).then_inc(q_l, 1)
                    if on(g, s, 0):
                        reciprocals(n)
                    if on(g, s, -2) and s != 2:
                        add_out(g, s)
                    if on(g, s, -1) and batch(g, s, TURN) is None and not soon(g, s):
                        low_probs(n)
                    c = chunk(g, s)
                    if c is not None:
                        dve.wait_ge(ld_d[3], 16)
                        dve.wait_ge(folded, c + 1)
                        dve.tensor_tensor(w1[:, c, :], y_bank[:], w1[:, c, :], ALU.add).then_inc(we_sum, 1)
                        if c == CH - 1:
                            dve.wait_ge(ld_d[4], 16)
                            dve.tensor_scalar(bg, bg, gate[:, 3:4], None, ALU.mult).then_inc(coefd, 1)
                    if on(g, s, LAG):
                        need(dve, rk_done, n + LAG + 1)
                        need(dve, kt_done, n + LAG)
                        need(dve, v_h, n + LAG + 1)
                        dve.tensor_scalar(knat[:], kv_bank[:, 0:P], rk[:], None, ALU.mult).then_inc(k_nat, 1)
                        dve.tensor_tensor(v_lo[:, at(s, LAG)], kv_bank[:, P:2 * P],
                                          v_hi[:, at(s, LAG)].bitcast(F32), ALU.subtract).then_inc(v_l, 1)
                    if on(g, s, LAG):
                        need(dve, ss_done, n + LAG + 1)
                        need(dve, rq_done, n + LAG)
                        dve.tensor_scalar(qss[:], ss_bank, P * RMS_EPS, None, ALU.add).then_inc(ss_out, 1)
                    if on(g, s, -1):
                        need(dve, o_h, n)
                        dve.tensor_tensor(oT_lo[:], o_bank[:], oT_hi[:].bitcast(F32),
                                          ALU.subtract).then_inc(o_l, 1)
                    if on(g, s, -2) and s == 2:
                        add_out(g, s)

                def low_probs(n):
                    need(dve, p_h, n)
                    dve.tensor_tensor(pT_lo[:], pt_bank[:], pT_hi[:].bitcast(F32), ALU.subtract).then_inc(p_l, 1)

                def reciprocals(n):
                    need(dve, exped, n + 1)
                    need(dve, normed, n)
                    dve.reciprocal(erec[:], esum[:]).then_inc(recip, 1)

                def add_out(g, s):
                    n = B * g + s
                    b = (s - 2) % B
                    need(dve, y_done, n - 1)
                    need(dve, y_add, n - 2)
                    dve.scalar_tensor_tensor(xb(b), y_bank[:], gate[:, 2:3], xb(b),
                                             ALU.mult, ALU.add).then_inc(y_add, 1)
                    if batch(g, s, STAT) is not None:
                        i = b % 2
                        dve.wait_ge(y_add, n - 1)
                        if b >= 2:
                            dve.wait_ge(d_norm, b - 1)
                        dve.bn_stats(d_stat[:, i, :], xb(b)).then_inc(d_stats, 1)
                        dve.wait_ge(d_stats, 2 * b + 1)
                        dve.bn_aggr(d_mv[:, i, :], d_stat[:, i, :]).then_inc(d_stats, 1)

                loops(dve, slot)


def dft_constants():
    import numpy as np
    t = np.arange(P)
    f = np.concatenate([np.arange(0, P // 2 + 1), np.arange(1, P // 2)])
    is_im = (np.arange(P) > P // 2)[:, None]
    ph = 2 * np.pi * np.outer(f, t) / P
    fwd = np.where(is_im, -np.sin(ph), np.cos(ph))
    fwd_sw = np.where(is_im, np.cos(ph), -np.sin(ph))
    weight = np.where((f == 0) | (f == P // 2), 1.0, 2.0)[:, None]
    inv1 = weight * np.cos(ph) / P
    inv2 = np.where(is_im, -1, 1) * weight * np.sin(ph) / P
    odd = np.concatenate([np.arange(P // 2)] * 2)
    is_im = (np.arange(P) >= P // 2)[:, None]
    ph = 2 * np.pi * np.outer(2 * odd + 1, t) / (2 * P)
    odd_fwd = np.where(is_im, -np.sin(ph), np.cos(ph))
    odd_fwd_sw = np.where(is_im, np.cos(ph), -np.sin(ph))
    odd_inv1 = np.cos(ph) / P
    odd_inv2 = np.where(is_im, 1, -1) * np.sin(ph) / P

    def less_last_row(m):
        m = m.copy()
        m[:, P - 1] -= m.sum(1)
        return m

    fwd_sw[0] = np.arange(P) == P - 1
    even_inv2 = -inv2 / 2
    even_inv2[0] = 0.5
    m = [fwd.T, fwd_sw.T, less_last_row(odd_fwd).T, less_last_row(odd_fwd_sw).T, odd_fwd.T, inv1, inv2,
         inv1 / 2, even_inv2, odd_inv1, odd_inv2, np.eye(P)]
    return np.ascontiguousarray(np.stack(m, axis=1).astype(np.float32))


def kernel(**inputs):
    import numpy as np
    import concourse.bacc as bacc
    from concourse.bass_utils import run_bass_kernel_spmd

    a = {k: np.asarray(v) for k, v in inputs.items()}

    def chunked(w):
        return w.reshape(w.shape[0], CH, P).transpose(2, 1, 0)

    wk = a["L1_xattn_Wk"].reshape(G, P, CH, P).transpose(0, 3, 2, 1)
    wv = a["L1_xattn_Wv"].reshape(G, P, CH, P).transpose(0, 3, 2, 1)
    laid = {
        "x": a["x"],
        "ctx_n": a["ctx_4096"],
        "ctx_t": a["ctx_4096"].reshape(B, P, CH, P).transpose(0, 3, 2, 1).reshape(B, P, D),
        "mask": a["mask_1x1xSxS2_ff0"].reshape(P, P),
        "gates": np.broadcast_to(np.stack([a["g_xattn"][0], a["g_ffn"][0], a["g_xattn"][1], a["g_ffn"][1]]), (P, 4)),
        "dft": dft_constants(),
        "wbase": chunked(a["L0_ffn_W_base"]),
        "wag": np.concatenate([chunked(a["L0_ffn_A"].reshape(ER, D)), chunked(a["L0_ffn_W_gate"])], axis=2),
        "bb": np.broadcast_to(a["L0_ffn_b_base"], (P, D)),
        "bcat": a["L0_ffn_B"].transpose(0, 2, 1).reshape(ER, D),
        "wq": a["L1_xattn_Wq"].reshape(G * HG, P, CH, P).transpose(0, 3, 2, 1).reshape(G * HG, P, D),
        "wkv": np.concatenate([wk, wv], axis=3).reshape(G, P, CH * 2 * P),
        "wo": a["L1_xattn_Wo"].reshape(D, G * HG, P).transpose(1, 2, 0),
        "qn": a["L1_xattn_q_norm_w"].reshape(P, 1),
        "kn": a["L1_xattn_k_norm_w"].reshape(P, 1),
        "lA": a["L1_ffn_lora_A"].reshape(P, D),
        "lB": a["L1_ffn_lora_B"].transpose(0, 2, 1).reshape(P, D),
        "lw": np.repeat(a["L1_ffn_lora_weights"], R).reshape(P, 1),
        "w1": chunked(a["L1_ffn_W"]),
        "b1": np.broadcast_to(a["L1_ffn_bias"], (P, D)),
    }
    nc = bacc.Bacc("TRN2", target_bir_lowering=False, num_devices=1)
    arrays, args = {}, []
    for name, v in laid.items():
        v = np.ascontiguousarray(v)
        arrays[f"in_{name}"] = v
        args.append(nc.dram_tensor(f"in_{name}", v.shape, mybir.dt.from_np(v.dtype), kind="ExternalInput").ap())
    args.append(nc.dram_tensor("out_0", (B, P, D), F32, kind="ExternalOutput").ap())
    names = list(laid)
    by = dict(zip(names, args))
    flamingo_kernel(nc, by["x"], by["ctx_n"], by["ctx_t"], by["mask"], by["gates"], by["dft"], by["wbase"],
                    by["wag"], by["bb"], by["bcat"], by["wq"], by["wkv"], by["wo"], by["qn"], by["kn"],
                    by["lA"], by["lB"], by["lw"], by["w1"], by["b1"], args[-1])
    r = run_bass_kernel_spmd(nc, [arrays], core_ids=[0])
    return r.results[0]["out_0"]
```
